# Optimizing a Trainium2 kernel written in Bass

```python
import numpy as np
import jax
import jax.numpy as jnp

def _softmax(x, axis=-1):
    return jax.nn.softmax(x, axis=axis)

def _gelu(x):
    return jax.nn.gelu(x, approximate=True)

def _silu(x):
    return jax.nn.silu(x)

def _sigmoid(x):
    return jax.nn.sigmoid(x)

def _layernorm(x, axis=-1, eps=1e-05):
    m = jnp.mean(x, axis=axis, keepdims=True)
    v = jnp.var(x, axis=axis, keepdims=True)
    return (x - m) / jnp.sqrt(v + eps)

def _scatter_add(tgt, idx, src, axis=0):
    return tgt.at[idx].add(src)

def _segment_sum(src, seg, n):
    return jax.ops.segment_sum(src, seg, n)
kernel_name = 'mk_decoder_postln_d1_seqx_r8_c02a98'

def setup_inputs(seed: int=0):
    np.random.seed(seed)
    _w = jnp.asarray

    def _rec_inputs():
        import jax
        import jax.numpy as jnp
        _rk = jax.random.key(seed)
        x = 7.22e-05 + 1 * jax.random.normal(jax.random.fold_in(_rk, 1), (16, 128, 256), jnp.float32)
        _lenS = 128 - jax.random.randint(jax.random.fold_in(_rk, 7), (16,), 0, max(1, 128 // 4) + 1, jnp.int32)
        _lenS2 = 128 - jax.random.randint(jax.random.fold_in(_rk, 8), (16,), 0, max(1, 128 // 4) + 1, jnp.int32)
        _ctx_2048P = jax.random.normal(jax.random.fold_in(_rk, 11), (16, 16, 256), jnp.float32)
        _ctx_2048c = jax.random.dirichlet(jax.random.fold_in(_rk, 511), 0.3 * jnp.ones((16,), jnp.float32), (16, 128))
        _ctx_2048t = jnp.einsum('bsk,bkd->bsd', _ctx_2048c, _ctx_2048P)
        _ctx_2048t = _ctx_2048t * jax.lax.rsqrt(jnp.mean(jnp.square(_ctx_2048t)) + 1e-12) * 0.953939
        ctx_2048 = 4.13588e-05 + 0.999923 * (_ctx_2048t + 0.3 * jax.random.normal(jax.random.fold_in(_rk, 611), (16, 128, 256), jnp.float32))
        _validS = jnp.arange(128)[None, :] < _lenS[:, None]
        _validS2 = jnp.arange(128)[None, :] < _lenS2[:, None]
        _causal = jnp.tril(jnp.ones((128, 128), dtype=bool))
        mask_SxS2_bc0 = jnp.logical_not(jnp.broadcast_to(_validS2[0:1, :], (128, 128)))
        mask_BxS2_bk0 = jnp.logical_not(jnp.broadcast_to(_validS2[:, :], (16, 128)))
        return (x, ctx_2048, mask_SxS2_bc0, mask_BxS2_bk0)
    x, ctx_2048, mask_SxS2_bc0, mask_BxS2_bk0 = _rec_inputs()

    def _L0_attn_setup():
        import jax, jax.numpy as jnp
        import numpy as np
        B, S, H = (1, 256, 256)
        N_HEADS = 16
        Q_LORA = 192
        KV_LORA = 64
        D_ROPE = 64
        D_NOPE = 128
        D_V = 128
        Q_HEAD_DIM = D_NOPE + D_ROPE
        ROPE_THETA = 10000.0
        EPS = 1e-06

        def _rmsnorm(x, w, eps=EPS):
            var = jnp.mean(jnp.square(x), axis=-1, keepdims=True)
            return x * jax.lax.rsqrt(var + eps) * w

        def _rope_tables(seq_len, dim, theta):
            inv_freq = 1.0 / theta ** (jnp.arange(0, dim, 2, dtype=jnp.float32) / dim)
            t = jnp.arange(seq_len, dtype=jnp.float32)
            freqs = jnp.outer(t, inv_freq)
            emb = jnp.concatenate([freqs, freqs], axis=-1)
            return (jnp.cos(emb), jnp.sin(emb))

        def _apply_rope(x, cos, sin):
            half = x.shape[-1] // 2
            x1, x2 = (x[..., :half], x[..., half:])
            rot = jnp.concatenate([-x2, x1], axis=-1)
            return x * cos + rot * sin
        key = jax.random.key(seed)
        ks = jax.random.split(key, 8)
        s = lambda fan_in: 1.0 / np.sqrt(fan_in)
        return {'x': jax.random.normal(ks[0], (B, S, H), jnp.float32), 'wq_a': jax.random.normal(ks[1], (H, Q_LORA), jnp.float32) * s(H), 'q_a_ln_w': jnp.ones((Q_LORA,), jnp.float32), 'wq_b': jax.random.normal(ks[2], (Q_LORA, N_HEADS * Q_HEAD_DIM), jnp.float32) * s(Q_LORA), 'wkv_a': jax.random.normal(ks[3], (H, KV_LORA + D_ROPE), jnp.float32) * s(H), 'kv_a_ln_w': jnp.ones((KV_LORA,), jnp.float32), 'wkv_b': jax.random.normal(ks[4], (KV_LORA, N_HEADS * (D_NOPE + D_V)), jnp.float32) * s(KV_LORA), 'wo': jax.random.normal(ks[5], (N_HEADS * D_V, H), jnp.float32) * s(N_HEADS * D_V)}
    _L0_attn_all = _L0_attn_setup()
    _L0_attn_in = {k: v for k, v in _L0_attn_all.items() if k in ('wq_a', 'q_a_ln_w', 'wq_b', 'wkv_a', 'kv_a_ln_w', 'wkv_b', 'wo')}
    del _L0_attn_all

    def _L0_xattn_setup():
        import jax, jax.numpy as jnp
        import numpy as np
        B, LQ, LKV = (4, 128, 128)
        HID, H, G = (256, 32, 8)
        HD = HID // H
        HPG = H // G
        key = jax.random.key(seed)
        ks = jax.random.split(key, 10)
        s = 0.02
        inp = {'X': jax.random.normal(ks[0], (B, LQ, HID), jnp.float32), 'encoder_output': jax.random.normal(ks[1], (B, LKV, HID), jnp.float32), 'causal_mask': jnp.triu(jnp.ones((LQ, LKV), bool), 1), 'padding_mask': jnp.zeros((B, LKV), bool).at[B // 2:, LKV - LKV // 4:].set(True), 'Wq': jax.random.normal(ks[2], (HID, HID), jnp.float32) * s, 'bq': jnp.zeros((HID,), jnp.float32), 'Wk': jax.random.normal(ks[3], (G * HD, HID), jnp.float32) * s, 'bk': jnp.zeros((G * HD,), jnp.float32), 'Wv': jax.random.normal(ks[4], (G * HD, HID), jnp.float32) * s, 'bv': jnp.zeros((G * HD,), jnp.float32), 'Wo': jax.random.normal(ks[5], (HID, HID), jnp.float32) * s, 'bo': jnp.zeros((HID,), jnp.float32)}
        return inp
    _L0_xattn_all = _L0_xattn_setup()
    _L0_xattn_in = {k: v for k, v in _L0_xattn_all.items() if k in ('Wq', 'bq', 'Wk', 'bk', 'Wv', 'bv', 'Wo', 'bo')}
    del _L0_xattn_all

    def _L0_ffn_setup():
        import jax, jax.numpy as jnp
        import numpy as np
        NUM_EXPERTS = 8
        TOP_K = 2
        key = jax.random.key(seed)
        k1, k2, k3, k4 = jax.random.split(key, 4)
        B, T, C, E, D = (4, 256, 256, NUM_EXPERTS, 256)
        scale = 0.02
        return {'x': jax.random.normal(k1, (B, T, C), dtype=jnp.float32), 'w_router': jax.random.normal(k2, (C, E), dtype=jnp.float32) * scale, 'w_fc': jax.random.normal(k3, (E, C, D), dtype=jnp.float32) * scale, 'w_proj': jax.random.normal(k4, (E, D, C), dtype=jnp.float32) * scale}
    _L0_ffn_all = _L0_ffn_setup()
    _L0_ffn_in = {k: v for k, v in _L0_ffn_all.items() if k in ('w_router', 'w_fc', 'w_proj')}
    del _L0_ffn_all
    return {'x': x, 'ctx_2048': ctx_2048, 'mask_SxS2_bc0': mask_SxS2_bc0, 'mask_BxS2_bk0': mask_BxS2_bk0, 'L0_attn_wq_a': _L0_attn_in['wq_a'], 'L0_attn_q_a_ln_w': _L0_attn_in['q_a_ln_w'], 'L0_attn_wq_b': _L0_attn_in['wq_b'], 'L0_attn_wkv_a': _L0_attn_in['wkv_a'], 'L0_attn_kv_a_ln_w': _L0_attn_in['kv_a_ln_w'], 'L0_attn_wkv_b': _L0_attn_in['wkv_b'], 'L0_attn_wo': _L0_attn_in['wo'], 'L0_xattn_Wq': _L0_xattn_in['Wq'], 'L0_xattn_bq': _L0_xattn_in['bq'], 'L0_xattn_Wk': _L0_xattn_in['Wk'], 'L0_xattn_bk': _L0_xattn_in['bk'], 'L0_xattn_Wv': _L0_xattn_in['Wv'], 'L0_xattn_bv': _L0_xattn_in['bv'], 'L0_xattn_Wo': _L0_xattn_in['Wo'], 'L0_xattn_bo': _L0_xattn_in['bo'], 'L0_ffn_w_router': _L0_ffn_in['w_router'], 'L0_ffn_w_fc': _L0_ffn_in['w_fc'], 'L0_ffn_w_proj': _L0_ffn_in['w_proj']}

def reference(x, ctx_2048, mask_SxS2_bc0, mask_BxS2_bk0, L0_attn_wq_a, L0_attn_q_a_ln_w, L0_attn_wq_b, L0_attn_wkv_a, L0_attn_kv_a_ln_w, L0_attn_wkv_b, L0_attn_wo, L0_xattn_Wq, L0_xattn_bq, L0_xattn_Wk, L0_xattn_bk, L0_xattn_Wv, L0_xattn_bv, L0_xattn_Wo, L0_xattn_bo, L0_ffn_w_router, L0_ffn_w_fc, L0_ffn_w_proj):
    import jax
    import jax.numpy as jnp

    def _L0_attn_ref(x, wq_a, q_a_ln_w, wq_b, wkv_a, kv_a_ln_w, wkv_b, wo):
        import jax, jax.numpy as jnp
        import numpy as np
        B, S, H = (1, 256, 256)
        N_HEADS = 16
        Q_LORA = 192
        KV_LORA = 64
        D_ROPE = 64
        D_NOPE = 128
        D_V = 128
        Q_HEAD_DIM = D_NOPE + D_ROPE
        ROPE_THETA = 10000.0
        EPS = 1e-06

        def _rmsnorm(x, w, eps=EPS):
            var = jnp.mean(jnp.square(x), axis=-1, keepdims=True)
            return x * jax.lax.rsqrt(var + eps) * w

        def _rope_tables(seq_len, dim, theta):
            inv_freq = 1.0 / theta ** (jnp.arange(0, dim, 2, dtype=jnp.float32) / dim)
            t = jnp.arange(seq_len, dtype=jnp.float32)
            freqs = jnp.outer(t, inv_freq)
            emb = jnp.concatenate([freqs, freqs], axis=-1)
            return (jnp.cos(emb), jnp.sin(emb))

        def _apply_rope(x, cos, sin):
            half = x.shape[-1] // 2
            x1, x2 = (x[..., :half], x[..., half:])
            rot = jnp.concatenate([-x2, x1], axis=-1)
            return x * cos + rot * sin
        b, s, _ = x.shape
        softmax_scale = Q_HEAD_DIM ** (-0.5)
        q = _rmsnorm(x @ wq_a, q_a_ln_w) @ wq_b
        q = q.reshape(b, s, N_HEADS, Q_HEAD_DIM)
        q_nope, q_pe = (q[..., :D_NOPE], q[..., D_NOPE:])
        ckv = x @ wkv_a
        compressed_kv, k_pe = (ckv[..., :KV_LORA], ckv[..., KV_LORA:])
        kv = _rmsnorm(compressed_kv, kv_a_ln_w) @ wkv_b
        kv = kv.reshape(b, s, N_HEADS, D_NOPE + D_V)
        k_nope, v = (kv[..., :D_NOPE], kv[..., D_NOPE:])
        cos, sin = _rope_tables(s, D_ROPE, ROPE_THETA)
        q_pe = _apply_rope(q_pe, cos[None, :, None, :], sin[None, :, None, :])
        k_pe = _apply_rope(k_pe, cos[None, :, :], sin[None, :, :])
        k_pe = jnp.broadcast_to(k_pe[:, :, None, :], (b, s, N_HEADS, D_ROPE))
        qf = jnp.concatenate([q_nope, q_pe], axis=-1)
        kf = jnp.concatenate([k_nope, k_pe], axis=-1)
        scores = jnp.einsum('bqhd,bkhd->bhqk', qf, kf) * softmax_scale
        causal = jnp.tril(jnp.ones((s, s), bool))
        scores = jnp.where(causal[None, None], scores, jnp.finfo(scores.dtype).min)
        attn = jax.nn.softmax(scores, axis=-1)
        out = jnp.einsum('bhqk,bkhd->bqhd', attn, v)
        return out.reshape(b, s, N_HEADS * D_V) @ wo

    def _L0_xattn_ref(X, encoder_output, causal_mask, padding_mask, Wq, bq, Wk, bk, Wv, bv, Wo, bo):
        import jax, jax.numpy as jnp
        import numpy as np
        B, LQ, LKV = (4, 128, 128)
        HID, H, G = (256, 32, 8)
        HD = HID // H
        HPG = H // G
        b = X.shape[0]
        q = X @ Wq.T + bq
        k = encoder_output @ Wk.T + bk
        v = encoder_output @ Wv.T + bv
        q = q.reshape(b, LQ, G, HPG, HD).transpose(0, 2, 3, 1, 4)
        k = k.reshape(b, LKV, G, HD).transpose(0, 2, 1, 3)
        v = v.reshape(b, LKV, G, HD).transpose(0, 2, 1, 3)
        scores = jnp.einsum('bgrqd,bgkd->bgrqk', q, k) / jnp.sqrt(jnp.float32(HD))
        scores = jnp.where(causal_mask[None, None, None, :, :], -jnp.inf, scores)
        scores = jnp.where(padding_mask[:, None, None, None, :], -jnp.inf, scores)
        w = jax.nn.softmax(scores, axis=-1)
        out = jnp.einsum('bgrqk,bgkd->bgrqd', w, v)
        out = out.reshape(b, H, LQ, HD).transpose(0, 2, 1, 3).reshape(b, LQ, HID)
        return out @ Wo.T + bo

    def _L0_ffn_ref(x, w_router, w_fc, w_proj):
        import jax, jax.numpy as jnp
        import numpy as np
        NUM_EXPERTS = 8
        TOP_K = 2
        B, T, C = x.shape
        E = w_fc.shape[0]
        x_flat = x.reshape(-1, C)
        N = x_flat.shape[0]
        router_logits = x_flat @ w_router
        top_vals, top_idx = jax.lax.top_k(router_logits, TOP_K)
        probs = jax.nn.softmax(top_vals, axis=-1)
        rows = jnp.arange(N)[:, None]
        w_tok = jnp.zeros((N, E), dtype=x.dtype).at[rows, top_idx].add(probs)
        h = jnp.einsum('nc,ecd->ned', x_flat, w_fc)
        h = jnp.square(jax.nn.relu(h))
        y = jnp.einsum('ned,edc->nec', h, w_proj)
        out = jnp.einsum('nec,ne->nc', y, w_tok)
        return out.reshape(B, T, C)
    x = _layernorm(x + _L0_attn_ref(x, L0_attn_wq_a, L0_attn_q_a_ln_w, L0_attn_wq_b, L0_attn_wkv_a, L0_attn_kv_a_ln_w, L0_attn_wkv_b, L0_attn_wo), axis=-1)
    x = _layernorm(x + _L0_xattn_ref(x, ctx_2048, mask_SxS2_bc0, mask_BxS2_bk0, L0_xattn_Wq, L0_xattn_bq, L0_xattn_Wk, L0_xattn_bk, L0_xattn_Wv, L0_xattn_bv, L0_xattn_Wo, L0_xattn_bo), axis=-1)
    x = _layernorm(x + _L0_ffn_ref(x, L0_ffn_w_router, L0_ffn_w_fc, L0_ffn_w_proj), axis=-1)
    return x

_drawn_inputs = setup_inputs


def setup_inputs(seed=0):
    import zlib

    import numpy as np

    out = dict(_drawn_inputs(seed))
    spreads = {'L0_attn_q_a_ln_w': (1.0, 0.2),
     'L0_attn_kv_a_ln_w': (1.0, 0.2),
     'L0_xattn_bq': (0.0, 0.8),
     'L0_xattn_bk': (0.0, 0.8),
     'L0_xattn_bv': (0.0, 0.1),
     'L0_xattn_bo': (0.0, 0.1)}
    factors = {'L0_xattn_Wq': 8.0, 'L0_xattn_Wk': 8.0}
    for name, (base, spread) in spreads.items():
        noise = np.random.default_rng([zlib.crc32(name.encode()), seed]).standard_normal(out[name].shape)
        drawn = base * np.exp(spread * noise) if base else spread * noise
        out[name] = jnp.asarray(drawn.astype(out[name].dtype))
    for name, factor in factors.items():
        out[name] = (out[name] * factor).astype(out[name].dtype)
    return out
```

```python
from contextlib import ExitStack

import numpy as np

import concourse.bass as bass
from concourse import mybir

F32 = mybir.dt.float32
F32R = mybir.dt.float32r
BF16 = mybir.dt.bfloat16
U8 = mybir.dt.uint8
U32 = mybir.dt.uint32
ALU = mybir.AluOpType
ACT = mybir.ActivationFunctionType
AX = mybir.AxisListType

B, S, D = 16, 128, 256
KT_D = D // 128
H, QL, KL, DR, DN, DV = 16, 192, 64, 64, 128, 128
QB = QL - 128
HC = 4
NCA = H // HC
XH, G, HD = 32, 8, 8
NCX = XH // HC
HALF = G // 2
SLOT = HALF * HD
E, TOPK = 8, 2
TC = 4
NCH = B // TC
BIG = 1e30
MLA_SCALE = float((DN + DR) ** -0.5)
XAT_SCALE = float(HD ** -0.5)
RMS_EPS, LN_EPS = 1e-6, 1e-5


def decoder_layer(nc, io):
    with ExitStack() as ctx:
        def sb(name, shape, dt=F32):
            return ctx.enter_context(nc.sbuf_tensor(name, shape, dt))

        def ps(name):
            return ctx.enter_context(nc.psum_tensor(name, [128, 512], F32))

        def sem(name):
            return ctx.enter_context(nc.semaphore(name))

        def f32(t):
            return t.bitcast(F32)

        x2_hbm = nc.dram_tensor("x2_hbm", (B, S, D), F32).ap()

        ident = sb("ident", [128, 128])
        identb = sb("identb", [128, 128], BF16)
        causal = sb("causal", [128, 128])
        causalb = sb("causalb", [128, 128], BF16)
        cosine = sb("cosine", [128, DR])
        sine = sb("sine", [128, DR])
        groupsel = sb("groupsel", [128, HALF])
        eidx = sb("eidx", [128, E])
        mhalf = sb("mhalf", [128, 1])
        rms_eps = sb("rms_eps", [128, 1])
        ln_eps = sb("ln_eps", [128, 1])
        carry = sb("carry", [128, 1])
        wah = sb("wah", [128, KT_D, 320], F32R)
        wal = sb("wal", [128, KT_D, 320], F32R)
        with nc.sbuf_tensor("stage1", [128, 4096], F32) as stage1:
            pass
        wfcl = sb("wfcl", [128, KT_D, E, D], F32R)
        stage2 = sb("stage2", [128, 4096])
        wqnT = stage1[:].rearrange("p (h a) -> p h a", h=H)
        wo_s = stage2[:].rearrange("p (h c) -> p h c", h=H)
        qln = sb("qln", [128, 2])
        kvln = sb("kvln", [128, KL])
        WQh = sb("WQh", [128, 2, H, 128], F32R)
        WQl = sb("WQl", [128, 2, H, 128], F32R)
        VO = sb("VO", [128, H // 2, D])
        xwh = sb("xwh", [128, KT_D, 640], F32R)
        xwl = sb("xwl", [128, KT_D, 640], F32R)
        bqkv = sb("bqkv", [128, 384])
        bo = sb("bo", [128, D])
        ssmask8 = sb("ssmask8", [128, 128], U8)
        ssmask = sb("ssmask", [128, 128], BF16)
        wr = sb("wr", [128, KT_D, E])
        wfch = sb("wfch", [128, KT_D, E, D], F32R)
        wfc = stage1[:].rearrange("p (k e d) -> p k e d", k=KT_D, e=E)
        wpj = stage2[:].rearrange("p (e k c) -> p e k c", e=E, k=KT_D)
        xT = sb("xT", [128, KT_D, 128])
        xTh = sb("xTh", [128, KT_D, 128], F32R)
        xTl = sb("xTl", [128, KT_D, 128], F32R)
        x_res = sb("x_res", [128, D])
        sqj = sb("sqj", [128, QL])
        ms = sb("ms", [128, 2])
        mse = sb("mse", [128, 2])
        rstd = sb("rstd", [128, 2])
        qn = sb("qn", [128, 256])
        qraw = sb("qraw", [128, QB])
        kv = sb("kv", [128, 129])
        kc = sb("kc", [128, DR])
        ks = sb("ks", [128, DR])
        qAh = sb("qAh", [128, 128], F32R)
        qAl = sb("qAl", [128, 128], F32R)
        qBs = sb("qBs", [128, 128], F32R)
        KT = sb("KT", [128, 128])
        Qs = sb("Qs", [128, HC, 128])
        rsin = sb("rsin", [128, HC, DR])
        rcos = sb("rcos", [128, HC, DR])
        QT = sb("QT", [128, HC * 128])
        mxa = sb("mxa", [128, HC])
        Pa = sb("Pa", [128, 2, 512])
        PTa = sb("PTa", [128, 2, 512])
        rec = sb("rec", [128, HC])
        Oa = sb("Oa", [128, HC, KL])
        OTa = sb("OTa", [128, H // 2, 128])
        r1 = sb("r1", [128, D])
        st1 = sb("st1", [128, 6])
        mv1 = sb("mv1", [128, 2])
        ve1 = sb("ve1", [128, 1])
        rs1 = sb("rs1", [128, 1])
        x1 = sb("x1", [128, D])
        ctxT = sb("ctxT", [128, KT_D, 128])
        xch = sb("xch", [128, 4, 128], F32R)
        xcl = sb("xcl", [128, 4, 128], F32R)
        x1b = sb("x1b", [128, D])
        qkv = sb("qkv", [128, 384])
        qarr = sb("qarr", [128, NCX, 4, SLOT])
        karr = sb("karr", [128, 2, 2, 2, SLOT])
        vx = sb("vx", [128, G, HD + 1])
        QX = sb("QX", [128, NCX, 128], F32R)
        KX = sb("KX", [128, 2, HALF, 128], F32R)
        pad8 = sb("pad8", [128, 128], U8)
        comb = sb("comb", [128, 128], BF16)
        mxx = sb("mxx", [128, NCX, HC])
        Px = sb("Px", [128, 2, 512])
        PTx = sb("PTx", [128, 2, 512])
        den = sb("den", [128, XH])
        recx = sb("recx", [128, XH])
        Ox = sb("Ox", [128, XH, HD])
        OTxh = sb("OTxh", [128, KT_D, 128], F32R)
        OTxl = sb("OTxl", [128, KT_D, 128], F32R)
        r2 = sb("r2", [128, D])
        st2 = sb("st2", [128, 6])
        mv2 = sb("mv2", [128, 2])
        ve2 = sb("ve2", [128, 1])
        rs2 = sb("rs2", [128, 1])
        x2 = sb("x2", [128, D])
        setup_only = ExitStack()

        def loaded(name, shape, dt=F32):
            return setup_only.enter_context(nc.sbuf_tensor(name, shape, dt))

        stage3 = loaded("stage3", [128, 4096])
        wkT = stage3[:, 0:1024].rearrange("p (h c) -> p h c", h=H)
        wvT = stage3[:, 1024:2048].rearrange("p (h c) -> p h c", h=H)
        wpe = stage3[:, 2048:4096].rearrange("p (k h c) -> p k h c", k=2, h=H)
        wa = loaded("wa", [128, KT_D, 320])
        xw = loaded("xw", [128, KT_D, 640])
        setup_only.close()
        x2c = sb("x2c", [128, TC, D])
        x2T = sb("x2T", [128, KT_D, TC * 128])
        x2Th = sb("x2Th", [128, KT_D, TC * 128], F32R)
        x2Tl = sb("x2Tl", [128, KT_D, TC * 128], F32R)
        lg = sb("lg", [128, TC, E])
        top = sb("top", [128, TC, E])
        topi = sb("topi", [128, TC, E], U32)
        topf = sb("topf", [128, TC, 2])
        dd = sb("dd", [128, TC])
        p2e = sb("p2e", [128, TC])
        p2d = sb("p2d", [128, TC])
        pr = sb("pr", [128, TC, 2])
        oh1 = sb("oh1", [128, TC, E])
        oh2 = sb("oh2", [128, TC, E])
        wt = sb("wt", [128, TC, E])
        hr = sb("hr", [128, 2, 512])
        h2 = sb("h2", [128, 2, KT_D, 512])
        acc = sb("acc", [128, TC, D])
        st3 = sb("st3", [128, TC, 6])
        mv3 = sb("mv3", [128, TC, 2])
        ve3 = sb("ve3", [128, TC])
        rs3 = sb("rs3", [128, TC])

        qb, ob = ps("qb"), ps("ob")
        sa = [ps("sa0"), ps("sa1")]
        mb, xo = ps("mb"), ps("xo")
        sx = [ps("sx0"), ps("sx1")]

        d_ld = sem("d_ld")
        c_ok = sem("c_ok")
        c_lo = sem("c_lo")
        s_p = sem("s_p")
        s_hi = sem("s_hi")
        s_lo = sem("s_lo")
        wf_ld = sem("wf_ld")
        wf_ok = sem("wf_ok")
        d_x = sem("d_x")
        d_xr = sem("d_xr")
        d_c = sem("d_c")
        d_x2 = sem("d_x2")
        a_xs = sem("a_xs")
        p_a = sem("p_a")
        a_sq = sem("a_sq")
        g_rs = sem("g_rs")
        v_qk = sem("v_qk")
        g_qk = sem("g_qk")
        p_aT = sem("p_aT")
        a_aT = sem("a_aT")
        v_aT = sem("v_aT")
        p_q = sem("p_q")
        a_q = sem("a_q")
        v_rp = sem("v_rp")
        g_rp = sem("g_rp")
        p_qT = sem("p_qT")
        v_qT = sem("v_qT")
        p_s = sem("p_s")
        v_mx = sem("v_mx")
        v_sub = sem("v_sub")
        a_ex = sem("a_ex")
        p_pT = sem("p_pT")
        a_pT = sem("a_pT")
        p_pv = sem("p_pv")
        v_rc = sem("v_rc")
        v_o = sem("v_o")
        p_oT = sem("p_oT")
        a_oT = sem("a_oT")
        p_y = sem("p_y")
        v_l1 = sem("v_l1")
        g_l1 = sem("g_l1")
        v_x1 = sem("v_x1")
        q_xT = sem("q_xT")
        b_xs = sem("b_xs")
        w_xs = sem("w_xs")
        g_x1 = sem("g_x1")
        q_qkv = sem("q_qkv")
        w_qkv = sem("w_qkv")
        b_ar = sem("b_ar")
        g_ar = sem("g_ar")
        q_kT = sem("q_kT")
        w_kx = sem("w_kx")
        q_qx = sem("q_qx")
        b_qx = sem("b_qx")
        w_cm = sem("w_cm")
        q_s = sem("q_s")
        w_mx = sem("w_mx")
        w_sub = sem("w_sub")
        b_ex = sem("b_ex")
        q_pT = sem("q_pT")
        b_pT = sem("b_pT")
        q_pv = sem("q_pv")
        w_o = sem("w_o")
        q_oT = sem("q_oT")
        b_oT = sem("b_oT")
        w_oT = sem("w_oT")
        q_y = sem("q_y")
        w_l2 = sem("w_l2")
        g_l2 = sem("g_l2")
        w_x2 = sem("w_x2")
        f_ld = sem("f_ld")
        f_T = sem("f_T")
        f_hi = sem("f_hi")
        f_lo = sem("f_lo")
        f_lg = sem("f_lg")
        f_v = sem("f_v")
        f_p2 = sem("f_p2")
        f_h = sem("f_h")
        f_r = sem("f_r")
        f_sq = sem("f_sq")
        f_y = sem("f_y")
        f_ac = sem("f_ac")
        f_ln = sem("f_ln")
        f_gl = sem("f_gl")
        f_st = sem("f_st")

        def have(eng, s, i, per, k):
            eng.wait_ge(s, i * per + k)

        def freed(eng, s, i, per, k):
            if not isinstance(i, int) or i > 0:
                eng.wait_ge(s, i * per + (k - per))

        def earlier(eng, s, c, per, k):
            if not isinstance(c, int) or (c == 0 and k > 0):
                eng.wait_ge(s, c * per + k)

        N_CONST, N_LO = 13, 4
        F_V, F_LN, F_AC = 13, 3 * TC, 1 + TC * E
        n_setup = 18
        SETUP = 16 * n_setup

        block = ctx.enter_context(nc.Block())

        @block.sync
        def _(sp):
            def bc(ap, n):
                return ap.partition_broadcast(128)
            loads = [
                (ident[:], io["c_ident"]), (causal[:], io["c_causal"]), (cosine[:], io["c_cos"]),
                (wa[:], io["wa"].rearrange("(k p) n -> p k n", p=128)),
                (qln[:], io["qln"]), (kvln[:], bc(io["kvln"], KL)),
                (sine[:], io["c_sin"]), (groupsel[:], io["c_groupsel"]), (eidx[:], io["c_eidx"]),
                (wqnT, io["wqnT"]), (stage3[:, 0:2048].rearrange("p (k h c) -> p k h c", k=2, h=H), io["wkvT"]),
                (wpe, io["wpe"]), (wo_s, io["wo"].rearrange("(h p) c -> p h c", p=128)),
                (xw[:], io["xw"].rearrange("(k p) n -> p k n", p=128)),
                (bqkv[:], bc(io["bqkv"], 384)), (bo[:], bc(io["bo"], D)),
                (ssmask8[:], io["ssmask"]), (wr[:], io["wr"].rearrange("(k p) n -> p k n", p=128)),
            ]
            assert len(loads) == n_setup
            for dst, src in loads:
                sp.dma_start(dst, src).then_inc(d_ld, 16)

            def load_x(i):
                freed(sp, a_xs, i, 2, 2)
                sp.dma_start(xT[:], io["xT"][:, :, bass.ds(i * S, S)]).then_inc(d_x, 16)
                freed(sp, v_l1, i, 3, 1)
                sp.dma_start(x_res[:], io["x"][i]).then_inc(d_xr, 16)

            def load_ctx(i):
                freed(sp, b_xs, i, 2, 2)
                freed(sp, w_xs, i, 2, 2)
                sp.dma_start(ctxT[:], io["ctxT"][:, :, bass.ds(i * S, S)]).then_inc(d_c, 16)
                freed(sp, w_cm, i, 1, 1)
                sp.dma_start(pad8[:], io["padmask"][i].partition_broadcast(128)).then_inc(d_c, 16)

            def store_x2(i):
                have(sp, w_x2, i, 1, 1)
                sp.dma_start(x2_hbm[i], x2[:]).then_inc(d_x2, 16)

            load_x(0)
            load_ctx(0)
            sp.wait_ge(s_p, 2 * NCA)
            sp.dma_start(wfc, io["wfc"]).then_inc(wf_ld, 16)
            sp.dma_start(wpj, io["wpj"]).then_inc(wf_ld, 16)
            load_x(1)
            load_ctx(1)
            store_x2(0)
            with sp.Fori(2, B) as j:
                load_x(j)
                load_ctx(j)
                store_x2(j - 1)
            store_x2(B - 1)
            sp.wait_ge(d_x2, 16 * B)

            def load_chunk(c):
                sp.dma_start(x2c[:], x2_hbm[bass.ds(c * TC, TC)].rearrange("t p d -> p t d")).then_inc(f_ld, 16)

            def store_chunk(c):
                sp.wait_ge(f_ln, c * F_LN + F_LN)
                sp.dma_start(io["out"][bass.ds(c * TC, TC)].rearrange("t p d -> p t d"), acc[:]).then_inc(f_st, 16)

            load_chunk(0)
            with sp.Fori(1, NCH) as c:
                sp.wait_ge(f_ac, c * F_AC + (1 - F_AC))
                load_chunk(c)
                store_chunk(c - 1)
            store_chunk(NCH - 1)
            sp.wait_ge(f_st, 16 * NCH)

        @block.tensor
        def _(pe):
            pe.wait_ge(c_ok, N_CONST)
            for n in range(NCA):
                if n >= 2:
                    pe.wait_ge(s_lo, 2 * (n - 2) + 2)
                bank = sa[n % 2]
                for j in range(HC):
                    h = HC * n + j
                    pe.matmul(bank[:, j * KL:(j + 1) * KL], wqnT[:, h, 0:128], wkT[:, h, :], start=True, stop=True)
                    last = pe.matmul(bank[:, 256 + j * KL:256 + (j + 1) * KL], wqnT[:, h, 128:256], wkT[:, h, :],
                                     start=True, stop=True)
                last.then_inc(s_p, 1)
                if n >= 2:
                    pe.wait_ge(s_hi, 3 * (n - 2) + 3)
                bank = sx[n % 2]
                for j in range(HC):
                    h = HC * n + j
                    last = pe.matmul(bank[64 * (j % 2):64 * (j % 2) + 64, (j // 2) * D:(j // 2 + 1) * D],
                                     wvT[:, h, :], wo_s[:, h, :], start=True, stop=True)
                last.then_inc(s_p, 1)
            pe.wait_ge(s_lo, 2 * NCA)
            pe.wait_ge(s_hi, 3 * NCA)
            pe.wait_ge(c_lo, N_LO)

            def split_matmul(out, terms):
                for k, (w, m) in enumerate(terms):
                    last = pe.matmul(out, w, m, start=(k == 0), stop=(k == len(terms) - 1))
                return last

            def mla_latents(i):
                have(pe, a_xs, i, 2, 2)
                freed(pe, v_l1, i, 3, 1)
                terms = []
                for k in range(KT_D):
                    terms += [(xTh[:, k, :], wah[:, k, :]), (xTh[:, k, :], wal[:, k, :]), (xTl[:, k, :], wah[:, k, :])]
                split_matmul(ob[:, 0:320], terms).then_inc(p_a, 1)

            def mla_latents_T(i):
                have(pe, g_qk, i, 3, 3)
                have(pe, v_qk, i, 5, 5)
                freed(pe, v_qT, i, NCA, NCA)
                pe.transpose(qb[:, 0:128], qn[:, 0:128], ident[:])
                pe.transpose(qb[:, 128:256], qn[:, 128:256], ident[:])
                pe.transpose(qb[:, 256:384], kv[:, 0:128], ident[:]).then_inc(p_aT, 1)

            def mla_query(i, n):
                if n == 0:
                    have(pe, a_aT, i, 3, 3)
                    have(pe, v_aT, i, 1, 1)
                else:
                    have(pe, v_qT, i, NCA, n)
                hs = slice(HC * n, HC * n + HC)
                split_matmul(qb[:], [(qAh[:], WQh[:, 0, hs, :]), (qAh[:], WQl[:, 0, hs, :]), (qAl[:], WQh[:, 0, hs, :]),
                                     (qBs[:], WQh[:, 1, hs, :]), (qBs[:], WQl[:, 1, hs, :])]).then_inc(p_q, 1)

            def mla_query_T(i, n):
                have(pe, g_rp, i, 2 * NCA, 2 * n + 2)
                for j in range(HC):
                    last = pe.transpose(qb[:, j * 128:(j + 1) * 128], Qs[:, j, :], ident[:])
                last.then_inc(p_qT, 1)

            def mla_scores(i, n):
                have(pe, v_qT, i, NCA, n + 1)
                if n >= 2:
                    have(pe, a_pT, i, NCA, n - 1)
                else:
                    freed(pe, a_pT, i, NCA, n + 3)
                bank = sa[n % 2]
                for j in range(HC):
                    pe.matmul(bank[:, j * 128:(j + 1) * 128], QT[:, j * 128:(j + 1) * 128], KT[:],
                              start=(j == 0), stop=False, skip_group_check=True)
                pe.matmul(bank[:], identb[:], causalb[:].unsqueeze(1).to_broadcast([128, HC, 128]),
                          start=False, stop=True, skip_group_check=True).then_inc(p_s, 1)

            def mla_probs_T(i, n):
                have(pe, a_ex, i, NCA, n + 1)
                for j in range(HC):
                    last = pe.transpose(sa[n % 2][:, j * 128:(j + 1) * 128], Pa[:, n % 2, j * 128:(j + 1) * 128], ident[:])
                last.then_inc(p_pT, 1)

            def mla_values(i, n):
                have(pe, a_pT, i, NCA, n + 1)
                if n > 0:
                    have(pe, a_oT, i, NCA, n)
                for j in range(HC):
                    last = pe.matmul(ob[:, j * 65:(j + 1) * 65], PTa[:, n % 2, j * 128:(j + 1) * 128], kv[:, 64:129],
                                     start=True, stop=True)
                last.then_inc(p_pv, 1)

            def mla_out_T(i, n):
                have(pe, v_o, i, NCA, n + 1)
                for k in range(2):
                    last = pe.transpose(ob[:, k * 128:(k + 1) * 128],
                                        Oa[:, 2 * k:2 * k + 2, :].rearrange("p h c -> p (h c)"), ident[:])
                last.then_inc(p_oT, 1)

            def mla_project(i):
                have(pe, a_oT, i, NCA, NCA)
                split_matmul(ob[:, 0:D], [(OTa[:, k, :], VO[:, k, :]) for k in range(H // 2)]).then_inc(p_y, 1)

            def xat_x_T(i):
                have(pe, v_x1, i, 1, 1)
                freed(pe, w_oT, i, 1, 1)
                for k in range(KT_D):
                    last = pe.transpose(mb[:, k * 128:(k + 1) * 128], x1[:, k * 128:(k + 1) * 128], ident[:])
                last.then_inc(q_xT, 1)

            def xat_qkv(i):
                have(pe, b_xs, i, 2, 2)
                have(pe, w_xs, i, 2, 2)
                freed(pe, w_l2, i, 3, 1)
                for lo, hi, t0 in ((0, 256, 0), (256, 384, 2)):
                    terms = []
                    for k in range(KT_D):
                        terms += [(xch[:, t0 + k, :], xwh[:, k, lo:hi]), (xch[:, t0 + k, :], xwl[:, k, lo:hi]),
                                  (xcl[:, t0 + k, :], xwh[:, k, lo:hi])]
                    last = split_matmul(xo[:, lo:hi], terms)
                last.then_inc(q_qkv, 1)

            def xat_keys_T(i):
                have(pe, b_ar, i, 2, 2)
                have(pe, g_ar, i, 3, 3)
                for k in range(2):
                    last = pe.transpose(mb[:, k * 128:(k + 1) * 128],
                                        karr[:, k].rearrange("p a b c -> p (a b c)"), ident[:])
                last.then_inc(q_kT, 1)

            def xat_queries_T(i, half):
                freed(pe, b_pT, i, NCX, NCX - 1 + half)
                for r in range(HC):
                    last = pe.transpose(sx[half][:, r * 128:(r + 1) * 128],
                                        qarr[:, half * HC + r].rearrange("p a b -> p (a b)"), ident[:])
                last.then_inc(q_qx, 1)

            def xat_scores(i, n):
                if n == 0:
                    have(pe, w_kx, i, 1, 1)
                    have(pe, w_cm, i, 1, 1)
                if n < 2:
                    have(pe, b_qx, i, 2, n + 1)
                else:
                    have(pe, b_pT, i, NCX, n - 1)
                bank = sx[n % 2]
                pe.matmul(bank[:], identb[:], comb[:].unsqueeze(1).to_broadcast([128, HC, 128]), start=True, stop=False)
                pe.matmul(bank[:], QX[:, n, :], KX[:, n // HC].rearrange("p g s -> p (g s)"), start=False, stop=True)\
                  .then_inc(q_s, 1)

            def xat_probs_T(i, n):
                have(pe, b_ex, i, NCX, n + 1)
                for j in range(HC):
                    last = pe.transpose(sx[n % 2][:, j * 128:(j + 1) * 128], Px[:, n % 2, j * 128:(j + 1) * 128], ident[:])
                last.then_inc(q_pT, 1)

            def xat_values(i, n):
                have(pe, b_pT, i, NCX, n + 1)
                for j in range(HC):
                    c = (n * HC + j) * (HD + 1)
                    last = pe.matmul(xo[:, c:c + HD + 1], PTx[:, n % 2, j * 128:(j + 1) * 128],
                                     vx[:, (n // HC) * HALF + j, :], start=True, stop=True)
                last.then_inc(q_pv, 1)

            def xat_out_T(i):
                have(pe, w_o, i, 3, 3)
                for k in range(KT_D):
                    last = pe.transpose(mb[:, k * 128:(k + 1) * 128],
                                        Ox[:, k * 16:(k + 1) * 16, :].rearrange("p h c -> p (h c)"), ident[:])
                last.then_inc(q_oT, 1)

            def xat_project(i):
                have(pe, b_oT, i, 1, 1)
                have(pe, w_oT, i, 1, 1)
                terms = []
                for k in range(KT_D):
                    terms += [(OTxh[:, k, :], xwh[:, k, 384:640]), (OTxh[:, k, :], xwl[:, k, 384:640]),
                              (OTxl[:, k, :], xwh[:, k, 384:640])]
                split_matmul(xo[:, 0:D], terms).then_inc(q_y, 1)

            def step(i, x):
                ma, xa = i is not None, x is not None
                if xa: xat_x_T(x)
                if ma: mla_latents(i)
                if xa: xat_qkv(x)
                if ma: mla_latents_T(i)
                if ma: mla_query(i, 0)
                if xa:
                    xat_keys_T(x)
                    xat_queries_T(x, 0)
                    xat_queries_T(x, 1)
                if ma: mla_query_T(i, 0)
                if xa:
                    xat_scores(x, 0)
                    xat_scores(x, 1)
                if ma: mla_scores(i, 0)
                for n in range(NCA):
                    if ma and n + 1 < NCA: mla_query(i, n + 1)
                    if xa: xat_probs_T(x, 2 * n)
                    if ma: mla_probs_T(i, n)
                    if xa: xat_values(x, 2 * n)
                    if xa and n + 1 < NCA: xat_scores(x, 2 * n + 2)
                    if ma and n > 0: mla_out_T(i, n - 1)
                    if ma and n + 1 < NCA: mla_query_T(i, n + 1)
                    if xa: xat_probs_T(x, 2 * n + 1)
                    if ma: mla_values(i, n)
                    if ma and n + 1 < NCA: mla_scores(i, n + 1)
                    if xa: xat_values(x, 2 * n + 1)
                    if xa and n + 1 < NCA: xat_scores(x, 2 * n + 3)
                if xa: xat_out_T(x)
                if ma: mla_out_T(i, NCA - 1)
                if xa: xat_project(x)
                if ma: mla_project(i)

            step(0, None)
            step(1, 0)
            with pe.Fori(2, B) as j:
                step(j, j - 1)
            step(None, B - 1)

            pe.wait_ge(wf_ok, 2)
            hb, yb = [sa[0], sa[1]], [sx[0], sx[1]]

            def chunk(c):
                pe.wait_ge(f_ld, c * 16 + 16)
                for k in range(KT_D):
                    bank = (qb, mb)[k]
                    for t in range(TC):
                        last = pe.transpose(bank[:, t * 128:(t + 1) * 128], x2c[:, t, k * 128:(k + 1) * 128], ident[:])
                    last.then_inc(f_T, 1)
                pe.wait_ge(f_lo, c * KT_D + KT_D)
                for t in range(TC):
                    split_matmul(ob[:, t * E:(t + 1) * E],
                                 [(x2T[:, k, t * 128:(t + 1) * 128], wr[:, k, :]) for k in range(KT_D)])\
                        .then_inc(f_lg, 1)
                def hidden(e):
                    for m in range(2):
                        earlier(pe, f_r, c, 2 * E, 2 * (e - 1) + m + 1)
                        terms = []
                        for k in range(KT_D):
                            w = slice(m * 128, (m + 1) * 128)
                            terms += [(wfch[:, k, e, w], x2Th[:, k, :]), (wfcl[:, k, e, w], x2Th[:, k, :]),
                                      (wfch[:, k, e, w], x2Tl[:, k, :])]
                        split_matmul(hb[m][:], terms).then_inc(f_h, 1)

                def project(e):
                    pe.wait_ge(f_sq, c * (2 * E) + (2 * e + 2))
                    for q in range(2):
                        earlier(pe, f_ac, c, F_AC, (e - 1) * TC + 2 * q + 3 - (e == 0))
                        for u in range(2):
                            t = 2 * q + u
                            last = split_matmul(yb[q][:, u * D:(u + 1) * D],
                                                [(h2[:, e % 2, k, t * 128:(t + 1) * 128], wpj[:, e, k, :]) for k in range(KT_D)])
                        last.then_inc(f_y, 1)

                hidden(0)
                for e in range(E):
                    if e + 1 < E:
                        hidden(e + 1)
                    project(e)

            chunk(0)
            with pe.Fori(1, NCH) as c:
                chunk(c)

        @block.scalar
        def _(act):
            act.wait_ge(d_ld, SETUP)
            act.activation(identb[:], ident[:], ACT.Copy).then_inc(c_ok, 1)
            act.activation(causalb[:], causal[:], ACT.Copy).then_inc(c_ok, 1)
            act.activation(wah[:], wa[:], ACT.Copy).then_inc(c_ok, 1)
            act.activation(xwh[:], xw[:], ACT.Copy).then_inc(c_ok, 1)
            act.activation(ssmask[:], ssmask8[:], ACT.Copy, scale=-BIG).then_inc(c_ok, 1)
            for k in range(2):
                act.activation(WQh[:, k, :, 0:DR], wpe[:, k], ACT.Copy, scale=qln[:, k:k + 1]).then_inc(c_ok, 1)
            for n in range(NCA):
                hs = slice(HC * n, HC * n + HC)
                act.wait_ge(s_p, 2 * n + 1)
                for k in range(2):
                    act.activation(WQh[:, k, hs, DR:128],
                                   sa[n % 2][:, k * 256:(k + 1) * 256].rearrange("p (h c) -> p h c", h=HC),
                                   ACT.Copy, scale=qln[:, k:k + 1]).then_inc(s_hi, 1)
                act.wait_ge(s_p, 2 * n + 2)
                act.activation(VO[:, 2 * n:2 * n + 2, :], sx[n % 2][:].rearrange("p (k c) -> p k c", k=2), ACT.Copy)\
                   .then_inc(s_hi, 1)

            def mla_split(i):
                have(act, d_x, i, 16, 16)
                freed(act, p_a, i, 1, 1)
                act.activation(xTh[:], xT[:], ACT.Copy).then_inc(a_xs, 1)

            def mla_squares(i):
                have(act, p_a, i, 1, 1)
                freed(act, g_rs, i, 2, 2)
                act.activation(sqj[:], ob[:, 0:QL], ACT.Square, scale=float(QL ** -0.5), accum_out=ms[:, 0:1]).then_inc(a_sq, 1)
                act.wait_ge(a_sq, i * 2 + 1)
                act.activation(sqj[:, 0:KL], ob[:, QL:QL + KL], ACT.Square, scale=float(KL ** -0.5),
                               accum_out=ms[:, 1:2]).then_inc(a_sq, 1)

            def mla_latents_take(i):
                have(act, p_aT, i, 1, 1)
                act.activation(qAh[:], qb[:, 0:128], ACT.Copy).then_inc(a_aT, 1)
                act.activation(qBs[:], qb[:, 128:256], ACT.Copy).then_inc(a_aT, 1)
                act.activation(KT[:], qb[:, 256:384], ACT.Copy).then_inc(a_aT, 1)

            def mla_query_take(i, n):
                have(act, p_q, i, NCA, n + 1)
                act.activation(Qs[:].rearrange("p h c -> p (h c)"), qb[:], ACT.Copy).then_inc(a_q, 1)

            def mla_exp(i, n):
                have(act, v_sub, i, NCA, n + 1)
                act.activation(Pa[:, n % 2, :], Pa[:, n % 2, :], ACT.Exp, scale=MLA_SCALE).then_inc(a_ex, 1)

            def mla_probs_take(i, n):
                have(act, p_pT, i, NCA, n + 1)
                if n >= 2:
                    have(act, p_pv, i, NCA, n - 1)
                else:
                    freed(act, p_pv, i, NCA, n + 3)
                act.activation(PTa[:, n % 2, :], sa[n % 2][:], ACT.Copy).then_inc(a_pT, 1)

            def mla_out_take(i, n):
                have(act, p_oT, i, NCA, n + 1)
                act.activation(OTa[:, 2 * n:2 * n + 2, :].rearrange("p k t -> p (k t)"), ob[:, 0:256], ACT.Copy)\
                   .then_inc(a_oT, 1)

            def xat_split(i):
                have(act, d_c, i, 32, 32)
                freed(act, q_qkv, i, 1, 1)
                act.activation(xch[:, 2:4, :], ctxT[:], ACT.Copy).then_inc(b_xs, 1)
                have(act, q_xT, i, 1, 1)
                act.activation(xch[:, 0:2, :].rearrange("p k t -> p (k t)"), mb[:, 0:256], ACT.Copy).then_inc(b_xs, 1)

            def xat_arrange_hi(i):
                have(act, w_qkv, i, 1, 1)
                freed(act, q_qx, i, 2, 2)
                act.activation(qarr[:, :, 0:2, :].bitcast(F32R),
                               qkv[:, 0:256].rearrange("p (n c) -> p n c", n=NCX).unsqueeze(2).to_broadcast([128, NCX, 2, SLOT]),
                               ACT.Copy).then_inc(b_ar, 1)
                act.activation(karr[:, :, :, 0, :].bitcast(F32R),
                               qkv[:, 256:320].rearrange("p (n c) -> p n c", n=2).unsqueeze(2).to_broadcast([128, 2, 2, SLOT]),
                               ACT.Copy).then_inc(b_ar, 1)

            def xat_queries_take(i, half):
                have(act, q_qx, i, 2, half + 1)
                act.activation(QX[:, half * HC:(half + 1) * HC, :].rearrange("p n t -> p (n t)"), sx[half][:], ACT.Copy)\
                   .then_inc(b_qx, 1)

            def xat_exp(i, n):
                have(act, w_sub, i, NCX, n + 1)
                act.activation(Px[:, n % 2, :], Px[:, n % 2, :], ACT.Exp, scale=XAT_SCALE).then_inc(b_ex, 1)

            def xat_probs_take(i, n):
                have(act, q_pT, i, NCX, n + 1)
                if n >= 2:
                    have(act, q_pv, i, NCX, n - 1)
                else:
                    freed(act, q_pv, i, NCX, n + NCX - 1)
                act.activation(PTx[:, n % 2, :], sx[n % 2][:], ACT.Copy).then_inc(b_pT, 1)

            def xat_out_take(i):
                have(act, q_oT, i, 1, 1)
                act.activation(OTxh[:].rearrange("p k t -> p (k t)"), mb[:, 0:256], ACT.Copy).then_inc(b_oT, 1)

            def step(i, x):
                ma, xa = i is not None, x is not None
                if ma: mla_split(i)
                if xa: xat_split(x)
                if ma: mla_squares(i)
                if xa: xat_arrange_hi(x)
                if ma: mla_latents_take(i)
                if ma: mla_query_take(i, 0)
                if xa:
                    xat_queries_take(x, 0)
                    xat_queries_take(x, 1)
                if xa:
                    xat_exp(x, 0)
                if ma: mla_exp(i, 0)
                for n in range(NCA):
                    if ma and n + 1 < NCA: mla_query_take(i, n + 1)
                    if xa: xat_probs_take(x, 2 * n)
                    if xa: xat_exp(x, 2 * n + 1)
                    if ma: mla_probs_take(i, n)
                    if ma and n > 0: mla_out_take(i, n - 1)
                    if xa: xat_probs_take(x, 2 * n + 1)
                    if xa and n + 1 < NCA: xat_exp(x, 2 * n + 2)
                    if ma and n + 1 < NCA: mla_exp(i, n + 1)
                if xa: xat_out_take(x)
                if ma: mla_out_take(i, NCA - 1)

            step(0, None)
            step(1, 0)
            with act.Fori(2, B) as j:
                step(j, j - 1)
            step(None, B - 1)

            def chunk(c):
                for k in range(KT_D):
                    act.wait_ge(f_T, c * KT_D + (k + 1))
                    act.activation(x2T[:, k, :], (qb, mb)[k][:], ACT.Copy).then_inc(f_hi, 1)
                    act.activation(x2Th[:, k, :], (qb, mb)[k][:], ACT.Copy).then_inc(f_hi, 1)
                act.wait_ge(f_v, c * F_V + 3)
                act.activation(p2e[:], dd[:], ACT.Exp).then_inc(f_p2, 1)
                for e in range(E):
                    for m in range(2):
                        act.wait_ge(f_h, c * (2 * E) + (2 * e + m + 1))
                        earlier(act, f_sq, c, 2 * E, 2 * (e - 1) + m + 1)
                        act.activation(hr[:, m, :], sa[m][:], ACT.Relu).then_inc(f_r, 1)

            chunk(0)
            with act.Fori(1, NCH) as c:
                chunk(c)

        @block.vector
        def _(dve):
            dve.memset(mhalf[:], -0.5).then_inc(c_ok, 1)
            dve.memset(rms_eps[:], RMS_EPS).then_inc(c_ok, 1)
            dve.memset(ln_eps[:], LN_EPS).then_inc(c_ok, 1)
            dve.memset(kv[:, 128:129], 1.0).then_inc(c_ok, 1)
            dve.memset(vx[:, :, HD:HD + 1], 1.0).then_inc(c_ok, 1)
            dve.wait_ge(d_ld, SETUP)
            dve.tensor_tensor(stage3[:, 0:2048].rearrange("p (h c) -> p h c", c=KL),
                              stage3[:, 0:2048].rearrange("p (h c) -> p h c", c=KL),
                              kvln[:].unsqueeze(1).to_broadcast([128, 2 * H, KL]), ALU.mult).then_inc(c_ok, 1)
            dve.wait_ge(c_ok, N_CONST)
            dve.tensor_tensor(wal[:], wa[:], f32(wah[:]), ALU.subtract).then_inc(c_lo, 1)
            dve.tensor_tensor(xwl[:], xw[:], f32(xwh[:]), ALU.subtract).then_inc(c_lo, 1)
            for k in range(2):
                dve.scalar_tensor_tensor(WQl[:, k, :, 0:DR], wpe[:, k], qln[:, k:k + 1], f32(WQh[:, k, :, 0:DR]),
                                         ALU.mult, ALU.subtract).then_inc(c_lo, 1)
            for n in range(NCA):
                hs = slice(HC * n, HC * n + HC)
                for k in range(2):
                    dve.wait_ge(s_hi, 3 * n + 2)
                    dve.scalar_tensor_tensor(WQl[:, k, hs, DR:128],
                                             sa[n % 2][:, k * 256:(k + 1) * 256].rearrange("p (h c) -> p h c", h=HC),
                                             qln[:, k:k + 1], f32(WQh[:, k, hs, DR:128]), ALU.mult, ALU.subtract)\
                       .then_inc(s_lo, 1)

            def mla_split(i):
                have(dve, a_xs, i, 2, 1)
                dve.tensor_tensor(xTl[:], xT[:], f32(xTh[:]), ALU.subtract).then_inc(a_xs, 1)

            def mla_normalise(i):
                have(dve, g_rs, i, 2, 2)
                freed(dve, p_aT, i, 1, 1)
                freed(dve, g_qk, i, 3, 3)
                freed(dve, p_pv, i, NCA, NCA)
                dve.tensor_scalar(qraw[:], ob[:, 128:QL], rstd[:, 0:1], None, ALU.mult).then_inc(v_qk, 1)
                dve.tensor_tensor(kc[:], ob[:, 256:320], cosine[:], ALU.mult).then_inc(v_qk, 1)
                dve.tensor_tensor(ks[:].rearrange("p (a c) -> p a c", a=2),
                                  ob[:, 256:320].rearrange("p (a c) -> p a c", a=2)[:, ::-1, :],
                                  sine[:].rearrange("p (a c) -> p a c", a=2), ALU.mult).then_inc(v_qk, 1)
                dve.tensor_scalar(qn[:, 0:128], ob[:, 0:128], rstd[:, 0:1], None, ALU.mult).then_inc(v_qk, 1)
                dve.tensor_scalar(kv[:, 64:128], ob[:, QL:QL + KL], rstd[:, 1:2], None, ALU.mult).then_inc(v_qk, 1)

            def mla_latents_lo(i):
                have(dve, a_aT, i, 3, 3)
                dve.tensor_tensor(qAl[:], qb[:, 0:128], f32(qAh[:]), ALU.subtract).then_inc(v_aT, 1)

            def mla_rotate_sine(i, n):
                have(dve, a_q, i, NCA, n + 1)
                if n > 0:
                    have(dve, g_rp, i, 2 * NCA, 2 * n)
                else:
                    freed(dve, g_rp, i, 2 * NCA, 2 * NCA)
                dve.tensor_tensor(rsin[:].rearrange("p h (a c) -> p h a c", a=2),
                                  Qs[:, :, 0:DR].rearrange("p h (a c) -> p h a c", a=2)[:, :, ::-1, :],
                                  sine[:].rearrange("p (a c) -> p a c", a=2).unsqueeze(1).to_broadcast([128, HC, 2, DR // 2]),
                                  ALU.mult).then_inc(v_rp, 1)

            def mla_query_T_take(i, n):
                have(dve, p_qT, i, NCA, n + 1)
                if n > 0:
                    have(dve, p_s, i, NCA, n)
                else:
                    freed(dve, p_s, i, NCA, NCA)
                dve.tensor_copy(QT[:], qb[:]).then_inc(v_qT, 1)

            def mla_max(i, n):
                have(dve, p_s, i, NCA, n + 1)
                if n > 0:
                    have(dve, v_sub, i, NCA, n)
                else:
                    freed(dve, v_sub, i, NCA, NCA)
                bank = sa[n % 2][:].rearrange("p (h s) -> p h s", h=HC)
                dve.tensor_reduce(mxa[:], bank, AX.X, ALU.max).then_inc(v_mx, 1)
                have(dve, v_mx, i, NCA, n + 1)
                dve.tensor_tensor(Pa[:, n % 2, :].rearrange("p (h s) -> p h s", h=HC), bank,
                                  mxa[:].unsqueeze(2).to_broadcast([128, HC, 128]), ALU.subtract).then_inc(v_sub, 1)

            def mla_out_norm(i, n):
                have(dve, p_pv, i, NCA, n + 1)
                if n > 0:
                    have(dve, v_o, i, NCA, n)
                else:
                    freed(dve, v_o, i, NCA, NCA)
                o = ob[:, 0:HC * 65].rearrange("p (h c) -> p h c", h=HC)
                dve.reciprocal(rec[:].unsqueeze(2), o[:, :, KL:KL + 1]).then_inc(v_rc, 1)
                have(dve, v_rc, i, NCA, n + 1)
                dve.tensor_tensor(Oa[:], o[:, :, 0:KL], rec[:].unsqueeze(2).to_broadcast([128, HC, KL]), ALU.mult)\
                   .then_inc(v_o, 1)

            def mla_norm_stats(i):
                have(dve, p_y, i, 1, 1)
                have(dve, d_xr, i, 16, 16)
                freed(dve, v_x1, i, 1, 1)
                dve.tensor_tensor(r1[:], x_res[:], ob[:, 0:D], ALU.add).then_inc(v_l1, 1)
                have(dve, v_l1, i, 3, 1)
                dve.bn_stats(st1[:], r1[:]).then_inc(v_l1, 1)
                have(dve, v_l1, i, 3, 2)
                freed(dve, g_l1, i, 2, 2)
                dve.tensor_copy(carry[:], st1[:, 0:1])
                dve.bn_aggr(mv1[:], st1[:]).then_inc(v_l1, 1)

            def mla_norm(i):
                have(dve, g_l1, i, 2, 2)
                freed(dve, q_xT, i, 1, 1)
                freed(dve, g_x1, i, 1, 1)
                dve.tensor_scalar(x1[:], r1[:], mv1[:, 0:1], rs1[:], ALU.subtract, ALU.mult).then_inc(v_x1, 1)

            def xat_split(i):
                have(dve, b_xs, i, 2, 1)
                dve.tensor_tensor(xcl[:, 2:4, :], ctxT[:], f32(xch[:, 2:4, :]), ALU.subtract).then_inc(w_xs, 1)
                have(dve, b_xs, i, 2, 2)
                dve.tensor_tensor(xcl[:, 0:2, :].rearrange("p k t -> p (k t)"), mb[:, 0:256],
                                  f32(xch[:, 0:2, :].rearrange("p k t -> p (k t)")), ALU.subtract).then_inc(w_xs, 1)

            def xat_bias(i):
                have(dve, q_qkv, i, 1, 1)
                freed(dve, b_ar, i, 2, 2)
                freed(dve, g_ar, i, 3, 3)
                dve.tensor_tensor(qkv[:], xo[:, 0:384], bqkv[:], ALU.add).then_inc(w_qkv, 1)

            def xat_mask(i):
                have(dve, d_c, i, 32, 32)
                freed(dve, q_s, i, NCX, NCX)
                dve.scalar_tensor_tensor(comb[:], pad8[:], -BIG, ssmask[:], ALU.mult, ALU.add).then_inc(w_cm, 1)

            def xat_keys(i):
                have(dve, q_kT, i, 1, 1)
                freed(dve, q_s, i, NCX, NCX)
                dve.tensor_tensor(KX[:],
                                  mb[:, 0:256].rearrange("p (k s) -> p k s", k=2).unsqueeze(2).to_broadcast([128, 2, HALF, 128]),
                                  groupsel[:].unsqueeze(1).unsqueeze(3).to_broadcast([128, 2, HALF, 128]), ALU.mult)\
                   .then_inc(w_kx, 1)

            def xat_max(i, n):
                have(dve, q_s, i, NCX, n + 1)
                if n == 0:
                    freed(dve, w_o, i, 3, 1)
                bank = sx[n % 2][:].rearrange("p (h s) -> p h s", h=HC)
                dve.tensor_reduce(mxx[:, n, :], bank, AX.X, ALU.max).then_inc(w_mx, 1)
                have(dve, w_mx, i, NCX, n + 1)
                dve.tensor_tensor(Px[:, n % 2, :].rearrange("p (h s) -> p h s", h=HC), bank,
                                  mxx[:, n, :].unsqueeze(2).to_broadcast([128, HC, 128]), ALU.subtract).then_inc(w_sub, 1)

            def xat_out_norm(i):
                have(dve, q_pv, i, NCX, NCX)
                o = xo[:, 0:XH * (HD + 1)].rearrange("p (h c) -> p h c", h=XH)
                dve.scalar_tensor_tensor(den[:].unsqueeze(2), mxx[:].rearrange("p n h -> p (n h)").unsqueeze(2), -BIG / 2,
                                         o[:, :, HD:HD + 1], ALU.is_gt, ALU.mult).then_inc(w_o, 1)
                have(dve, w_o, i, 3, 1)
                dve.reciprocal(recx[:], den[:]).then_inc(w_o, 1)
                have(dve, w_o, i, 3, 2)
                freed(dve, q_oT, i, 1, 1)
                dve.tensor_tensor(Ox[:], o[:, :, 0:HD], recx[:].unsqueeze(2).to_broadcast([128, XH, HD]), ALU.mult)\
                   .then_inc(w_o, 1)

            def xat_out_lo(i):
                have(dve, b_oT, i, 1, 1)
                dve.tensor_tensor(OTxl[:].rearrange("p k t -> p (k t)"), mb[:, 0:256],
                                  f32(OTxh[:].rearrange("p k t -> p (k t)")), ALU.subtract).then_inc(w_oT, 1)

            def xat_norm_stats(i):
                have(dve, q_y, i, 1, 1)
                have(dve, g_x1, i, 1, 1)
                freed(dve, w_x2, i, 1, 1)
                dve.tensor_tensor(r2[:], x1b[:], xo[:, 0:D], ALU.add).then_inc(w_l2, 1)
                have(dve, w_l2, i, 3, 1)
                dve.bn_stats(st2[:], r2[:]).then_inc(w_l2, 1)
                have(dve, w_l2, i, 3, 2)
                freed(dve, g_l2, i, 2, 2)
                dve.tensor_copy(carry[:], st2[:, 0:1])
                dve.bn_aggr(mv2[:], st2[:]).then_inc(w_l2, 1)

            def xat_norm(i):
                have(dve, g_l2, i, 2, 2)
                freed(dve, d_x2, i, 16, 16)
                dve.tensor_scalar(x2[:], r2[:], mv2[:, 0:1], rs2[:], ALU.subtract, ALU.mult).then_inc(w_x2, 1)

            def step(i, x):
                ma, xa = i is not None, x is not None
                if ma: mla_split(i)
                if xa: xat_split(x)
                if xa: xat_mask(x)
                if xa: xat_bias(x)
                if ma: mla_normalise(i)
                if ma: mla_latents_lo(i)
                if xa: xat_keys(x)
                if ma: mla_rotate_sine(i, 0)
                if xa: xat_max(x, 0)
                if ma: mla_query_T_take(i, 0)
                if xa: xat_max(x, 1)
                if ma: mla_max(i, 0)
                for n in range(NCA):
                    if ma and n + 1 < NCA: mla_rotate_sine(i, n + 1)
                    if xa and n + 1 < NCA: xat_max(x, 2 * n + 2)
                    if ma and n + 1 < NCA: mla_query_T_take(i, n + 1)
                    if ma: mla_out_norm(i, n)
                    if xa and n + 1 < NCA: xat_max(x, 2 * n + 3)
                    if ma and n + 1 < NCA: mla_max(i, n + 1)
                if xa:
                    xat_out_norm(x)
                    xat_out_lo(x)
                    xat_norm_stats(x)
                if ma: mla_norm_stats(i)
                if xa: xat_norm(x)
                if ma: mla_norm(i)

            step(0, None)
            step(1, 0)
            with dve.Fori(2, B) as j:
                step(j, j - 1)
            step(None, B - 1)

            def chunk(c):
                def after(k):
                    dve.wait_ge(f_v, c * F_V + k)

                for k in range(KT_D):
                    dve.wait_ge(f_hi, c * (2 * KT_D) + (2 * k + 2))
                    dve.tensor_tensor(x2Tl[:, k, :], x2T[:, k, :], f32(x2Th[:, k, :]), ALU.subtract).then_inc(f_lo, 1)
                dve.wait_ge(f_lg, c * TC + TC)
                dve.tensor_copy(lg[:].rearrange("p t e -> p (t e)"), ob[:, 0:TC * E]).then_inc(f_v, 1)
                after(1)
                if not isinstance(c, int):
                    dve.wait_ge(f_st, c * 16)
                dve.tensor_copy(acc[:], x2c[:]).then_inc(f_ac, 1)
                for t in range(TC):
                    last = dve.max(top[:, t, :], lg[:, t, :])
                last.then_inc(f_v, 1)
                after(2)
                dve.tensor_tensor(dd[:].unsqueeze(2), top[:, :, 1:2], top[:, :, 0:1], ALU.subtract).then_inc(f_v, 1)
                for t in range(TC):
                    last = dve.max_index(topi[:, t, :], top[:, t, :], lg[:, t, :])
                last.then_inc(f_v, 1)
                after(4)
                dve.tensor_copy(topf[:], topi[:, :, 0:2]).then_inc(f_v, 1)
                dve.wait_ge(f_p2, c + 1)
                dve.tensor_scalar(p2d[:], p2e[:], 1.0, None, ALU.add).then_inc(f_v, 1)
                after(6)
                dve.reciprocal(pr[:, :, 0:1].rearrange("p t a -> p (t a)"), p2d[:]).then_inc(f_v, 1)
                after(7)
                dve.tensor_tensor(pr[:, :, 1:2].rearrange("p t a -> p (t a)"), p2e[:],
                                  pr[:, :, 0:1].rearrange("p t a -> p (t a)"), ALU.mult).then_inc(f_v, 1)
                after(8)
                for oh, a in ((oh1, 0), (oh2, 1)):
                    dve.tensor_tensor(oh[:], eidx[:].unsqueeze(1).to_broadcast([128, TC, E]),
                                      topf[:, :, a:a + 1].to_broadcast([128, TC, E]), ALU.is_equal).then_inc(f_v, 1)
                after(10)
                for oh, a in ((oh1, 0), (oh2, 1)):
                    dve.tensor_tensor(oh[:], oh[:], pr[:, :, a:a + 1].to_broadcast([128, TC, E]), ALU.mult).then_inc(f_v, 1)
                after(12)
                dve.tensor_tensor(wt[:], oh1[:], oh2[:], ALU.add).then_inc(f_v, 1)
                after(13)
                for e in range(E):
                    for t in range(TC):
                        if t % 2 == 0:
                            dve.wait_ge(f_y, c * (2 * E) + (2 * e + t // 2 + 1))
                        dve.wait_ge(f_ac, c * F_AC + (1 if e == 0 else (e - 1) * TC + t + 2))
                        dve.scalar_tensor_tensor(acc[:, t, :], (sx[0], sx[1])[t // 2][:, (t % 2) * D:(t % 2 + 1) * D],
                                                 wt[:, t, e:e + 1], acc[:, t, :], ALU.mult, ALU.add).then_inc(f_ac, 1)
                dve.wait_ge(f_ac, c * F_AC + F_AC)
                for t in range(TC):
                    dve.bn_stats(st3[:, t, :], acc[:, t, :]).then_inc(f_ln, 1)
                dve.wait_ge(f_ln, c * F_LN + TC)
                dve.tensor_copy(carry[:], st3[:, 0, 0:1])
                for t in range(TC):
                    dve.bn_aggr(mv3[:, t, :], st3[:, t, :]).then_inc(f_ln, 1)
                dve.wait_ge(f_gl, c * 2 + 2)
                for t in range(TC):
                    dve.tensor_scalar(acc[:, t, :], acc[:, t, :], mv3[:, t, 0:1], rs3[:, t:t + 1],
                                      ALU.subtract, ALU.mult).then_inc(f_ln, 1)

            chunk(0)
            with dve.Fori(1, NCH) as c:
                chunk(c)

        @block.gpsimd
        def _(gp):
            gp.wait_ge(c_ok, N_CONST)

            def power(dst, var, tmp, eps, s, i, per=2):
                gp.tensor_tensor(tmp, var, eps.to_broadcast(list(tmp.shape)), ALU.add).then_inc(s, 1)
                gp.wait_ge(s, i * per + 1)
                gp.tensor_tensor(dst, tmp, mhalf[:, 0:1].to_broadcast(list(tmp.shape)), ALU.pow).then_inc(s, 1)

            def mla_rstd(i):
                have(gp, a_sq, i, 2, 2)
                freed(gp, v_qk, i, 5, 5)
                power(rstd[:], ms[:], mse[:], rms_eps[:], g_rs, i)

            def mla_rest(i):
                have(gp, v_qk, i, 5, 3)
                freed(gp, p_aT, i, 1, 1)
                gp.tensor_tensor(kv[:, 0:64], kc[:], ks[:], ALU.add).then_inc(g_qk, 1)
                gp.tensor_copy(qn[:, 128:192].bitcast(F32R), qraw[:]).then_inc(g_qk, 1)
                have(gp, g_qk, i, 3, 2)
                gp.tensor_tensor(qn[:, 192:256], qraw[:], qn[:, 128:192], ALU.subtract).then_inc(g_qk, 1)

            def mla_rotate(i, n):
                have(gp, a_q, i, NCA, n + 1)
                gp.tensor_tensor(rcos[:], Qs[:, :, 0:DR], cosine[:].unsqueeze(1).to_broadcast([128, HC, DR]), ALU.mult)\
                  .then_inc(g_rp, 1)
                have(gp, g_rp, i, 2 * NCA, 2 * n + 1)
                have(gp, v_rp, i, NCA, n + 1)
                gp.tensor_tensor(Qs[:, :, 0:DR], rcos[:], rsin[:], ALU.add).then_inc(g_rp, 1)

            def mla_norm(i):
                have(gp, v_l1, i, 3, 3)
                freed(gp, v_x1, i, 1, 1)
                power(rs1[:], mv1[:, 1:2], ve1[:], ln_eps[:], g_l1, i)

            def xat_keep(i):
                have(gp, v_x1, i, 1, 1)
                freed(gp, w_l2, i, 3, 1)
                gp.tensor_tensor(x1b[:], x1[:], bo[:], ALU.add).then_inc(g_x1, 1)

            def xat_arrange_lo(i):
                have(gp, w_qkv, i, 1, 1)
                freed(gp, q_pv, i, NCX, NCX)
                have(gp, b_ar, i, 2, 2)
                gp.tensor_tensor(karr[:, :, :, 1, :],
                                 qkv[:, 256:320].rearrange("p (n c) -> p n c", n=2).unsqueeze(2).to_broadcast([128, 2, 2, SLOT]),
                                 karr[:, :, :, 0, :], ALU.subtract).then_inc(g_ar, 1)
                gp.tensor_copy(vx[:, :, 0:HD], qkv[:, 320:384].rearrange("p (g d) -> p g d", g=G)).then_inc(g_ar, 1)
                gp.tensor_tensor(qarr[:, :, 2:4, :],
                                 qkv[:, 0:256].rearrange("p (n c) -> p n c", n=NCX).unsqueeze(2).to_broadcast([128, NCX, 2, SLOT]),
                                 qarr[:, :, 0:2, :], ALU.subtract).then_inc(g_ar, 1)

            def xat_norm(i):
                have(gp, w_l2, i, 3, 3)
                freed(gp, w_x2, i, 1, 1)
                power(rs2[:], mv2[:, 1:2], ve2[:], ln_eps[:], g_l2, i)

            def step(i, x):
                ma, xa = i is not None, x is not None
                if xa: xat_keep(x)
                if xa: xat_arrange_lo(x)
                if ma: mla_rstd(i)
                if ma: mla_rest(i)
                if ma:
                    for n in range(NCA):
                        mla_rotate(i, n)
                if xa: xat_norm(x)
                if ma: mla_norm(i)

            step(0, None)
            gp.wait_ge(wf_ld, 32)
            gp.tensor_copy(wfch[:], wfc).then_inc(wf_ok, 1)
            gp.wait_ge(wf_ok, 1)
            gp.tensor_tensor(wfcl[:], wfc, f32(wfch[:]), ALU.subtract).then_inc(wf_ok, 1)
            step(1, 0)
            with gp.Fori(2, B) as j:
                step(j, j - 1)
            step(None, B - 1)

            def chunk(c):
                for e in range(E):
                    for m in range(2):
                        gp.wait_ge(f_r, c * (2 * E) + (2 * e + m + 1))
                        earlier(gp, f_y, c, 2 * E, 2 * (e - 1))
                        gp.tensor_tensor(h2[:, e % 2, m, :], hr[:, m, :], hr[:, m, :], ALU.mult).then_inc(f_sq, 1)
                gp.wait_ge(f_ln, c * F_LN + 2 * TC)
                power(rs3[:], mv3[:, :, 1:2].rearrange("p t a -> p (t a)"), ve3[:], ln_eps[:], f_gl, c)

            chunk(0)
            with gp.Fori(1, NCH) as c:
                chunk(c)


def kernel(**inputs):
    import concourse.bacc as bacc
    from concourse.bass_utils import run_bass_kernel_spmd

    a = {k: np.asarray(v) for k, v in inputs.items()}
    x, ctx = a["x"], a["ctx_2048"]
    wq_b = a["L0_attn_wq_b"].reshape(QL, H, DN + DR)
    wkv_b = a["L0_attn_wkv_b"].reshape(KL, H, DN + DV)
    rest = slice(128, QL)
    nopeT = wq_b[:, :, :DN].transpose(2, 1, 0)
    qln = a["L0_attn_q_a_ln_w"]

    def group_order(w, axis):
        w = np.moveaxis(w, axis, -1)
        lead = w.shape[:-1]
        w = w.reshape(*lead, 2, HALF, HC, HD).swapaxes(-3, -2).reshape(*lead, XH * HD)
        return np.moveaxis(w, -1, axis)

    def tokens_last(v):
        return v.reshape(B * S, KT_D, 128).transpose(2, 1, 0)

    inv = 1.0 / np.float32(10000.0) ** (np.arange(0, DR, 2, dtype=np.float32) / np.float32(DR))
    angle = np.outer(np.arange(S, dtype=np.float32), inv.astype(np.float32)).astype(np.float32)
    cos, sin = np.cos(angle), np.sin(angle)
    row = np.arange(128)
    arrays = {
        "x": x, "xT": tokens_last(x), "ctxT": tokens_last(ctx),
        "ssmask": a["mask_SxS2_bc0"], "padmask": a["mask_BxS2_bk0"],
        "wa": np.concatenate([a["L0_attn_wq_a"], a["L0_attn_wkv_a"]], axis=1),
        "wqnT": np.concatenate([nopeT, nopeT[:, :, rest]], axis=2),
        "wkvT": np.stack([wkv_b[:, :, :DN].transpose(2, 1, 0), wkv_b[:, :, DN:].transpose(2, 1, 0)], axis=1),
        "wpe": np.stack([wq_b[:128, :, DN:], np.concatenate([wq_b[rest, :, DN:]] * 2)], axis=1),
        "wo": a["L0_attn_wo"],
        "qln": np.stack([qln[:128], np.concatenate([qln[rest]] * 2)], axis=1),
        "kvln": a["L0_attn_kv_a_ln_w"],
        "xw": np.concatenate([group_order(a["L0_xattn_Wq"], 0).T, a["L0_xattn_Wk"].T, a["L0_xattn_Wv"].T,
                              group_order(a["L0_xattn_Wo"], 1).T], axis=1),
        "bqkv": np.concatenate([group_order(a["L0_xattn_bq"], 0), a["L0_xattn_bk"], a["L0_xattn_bv"]]),
        "bo": a["L0_xattn_bo"],
        "wr": a["L0_ffn_w_router"], 
        "wfc": a["L0_ffn_w_fc"].reshape(E, KT_D, 128, D).transpose(2, 1, 0, 3),
        "wpj": a["L0_ffn_w_proj"].reshape(E, KT_D, 128, D).transpose(2, 0, 1, 3),
        "c_ident": np.eye(128, dtype=np.float32),
        "c_causal": np.where(row[None, :] > row[:, None], np.float32(-BIG), np.float32(0)),
        "c_cos": np.concatenate([cos, cos], axis=1), "c_sin": np.concatenate([-sin, sin], axis=1),
        "c_groupsel": (row[:, None] % SLOT // HD == np.arange(HALF)).astype(np.float32),
        "c_eidx": np.tile(np.arange(E, dtype=np.float32), (128, 1)),
    }
    arrays = {k: np.ascontiguousarray(v) for k, v in arrays.items()}
    nc = bacc.Bacc("TRN2", target_bir_lowering=False, num_devices=1)
    io = {k: nc.dram_tensor(f"in_{k}", v.shape, mybir.dt.from_np(v.dtype), kind="ExternalInput").ap()
          for k, v in arrays.items()}
    io["out"] = nc.dram_tensor("out_x", (B, S, D), F32, kind="ExternalOutput").ap()
    decoder_layer(nc, io)
    r = run_bass_kernel_spmd(nc, [{f"in_{k}": v for k, v in arrays.items()}], core_ids=[0])
    return r.results[0]["out_x"]
```

```python
from contextlib import ExitStack

import numpy as np

import concourse.bass as bass
from concourse import mybir

F32 = mybir.dt.float32
F32R = mybir.dt.float32r
BF16 = mybir.dt.bfloat16
U8 = mybir.dt.uint8
U32 = mybir.dt.uint32
ALU = mybir.AluOpType
ACT = mybir.ActivationFunctionType
AX = mybir.AxisListType

B, S, D = 16, 128, 256
KT_D = D // 128
H, QL, KL, DR, DN, DV = 16, 192, 64, 64, 128, 128
QB = QL - 128
HC = 4
NCA = H // HC
XH, G, HD = 32, 8, 8
NCX = XH // HC
HALF = G // 2
SLOT = HALF * HD
E, TOPK = 8, 2
TC = 4
NCH = B // TC
BIG = 1e30
MLA_SCALE = float((DN + DR) ** -0.5)
XAT_SCALE = float(HD ** -0.5)
RMS_EPS, LN_EPS = 1e-6, 1e-5


def decoder_layer(nc, io):
    with ExitStack() as ctx:
        def sb(name, shape, dt=F32):
            return ctx.enter_context(nc.sbuf_tensor(name, shape, dt))

        def ps(name):
            return ctx.enter_context(nc.psum_tensor(name, [128, 512], F32))

        def sem(name):
            return ctx.enter_context(nc.semaphore(name))

        def f32(t):
            return t.bitcast(F32)

        x2_hbm = nc.dram_tensor("x2_hbm", (B, S, D), F32).ap()

        ident = sb("ident", [128, 128])
        identb = sb("identb", [128, 128], BF16)
        causal = sb("causal", [128, 128])
        causalb = sb("causalb", [128, 128], BF16)
        cosine = sb("cosine", [128, DR])
        sine = sb("sine", [128, DR])
        groupsel = sb("groupsel", [128, HALF])
        eidx = sb("eidx", [128, E])
        mhalf = sb("mhalf", [128, 1])
        zero = sb("zero", [128, 1])
        rms_eps = sb("rms_eps", [128, 1])
        ln_eps = sb("ln_eps", [128, 1])
        carry = sb("carry", [128, 1])
        wah = sb("wah", [128, KT_D, 320], F32R)
        wal = sb("wal", [128, KT_D, 320], F32R)
        with nc.sbuf_tensor("stage1", [128, 4096], F32) as stage1:
            pass
        wfcl = sb("wfcl", [128, KT_D, E, D], F32R)
        stage2 = sb("stage2", [128, 4096])
        wqnT = stage1[:].rearrange("p (h a) -> p h a", h=H)
        wo_s = stage2[:].rearrange("p (h c) -> p h c", h=H)
        qln = sb("qln", [128, 2])
        kvln = sb("kvln", [128, KL])
        WQh = sb("WQh", [128, 2, H, 128], F32R)
        WQl = sb("WQl", [128, 2, H, 128], F32R)
        VO = sb("VO", [128, H // 2, D])
        xwh = sb("xwh", [128, KT_D, 640], F32R)
        xwl = sb("xwl", [128, KT_D, 640], F32R)
        bqkv = sb("bqkv", [128, 384])
        bo = sb("bo", [128, D])
        ssmask8 = sb("ssmask8", [128, 128], U8)
        ssmask = sb("ssmask", [128, 128], BF16)
        wr = sb("wr", [128, KT_D, E])
        wfch = sb("wfch", [128, KT_D, E, D], F32R)
        wfc = stage1[:].rearrange("p (k e d) -> p k e d", k=KT_D, e=E)
        wpj = stage2[:].rearrange("p (e k c) -> p e k c", e=E, k=KT_D)
        xT = sb("xT", [128, KT_D, 128])
        xTh = sb("xTh", [128, KT_D, 128], F32R)
        xTl = sb("xTl", [128, KT_D, 128], F32R)
        x_res = sb("x_res", [128, D])
        sqj = sb("sqj", [128, QL])
        ms = sb("ms", [128, 2])
        mse = sb("mse", [128, 2])
        rstd = sb("rstd", [128, 2])
        qn = sb("qn", [128, 256])
        qraw = sb("qraw", [128, QB])
        kvn = sb("kvn", [128, 128])
        kv = sb("kv", [128, KL + 1])
        kc = sb("kc", [128, DR])
        ks = sb("ks", [128, DR])
        qAh = sb("qAh", [128, 128], F32R)
        qAl = sb("qAl", [128, 128], F32R)
        qBs = sb("qBs", [128, 128], F32R)
        KT = sb("KT", [128, 128])
        Qs = sb("Qs", [128, HC, 128])
        rsin = sb("rsin", [128, HC, DR])
        rcos = sb("rcos", [128, HC, DR])
        QT = sb("QT", [128, HC * 128])
        mxa = sb("mxa", [128, HC])
        Pa = sb("Pa", [128, 2, 512])
        PTa = sb("PTa", [128, 2, 512])
        rec = sb("rec", [128, HC])
        Oa = sb("Oa", [128, HC, KL])
        OTa = sb("OTa", [128, H // 2, 128])
        r1 = sb("r1", [128, D])
        st1 = sb("st1", [128, 6])
        mv1 = sb("mv1", [128, 2])
        ve1 = sb("ve1", [128, 1])
        rs1 = sb("rs1", [128, 1])
        x1 = sb("x1", [128, D])
        ctxT = sb("ctxT", [128, KT_D, 128])
        xch = sb("xch", [128, 4, 128], F32R)
        xcl = sb("xcl", [128, 4, 128], F32R)
        x1b = sb("x1b", [128, D])
        x1k = sb("x1k", [128, D])
        qkv = sb("qkv", [128, 384])
        qarr = sb("qarr", [128, NCX, 4, SLOT])
        karr = sb("karr", [128, 2, 2, 2, SLOT])
        vx = sb("vx", [128, G, HD + 1])
        QX = sb("QX", [128, NCX, 128], F32R)
        KX = sb("KX", [128, 2, HALF, 128], F32R)
        pad8 = sb("pad8", [128, 128], U8)
        comb = sb("comb", [128, 128], BF16)
        mxx = sb("mxx", [128, NCX, HC])
        Px = sb("Px", [128, 2, 512])
        PTx = sb("PTx", [128, 2, 512])
        den = sb("den", [128, XH])
        recx = sb("recx", [128, XH])
        Ox = sb("Ox", [128, XH, HD])
        OTxh = sb("OTxh", [128, KT_D, 128], F32R)
        OTxl = sb("OTxl", [128, KT_D, 128], F32R)
        r2 = sb("r2", [128, D])
        st2 = sb("st2", [128, 6])
        mv2 = sb("mv2", [128, 2])
        ve2 = sb("ve2", [128, 1])
        rs2 = sb("rs2", [128, 1])
        x2 = sb("x2", [128, D])
        setup_only = ExitStack()

        def loaded(name, shape, dt=F32):
            return setup_only.enter_context(nc.sbuf_tensor(name, shape, dt))

        stage3 = loaded("stage3", [128, 4096])
        wkT = stage3[:, 0:1024].rearrange("p (h c) -> p h c", h=H)
        wvT = stage3[:, 1024:2048].rearrange("p (h c) -> p h c", h=H)
        wpe = stage3[:, 2048:4096].rearrange("p (k h c) -> p k h c", k=2, h=H)
        wa = loaded("wa", [128, KT_D, 320])
        xw = loaded("xw", [128, KT_D, 640])
        setup_only.close()
        x2c = sb("x2c", [128, TC, D])
        x2T = sb("x2T", [128, KT_D, TC * 128])
        x2Th = sb("x2Th", [128, KT_D, TC * 128], F32R)
        x2Tl = sb("x2Tl", [128, KT_D, TC * 128], F32R)
        lg = sb("lg", [128, TC, E])
        top = sb("top", [128, TC, E])
        topi = sb("topi", [128, TC, E], U32)
        topf = sb("topf", [128, TC, 2])
        dd = sb("dd", [128, TC])
        p2e = sb("p2e", [128, TC])
        p2d = sb("p2d", [128, TC])
        pr = sb("pr", [128, TC, 2])
        oh1 = sb("oh1", [128, TC, E])
        oh2 = sb("oh2", [128, TC, E])
        wt = sb("wt", [128, TC, E])
        hr = sb("hr", [128, 2, 512])
        h2 = sb("h2", [128, 2, KT_D, 512])
        acc = sb("acc", [128, TC, D])
        st3 = sb("st3", [128, TC, 6])
        mv3 = sb("mv3", [128, TC, 2])
        ve3 = sb("ve3", [128, TC])
        rs3 = sb("rs3", [128, TC])

        qb, ob = ps("qb"), ps("ob")
        sa = [ps("sa0"), ps("sa1")]
        mb, xo = ps("mb"), ps("xo")
        sx = [ps("sx0"), ps("sx1")]

        d_ld = sem("d_ld")
        c_ok = sem("c_ok")
        c_lo = sem("c_lo")
        s_p = sem("s_p")
        s_hi = sem("s_hi")
        s_lo = sem("s_lo")
        wf_ld = sem("wf_ld")
        wf_ok = sem("wf_ok")
        d_x = sem("d_x")
        d_xr = sem("d_xr")
        d_c = sem("d_c")
        d_p = sem("d_p")
        d_x2 = sem("d_x2")
        a_xs = sem("a_xs")
        p_a = sem("p_a")
        a_sq = sem("a_sq")
        g_rs = sem("g_rs")
        v_qk = sem("v_qk")
        g_qk = sem("g_qk")
        g_kv = sem("g_kv")
        p_aT = sem("p_aT")
        a_aT = sem("a_aT")
        v_aT = sem("v_aT")
        p_q = sem("p_q")
        a_q = sem("a_q")
        v_rp = sem("v_rp")
        g_rp = sem("g_rp")
        p_qT = sem("p_qT")
        v_qT = sem("v_qT")
        p_s = sem("p_s")
        v_mx = sem("v_mx")
        v_sub = sem("v_sub")
        a_ex = sem("a_ex")
        p_pT = sem("p_pT")
        a_pT = sem("a_pT")
        p_pv = sem("p_pv")
        v_rc = sem("v_rc")
        v_o = sem("v_o")
        p_oT = sem("p_oT")
        a_oT = sem("a_oT")
        p_y = sem("p_y")
        v_l1 = sem("v_l1")
        g_l1 = sem("g_l1")
        v_x1 = sem("v_x1")
        q_xT = sem("q_xT")
        b_xs = sem("b_xs")
        w_xs = sem("w_xs")
        g_x1 = sem("g_x1")
        g_xb = sem("g_xb")
        q_qkv = sem("q_qkv")
        w_qkv = sem("w_qkv")
        b_ar = sem("b_ar")
        g_ar = sem("g_ar")
        g_vx = sem("g_vx")
        q_kT = sem("q_kT")
        w_kx = sem("w_kx")
        q_qx = sem("q_qx")
        b_qx = sem("b_qx")
        w_cm = sem("w_cm")
        q_s = sem("q_s")
        w_mx = sem("w_mx")
        w_sub = sem("w_sub")
        b_ex = sem("b_ex")
        q_pT = sem("q_pT")
        b_pT = sem("b_pT")
        q_pv = sem("q_pv")
        w_o = sem("w_o")
        q_oT = sem("q_oT")
        b_oT = sem("b_oT")
        w_oT = sem("w_oT")
        q_y = sem("q_y")
        w_l2 = sem("w_l2")
        g_l2 = sem("g_l2")
        w_x2 = sem("w_x2")
        f_ld = sem("f_ld")
        f_T = sem("f_T")
        f_hi = sem("f_hi")
        f_lo = sem("f_lo")
        f_lg = sem("f_lg")
        f_v = sem("f_v")
        f_p2 = sem("f_p2")
        f_h = sem("f_h")
        f_r = sem("f_r")
        f_sq = sem("f_sq")
        f_y = sem("f_y")
        f_ac = sem("f_ac")
        f_ln = sem("f_ln")
        f_gl = sem("f_gl")
        f_st = sem("f_st")

        def there(i):
            return not isinstance(i, int) or 0 <= i < B

        def have(eng, s, i, per, k):
            if there(i):
                eng.wait_ge(s, i * per + k)

        def freed(eng, s, i, per, k):
            have(eng, s, i - 1, per, k)

        def mla_chunk(j, c):
            return j + c // NCA, c % NCA

        def xat_chunk(x, c):
            return x + c // NCX, c % NCX

        def pipeline(eng, step):
            for j in range(-1, LOOP_FROM):
                step(j)
            with eng.Fori(LOOP_FROM, B - 2) as j:
                step(j)
            for j in range(B - 2, B + 3):
                step(j)

        def earlier(eng, s, c, per, k):
            if not isinstance(c, int) or (c == 0 and k > 0):
                eng.wait_ge(s, c * per + k)

        LOOP_FROM = 4
        N_CONST, N_LO = 14, 4
        F_V, F_LN, F_AC = 13, 3 * TC, 1 + TC * E
        n_setup = 18
        SETUP = 16 * n_setup

        block = ctx.enter_context(nc.Block())

        @block.sync
        def _(sp):
            def bc(ap, n):
                return ap.partition_broadcast(128)
            loads = [
                (ident[:], io["c_ident"]), (causal[:], io["c_causal"]), (cosine[:], io["c_cos"]),
                (wa[:], io["wa"].rearrange("(k p) n -> p k n", p=128)),
                (qln[:], io["qln"]), (kvln[:], bc(io["kvln"], KL)),
                (sine[:], io["c_sin"]), (groupsel[:], io["c_groupsel"]), (eidx[:], io["c_eidx"]),
                (wqnT, io["wqnT"]), (stage3[:, 0:2048].rearrange("p (k h c) -> p k h c", k=2, h=H), io["wkvT"]),
                (wpe, io["wpe"]), (wo_s, io["wo"].rearrange("(h p) c -> p h c", p=128)),
                (xw[:], io["xw"].rearrange("(k p) n -> p k n", p=128)),
                (bqkv[:], bc(io["bqkv"], 384)), (bo[:], bc(io["bo"], D)),
                (ssmask8[:], io["ssmask"]), (wr[:], io["wr"].rearrange("(k p) n -> p k n", p=128)),
            ]
            assert len(loads) == n_setup
            for dst, src in loads:
                sp.dma_start(dst, src).then_inc(d_ld, 16)

            def load_xT(i):
                freed(sp, a_xs, i, 2, 2)
                sp.dma_start(xT[:], io["xT"][:, :, bass.ds(i * S, S)]).then_inc(d_x, 16)

            def load_x_res(i):
                freed(sp, v_l1, i, 3, 1)
                sp.dma_start(x_res[:], io["x"][i]).then_inc(d_xr, 16)

            def load_ctx(i):
                freed(sp, b_xs, i, 2, 1)
                freed(sp, w_xs, i, 2, 1)
                sp.dma_start(ctxT[:], io["ctxT"][:, :, bass.ds(i * S, S)]).then_inc(d_c, 16)

            def load_pad(i):
                freed(sp, w_cm, i, 1, 1)
                sp.dma_start(pad8[:], io["padmask"][i].partition_broadcast(128)).then_inc(d_p, 16)

            def store_x2(i):
                have(sp, w_x2, i, 1, 1)
                sp.dma_start(x2_hbm[i], x2[:]).then_inc(d_x2, 16)

            def step(j):
                if there(j + 2): load_xT(j + 2)
                if there(j): load_x_res(j)
                if there(j - 3): store_x2(j - 3)
                if there(j): load_ctx(j)
                if there(j): load_pad(j)
                if isinstance(j, int) and j == -1:
                    sp.wait_ge(s_p, 2 * NCA)
                    sp.dma_start(wfc, io["wfc"]).then_inc(wf_ld, 16)
                    sp.dma_start(wpj, io["wpj"]).then_inc(wf_ld, 16)

            load_xT(0)
            pipeline(sp, step)
            sp.wait_ge(d_x2, 16 * B)

            def load_chunk(c):
                sp.dma_start(x2c[:], x2_hbm[bass.ds(c * TC, TC)].rearrange("t p d -> p t d")).then_inc(f_ld, 16)

            def store_chunk(c):
                sp.wait_ge(f_ln, c * F_LN + F_LN)
                sp.dma_start(io["out"][bass.ds(c * TC, TC)].rearrange("t p d -> p t d"), acc[:]).then_inc(f_st, 16)

            load_chunk(0)
            with sp.Fori(1, NCH) as c:
                sp.wait_ge(f_ac, c * F_AC + (1 - F_AC))
                load_chunk(c)
                store_chunk(c - 1)
            store_chunk(NCH - 1)
            sp.wait_ge(f_st, 16 * NCH)

        @block.tensor
        def _(pe):
            pe.wait_ge(c_ok, N_CONST)
            for n in range(NCA):
                if n >= 2:
                    pe.wait_ge(s_lo, 2 * (n - 2) + 2)
                bank = sa[n % 2]
                for j in range(HC):
                    h = HC * n + j
                    pe.matmul(bank[:, j * KL:(j + 1) * KL], wqnT[:, h, 0:128], wkT[:, h, :], start=True, stop=True)
                    last = pe.matmul(bank[:, 256 + j * KL:256 + (j + 1) * KL], wqnT[:, h, 128:256], wkT[:, h, :],
                                     start=True, stop=True)
                last.then_inc(s_p, 1)
                if n >= 2:
                    pe.wait_ge(s_hi, 3 * (n - 2) + 3)
                bank = sx[n % 2]
                for j in range(HC):
                    h = HC * n + j
                    last = pe.matmul(bank[64 * (j % 2):64 * (j % 2) + 64, (j // 2) * D:(j // 2 + 1) * D],
                                     wvT[:, h, :], wo_s[:, h, :], start=True, stop=True)
                last.then_inc(s_p, 1)
            pe.wait_ge(s_lo, 2 * NCA)
            pe.wait_ge(s_hi, 3 * NCA)
            pe.wait_ge(c_lo, N_LO)

            def split_matmul(out, terms):
                for k, (w, m) in enumerate(terms):
                    last = pe.matmul(out, w, m, start=(k == 0), stop=(k == len(terms) - 1))
                return last

            def mla_latents(i):
                have(pe, a_xs, i, 2, 2)
                freed(pe, a_oT, i, NCA, 1)
                terms = []
                for k in range(KT_D):
                    terms += [(xTh[:, k, :], wah[:, k, :]), (xTh[:, k, :], wal[:, k, :]), (xTl[:, k, :], wah[:, k, :])]
                split_matmul(ob[:, 0:320], terms).then_inc(p_a, 1)

            def mla_latents_T(i):
                have(pe, g_qk, i, 3, 3)
                have(pe, v_qk, i, 5, 5)
                freed(pe, v_qT, i, NCA, NCA)
                pe.transpose(qb[:, 0:128], qn[:, 0:128], ident[:])
                pe.transpose(qb[:, 128:256], qn[:, 128:256], ident[:])
                pe.transpose(qb[:, 256:384], kvn[:], ident[:]).then_inc(p_aT, 1)

            def mla_query(i, n):
                if n == 0:
                    have(pe, a_aT, i, 3, 3)
                    have(pe, v_aT, i, 1, 1)
                else:
                    have(pe, v_qT, i, NCA, n)
                hs = slice(HC * n, HC * n + HC)
                split_matmul(qb[:], [(qAh[:], WQh[:, 0, hs, :]), (qAh[:], WQl[:, 0, hs, :]), (qAl[:], WQh[:, 0, hs, :]),
                                     (qBs[:], WQh[:, 1, hs, :]), (qBs[:], WQl[:, 1, hs, :])]).then_inc(p_q, 1)

            def mla_query_T(i, n):
                have(pe, g_rp, i, 2 * NCA, 2 * n + 2)
                for j in range(HC):
                    last = pe.transpose(qb[:, j * 128:(j + 1) * 128], Qs[:, j, :], ident[:])
                last.then_inc(p_qT, 1)

            def mla_scores(i, n):
                have(pe, v_qT, i, NCA, n + 1)
                if n >= 2:
                    have(pe, a_pT, i, NCA, n - 1)
                else:
                    freed(pe, a_pT, i, NCA, n + 3)
                bank = sa[n % 2]
                for j in range(HC):
                    pe.matmul(bank[:, j * 128:(j + 1) * 128], QT[:, j * 128:(j + 1) * 128], KT[:],
                              start=(j == 0), stop=False, skip_group_check=True)
                pe.matmul(bank[:], identb[:], causalb[:].unsqueeze(1).to_broadcast([128, HC, 128]),
                          start=False, stop=True, skip_group_check=True).then_inc(p_s, 1)

            def mla_probs_T(i, n):
                have(pe, a_ex, i, NCA, n + 1)
                for j in range(HC):
                    last = pe.transpose(sa[n % 2][:, j * 128:(j + 1) * 128], Pa[:, n % 2, j * 128:(j + 1) * 128], ident[:])
                last.then_inc(p_pT, 1)

            def mla_values(i, n):
                have(pe, a_pT, i, NCA, n + 1)
                if n == 0:
                    have(pe, g_kv, i, 1, 1)
                    freed(pe, v_l1, i, 3, 1)
                elif n == 1:
                    have(pe, a_oT, i, NCA, n)
                    have(pe, v_qk, i + 1, 5, 5)
                else:
                    have(pe, a_oT, i, NCA, n)
                for j in range(HC):
                    last = pe.matmul(ob[:, j * 65:(j + 1) * 65], PTa[:, n % 2, j * 128:(j + 1) * 128], kv[:],
                                     start=True, stop=True)
                last.then_inc(p_pv, 1)

            def mla_out_T(i, n):
                have(pe, v_o, i, NCA, n + 1)
                for k in range(2):
                    last = pe.transpose(ob[:, k * 128:(k + 1) * 128],
                                        Oa[:, 2 * k:2 * k + 2, :].rearrange("p h c -> p (h c)"), ident[:])
                last.then_inc(p_oT, 1)

            def mla_project(i):
                have(pe, a_oT, i, NCA, NCA)
                split_matmul(ob[:, 0:D], [(OTa[:, k, :], VO[:, k, :]) for k in range(H // 2)]).then_inc(p_y, 1)

            def xat_x_T(i):
                have(pe, v_x1, i, 1, 1)
                have(pe, w_l2, i - 2, 3, 1)
                for k in range(KT_D):
                    last = pe.transpose(mb[:, k * 128:(k + 1) * 128], x1[:, k * 128:(k + 1) * 128], ident[:])
                last.then_inc(q_xT, 1)

            def xat_qkv(i):
                have(pe, b_xs, i, 2, 2)
                have(pe, w_xs, i, 2, 2)
                for lo, hi, t0 in ((0, 256, 0), (256, 384, 2)):
                    terms = []
                    for k in range(KT_D):
                        terms += [(xch[:, t0 + k, :], xwh[:, k, lo:hi]), (xch[:, t0 + k, :], xwl[:, k, lo:hi]),
                                  (xcl[:, t0 + k, :], xwh[:, k, lo:hi])]
                    last = split_matmul(mb[:, lo:hi], terms)
                last.then_inc(q_qkv, 1)

            def xat_keys_T(i):
                have(pe, b_ar, i, 2, 2)
                have(pe, g_ar, i, 2, 1)
                for k in range(2):
                    last = pe.transpose(mb[:, k * 128:(k + 1) * 128],
                                        karr[:, k].rearrange("p a b c -> p (a b c)"), ident[:])
                last.then_inc(q_kT, 1)

            def xat_queries_T(i, half):
                have(pe, g_ar, i, 2, 2)
                if half == 0:
                    have(pe, w_kx, i, 2, 2)
                else:
                    have(pe, b_qx, i, 2, 1)
                for r in range(HC):
                    last = pe.transpose(mb[:, r * 128:(r + 1) * 128],
                                        qarr[:, half * HC + r].rearrange("p a b -> p (a b)"), ident[:])
                last.then_inc(q_qx, 1)

            def xat_scores(i, n):
                if n == 0:
                    have(pe, w_kx, i, 2, 2)
                    have(pe, w_cm, i, 1, 1)
                if n % HC == 0:
                    have(pe, b_qx, i, 2, n // HC + 1)
                if n < 2:
                    freed(pe, b_pT, i, NCX, n + NCX - 1)
                else:
                    have(pe, b_pT, i, NCX, n - 1)
                bank = sx[n % 2]
                pe.matmul(bank[:], identb[:], comb[:].unsqueeze(1).to_broadcast([128, HC, 128]), start=True, stop=False)
                pe.matmul(bank[:], QX[:, n, :], KX[:, n // HC].rearrange("p g s -> p (g s)"), start=False, stop=True)\
                  .then_inc(q_s, 1)

            def xat_probs_T(i, n):
                have(pe, b_ex, i, NCX, n + 1)
                for j in range(HC):
                    last = pe.transpose(sx[n % 2][:, j * 128:(j + 1) * 128], Px[:, n % 2, j * 128:(j + 1) * 128], ident[:])
                last.then_inc(q_pT, 1)

            def xat_values(i, n):
                have(pe, b_pT, i, NCX, n + 1)
                if n == 0:
                    have(pe, g_vx, i, 1, 1)
                    freed(pe, w_o, i, 3, 3)
                for j in range(HC):
                    c = (n * HC + j) * (HD + 1)
                    last = pe.matmul(xo[:, c:c + HD + 1], PTx[:, n % 2, j * 128:(j + 1) * 128],
                                     vx[:, (n // HC) * HALF + j, :], start=True, stop=True)
                last.then_inc(q_pv, 1)

            def xat_out_T(i):
                have(pe, w_o, i, 3, 3)
                have(pe, b_qx, i + 1, 2, 2)
                for k in range(KT_D):
                    last = pe.transpose(mb[:, k * 128:(k + 1) * 128],
                                        Ox[:, k * 16:(k + 1) * 16, :].rearrange("p h c -> p (h c)"), ident[:])
                last.then_inc(q_oT, 1)

            def xat_project(i):
                have(pe, b_oT, i, 1, 1)
                have(pe, w_oT, i, 1, 1)
                terms = []
                for k in range(KT_D):
                    terms += [(OTxh[:, k, :], xwh[:, k, 384:640]), (OTxh[:, k, :], xwl[:, k, 384:640]),
                              (OTxl[:, k, :], xwh[:, k, 384:640])]
                split_matmul(mb[:, 0:D], terms).then_inc(q_y, 1)

            def piece(x, c):
                if there(xat_chunk(x, c + 2)[0]): xat_scores(*xat_chunk(x, c + 2))
                if there(xat_chunk(x, c + 1)[0]): xat_probs_T(*xat_chunk(x, c + 1))
                if there(x): xat_values(x, c)

            def step(j):
                for n in range(NCA):
                    if n == 0 and there(j - 1): mla_project(j - 1)
                    if there(mla_chunk(j, n + 1)[0]): mla_scores(*mla_chunk(j, n + 1))
                    if n == 2 and there(j + 1): mla_latents_T(j + 1)
                    piece(j - 2, 2 * n)
                    if n == 0 and there(j - 3): xat_out_T(j - 3)
                    if n == 1 and there(j - 1): xat_x_T(j - 1)
                    if n == 3 and there(j - 1): xat_queries_T(j - 1, 1)
                    if there(mla_chunk(j, n + 2)[0]): mla_query(*mla_chunk(j, n + 2))
                    if n == 2 and there(j - 1): xat_keys_T(j - 1)
                    if there(j): mla_values(j, n)
                    piece(j - 2, 2 * n + 1)
                    if n == 0 and there(j - 3): xat_project(j - 3)
                    if n == 1 and there(j - 1): xat_qkv(j - 1)
                    if there(j): mla_out_T(j, n)
                    if there(mla_chunk(j, n + 2)[0]): mla_query_T(*mla_chunk(j, n + 2))
                    if n == 0 and there(j + 1): mla_latents(j + 1)
                    if n == 2 and there(j - 1): xat_queries_T(j - 1, 0)
                    if there(mla_chunk(j, n + 1)[0]): mla_probs_T(*mla_chunk(j, n + 1))

            pipeline(pe, step)

            pe.wait_ge(wf_ok, 2)
            hb, yb = [sa[0], sa[1]], [sx[0], sx[1]]

            def chunk(c):
                pe.wait_ge(f_ld, c * 16 + 16)
                for k in range(KT_D):
                    bank = (qb, mb)[k]
                    for t in range(TC):
                        last = pe.transpose(bank[:, t * 128:(t + 1) * 128], x2c[:, t, k * 128:(k + 1) * 128], ident[:])
                    last.then_inc(f_T, 1)
                pe.wait_ge(f_lo, c * KT_D + KT_D)
                for t in range(TC):
                    split_matmul(ob[:, t * E:(t + 1) * E],
                                 [(x2T[:, k, t * 128:(t + 1) * 128], wr[:, k, :]) for k in range(KT_D)])\
                        .then_inc(f_lg, 1)
                def hidden(e):
                    for m in range(2):
                        earlier(pe, f_r, c, 2 * E, 2 * (e - 1) + m + 1)
                        terms = []
                        for k in range(KT_D):
                            w = slice(m * 128, (m + 1) * 128)
                            terms += [(wfch[:, k, e, w], x2Th[:, k, :]), (wfcl[:, k, e, w], x2Th[:, k, :]),
                                      (wfch[:, k, e, w], x2Tl[:, k, :])]
                        split_matmul(hb[m][:], terms).then_inc(f_h, 1)

                def project(e):
                    pe.wait_ge(f_sq, c * (2 * E) + (2 * e + 2))
                    for q in range(2):
                        earlier(pe, f_ac, c, F_AC, (e - 1) * TC + 2 * q + 3 - (e == 0))
                        for u in range(2):
                            t = 2 * q + u
                            last = split_matmul(yb[q][:, u * D:(u + 1) * D],
                                                [(h2[:, e % 2, k, t * 128:(t + 1) * 128], wpj[:, e, k, :]) for k in range(KT_D)])
                        last.then_inc(f_y, 1)

                hidden(0)
                for e in range(E):
                    if e + 1 < E:
                        hidden(e + 1)
                    project(e)

            chunk(0)
            with pe.Fori(1, NCH) as c:
                chunk(c)

        @block.scalar
        def _(act):
            act.wait_ge(d_ld, SETUP)
            act.activation(identb[:], ident[:], ACT.Copy).then_inc(c_ok, 1)
            act.activation(causalb[:], causal[:], ACT.Copy).then_inc(c_ok, 1)
            act.activation(wah[:], wa[:], ACT.Copy).then_inc(c_ok, 1)
            act.activation(xwh[:], xw[:], ACT.Copy).then_inc(c_ok, 1)
            act.activation(ssmask[:], ssmask8[:], ACT.Copy, scale=-BIG).then_inc(c_ok, 1)
            for k in range(2):
                act.activation(WQh[:, k, :, 0:DR], wpe[:, k], ACT.Copy, scale=qln[:, k:k + 1]).then_inc(c_ok, 1)
            for n in range(NCA):
                hs = slice(HC * n, HC * n + HC)
                act.wait_ge(s_p, 2 * n + 1)
                for k in range(2):
                    act.activation(WQh[:, k, hs, DR:128],
                                   sa[n % 2][:, k * 256:(k + 1) * 256].rearrange("p (h c) -> p h c", h=HC),
                                   ACT.Copy, scale=qln[:, k:k + 1]).then_inc(s_hi, 1)
                act.wait_ge(s_p, 2 * n + 2)
                act.activation(VO[:, 2 * n:2 * n + 2, :], sx[n % 2][:].rearrange("p (k c) -> p k c", k=2), ACT.Copy)\
                   .then_inc(s_hi, 1)

            def mla_split(i):
                have(act, d_x, i, 16, 16)
                freed(act, p_a, i, 1, 1)
                act.activation(xTh[:], xT[:], ACT.Copy).then_inc(a_xs, 1)

            def mla_squares(i):
                have(act, p_a, i, 1, 1)
                freed(act, g_rs, i, 2, 2)
                act.activation(sqj[:], ob[:, 0:QL], ACT.Square, scale=float(QL ** -0.5), accum_out=ms[:, 0:1]).then_inc(a_sq, 1)
                act.wait_ge(a_sq, i * 2 + 1)
                act.activation(sqj[:, 0:KL], ob[:, QL:QL + KL], ACT.Square, scale=float(KL ** -0.5),
                               accum_out=ms[:, 1:2]).then_inc(a_sq, 1)

            def mla_latents_take(i):
                have(act, p_aT, i, 1, 1)
                act.activation(qAh[:], qb[:, 0:128], ACT.Copy).then_inc(a_aT, 1)
                act.activation(qBs[:], qb[:, 128:256], ACT.Copy).then_inc(a_aT, 1)
                act.activation(KT[:], qb[:, 256:384], ACT.Copy).then_inc(a_aT, 1)

            def mla_query_take(i, n):
                have(act, p_q, i, NCA, n + 1)
                act.activation(Qs[:].rearrange("p h c -> p (h c)"), qb[:], ACT.Copy).then_inc(a_q, 1)

            def mla_exp(i, n):
                have(act, v_sub, i, NCA, n + 1)
                act.activation(Pa[:, n % 2, :], Pa[:, n % 2, :], ACT.Exp, scale=MLA_SCALE).then_inc(a_ex, 1)

            def mla_probs_take(i, n):
                have(act, p_pT, i, NCA, n + 1)
                if n >= 2:
                    have(act, p_pv, i, NCA, n - 1)
                else:
                    freed(act, p_pv, i, NCA, n + 3)
                act.activation(PTa[:, n % 2, :], sa[n % 2][:], ACT.Copy).then_inc(a_pT, 1)

            def mla_out_take(i, n):
                have(act, p_oT, i, NCA, n + 1)
                act.activation(OTa[:, 2 * n:2 * n + 2, :].rearrange("p k t -> p (k t)"), ob[:, 0:256], ACT.Copy)\
                   .then_inc(a_oT, 1)

            def xat_split_ctx(i):
                have(act, d_c, i, 16, 16)
                freed(act, q_qkv, i, 1, 1)
                act.activation(xch[:, 2:4, :], ctxT[:], ACT.Copy).then_inc(b_xs, 1)

            def xat_split_x(i):
                have(act, q_xT, i, 1, 1)
                act.activation(xch[:, 0:2, :].rearrange("p k t -> p (k t)"), mb[:, 0:256], ACT.Copy).then_inc(b_xs, 1)

            def xat_arrange_hi(i):
                have(act, w_qkv, i, 1, 1)
                freed(act, q_qx, i, 2, 2)
                act.activation(qarr[:, :, 0:2, :].bitcast(F32R),
                               qkv[:, 0:256].rearrange("p (n c) -> p n c", n=NCX).unsqueeze(2).to_broadcast([128, NCX, 2, SLOT]),
                               ACT.Copy).then_inc(b_ar, 1)
                act.activation(karr[:, :, :, 0, :].bitcast(F32R),
                               qkv[:, 256:320].rearrange("p (n c) -> p n c", n=2).unsqueeze(2).to_broadcast([128, 2, 2, SLOT]),
                               ACT.Copy).then_inc(b_ar, 1)

            def xat_queries_take(i, half):
                have(act, q_qx, i, 2, half + 1)
                freed(act, q_s, i, NCX, (half + 1) * HC)
                act.activation(QX[:, half * HC:(half + 1) * HC, :].rearrange("p n t -> p (n t)"), mb[:], ACT.Copy)\
                   .then_inc(b_qx, 1)

            def xat_exp(i, n):
                have(act, w_sub, i, NCX, n + 1)
                act.activation(Px[:, n % 2, :], Px[:, n % 2, :], ACT.Exp, scale=XAT_SCALE).then_inc(b_ex, 1)

            def xat_probs_take(i, n):
                have(act, q_pT, i, NCX, n + 1)
                if n >= 2:
                    have(act, q_pv, i, NCX, n - 1)
                else:
                    freed(act, q_pv, i, NCX, n + NCX - 1)
                act.activation(PTx[:, n % 2, :], sx[n % 2][:], ACT.Copy).then_inc(b_pT, 1)

            def xat_out_take(i):
                have(act, q_oT, i, 1, 1)
                act.activation(OTxh[:].rearrange("p k t -> p (k t)"), mb[:, 0:256], ACT.Copy).then_inc(b_oT, 1)

            def step(j):
                for n in range(NCA):
                    if n == 2 and there(j + 1): mla_latents_take(j + 1)
                    if there(xat_chunk(j - 2, 2 * n + 1)[0]): xat_probs_take(*xat_chunk(j - 2, 2 * n + 1))
                    if there(mla_chunk(j, n + 1)[0]): mla_exp(*mla_chunk(j, n + 1))
                    if there(xat_chunk(j - 2, 2 * n + 2)[0]): xat_exp(*xat_chunk(j - 2, 2 * n + 2))
                    if n == 0 and there(j - 3): xat_out_take(j - 3)
                    if n == 1 and there(j - 1): xat_split_x(j - 1)
                    if n == 3 and there(j - 1): xat_queries_take(j - 1, 1)
                    if there(mla_chunk(j, n + 2)[0]): mla_query_take(*mla_chunk(j, n + 2))
                    if there(xat_chunk(j - 2, 2 * n + 2)[0]): xat_probs_take(*xat_chunk(j - 2, 2 * n + 2))
                    if there(xat_chunk(j - 2, 2 * n + 3)[0]): xat_exp(*xat_chunk(j - 2, 2 * n + 3))
                    if there(j): mla_out_take(j, n)
                    if n == 0 and there(j + 1): mla_squares(j + 1)
                    if n == 1 and there(j - 1): xat_arrange_hi(j - 1)
                    if n == 2 and there(j - 1): xat_queries_take(j - 1, 0)
                    if there(mla_chunk(j, n + 1)[0]): mla_probs_take(*mla_chunk(j, n + 1))
                    if n == 3 and there(j): xat_split_ctx(j)
                    if n == 3 and there(j + 2): mla_split(j + 2)

            mla_split(0)
            pipeline(act, step)

            def chunk(c):
                for k in range(KT_D):
                    act.wait_ge(f_T, c * KT_D + (k + 1))
                    act.activation(x2T[:, k, :], (qb, mb)[k][:], ACT.Copy).then_inc(f_hi, 1)
                    act.activation(x2Th[:, k, :], (qb, mb)[k][:], ACT.Copy).then_inc(f_hi, 1)
                act.wait_ge(f_v, c * F_V + 3)
                act.activation(p2e[:], dd[:], ACT.Exp).then_inc(f_p2, 1)
                for e in range(E):
                    for m in range(2):
                        act.wait_ge(f_h, c * (2 * E) + (2 * e + m + 1))
                        earlier(act, f_sq, c, 2 * E, 2 * (e - 1) + m + 1)
                        act.activation(hr[:, m, :], sa[m][:], ACT.Relu).then_inc(f_r, 1)

            chunk(0)
            with act.Fori(1, NCH) as c:
                chunk(c)

        @block.vector
        def _(dve):
            dve.memset(mhalf[:], -0.5).then_inc(c_ok, 1)
            dve.memset(zero[:], 0.0).then_inc(c_ok, 1)
            dve.memset(rms_eps[:], RMS_EPS).then_inc(c_ok, 1)
            dve.memset(ln_eps[:], LN_EPS).then_inc(c_ok, 1)
            dve.memset(kv[:, KL:KL + 1], 1.0).then_inc(c_ok, 1)
            dve.memset(vx[:, :, HD:HD + 1], 1.0).then_inc(c_ok, 1)
            dve.wait_ge(d_ld, SETUP)
            dve.tensor_tensor(stage3[:, 0:2048].rearrange("p (h c) -> p h c", c=KL),
                              stage3[:, 0:2048].rearrange("p (h c) -> p h c", c=KL),
                              kvln[:].unsqueeze(1).to_broadcast([128, 2 * H, KL]), ALU.mult).then_inc(c_ok, 1)
            dve.wait_ge(c_ok, N_CONST)
            dve.tensor_tensor(wal[:], wa[:], f32(wah[:]), ALU.subtract).then_inc(c_lo, 1)
            dve.tensor_tensor(xwl[:], xw[:], f32(xwh[:]), ALU.subtract).then_inc(c_lo, 1)
            for k in range(2):
                dve.scalar_tensor_tensor(WQl[:, k, :, 0:DR], wpe[:, k], qln[:, k:k + 1], f32(WQh[:, k, :, 0:DR]),
                                         ALU.mult, ALU.subtract).then_inc(c_lo, 1)
            for n in range(NCA):
                hs = slice(HC * n, HC * n + HC)
                for k in range(2):
                    dve.wait_ge(s_hi, 3 * n + 2)
                    dve.scalar_tensor_tensor(WQl[:, k, hs, DR:128],
                                             sa[n % 2][:, k * 256:(k + 1) * 256].rearrange("p (h c) -> p h c", h=HC),
                                             qln[:, k:k + 1], f32(WQh[:, k, hs, DR:128]), ALU.mult, ALU.subtract)\
                       .then_inc(s_lo, 1)

            def mla_split(i):
                have(dve, a_xs, i, 2, 1)
                dve.tensor_tensor(xTl[:], xT[:], f32(xTh[:]), ALU.subtract).then_inc(a_xs, 1)

            def mla_normalise(i):
                have(dve, g_rs, i, 2, 2)
                freed(dve, p_aT, i, 1, 1)
                freed(dve, g_qk, i, 3, 3)
                freed(dve, g_kv, i, 1, 1)
                dve.tensor_scalar(qraw[:], ob[:, 128:QL], rstd[:, 0:1], None, ALU.mult).then_inc(v_qk, 1)
                dve.tensor_tensor(kc[:], ob[:, 256:320], cosine[:], ALU.mult).then_inc(v_qk, 1)
                dve.tensor_tensor(ks[:].rearrange("p (a c) -> p a c", a=2),
                                  ob[:, 256:320].rearrange("p (a c) -> p a c", a=2)[:, ::-1, :],
                                  sine[:].rearrange("p (a c) -> p a c", a=2), ALU.mult).then_inc(v_qk, 1)
                dve.tensor_scalar(qn[:, 0:128], ob[:, 0:128], rstd[:, 0:1], None, ALU.mult).then_inc(v_qk, 1)
                dve.tensor_scalar(kvn[:, 64:128], ob[:, QL:QL + KL], rstd[:, 1:2], None, ALU.mult).then_inc(v_qk, 1)

            def mla_latents_lo(i):
                have(dve, a_aT, i, 3, 3)
                dve.tensor_tensor(qAl[:], qb[:, 0:128], f32(qAh[:]), ALU.subtract).then_inc(v_aT, 1)

            def mla_rotate_sine(i, n):
                have(dve, a_q, i, NCA, n + 1)
                if n > 0:
                    have(dve, g_rp, i, 2 * NCA, 2 * n)
                else:
                    freed(dve, g_rp, i, 2 * NCA, 2 * NCA)
                dve.tensor_tensor(rsin[:].rearrange("p h (a c) -> p h a c", a=2),
                                  Qs[:, :, 0:DR].rearrange("p h (a c) -> p h a c", a=2)[:, :, ::-1, :],
                                  sine[:].rearrange("p (a c) -> p a c", a=2).unsqueeze(1).to_broadcast([128, HC, 2, DR // 2]),
                                  ALU.mult).then_inc(v_rp, 1)

            def mla_query_T_take(i, n):
                have(dve, p_qT, i, NCA, n + 1)
                if n > 0:
                    have(dve, p_s, i, NCA, n)
                else:
                    freed(dve, p_s, i, NCA, NCA)
                dve.tensor_copy(QT[:], qb[:]).then_inc(v_qT, 1)

            def mla_max(i, n):
                have(dve, p_s, i, NCA, n + 1)
                if n > 0:
                    have(dve, v_sub, i, NCA, n)
                else:
                    freed(dve, v_sub, i, NCA, NCA)
                bank = sa[n % 2][:].rearrange("p (h s) -> p h s", h=HC)
                dve.tensor_reduce(mxa[:], bank, AX.X, ALU.max).then_inc(v_mx, 1)
                have(dve, v_mx, i, NCA, n + 1)
                dve.tensor_tensor(Pa[:, n % 2, :].rearrange("p (h s) -> p h s", h=HC), bank,
                                  mxa[:].unsqueeze(2).to_broadcast([128, HC, 128]), ALU.subtract).then_inc(v_sub, 1)

            def mla_out_norm(i, n):
                have(dve, p_pv, i, NCA, n + 1)
                if n > 0:
                    have(dve, v_o, i, NCA, n)
                else:
                    freed(dve, v_o, i, NCA, NCA)
                o = ob[:, 0:HC * 65].rearrange("p (h c) -> p h c", h=HC)
                dve.reciprocal(rec[:].unsqueeze(2), o[:, :, KL:KL + 1]).then_inc(v_rc, 1)
                have(dve, v_rc, i, NCA, n + 1)
                dve.tensor_tensor(Oa[:], o[:, :, 0:KL], rec[:].unsqueeze(2).to_broadcast([128, HC, KL]), ALU.mult)\
                   .then_inc(v_o, 1)

            def mla_norm_stats(i):
                have(dve, p_y, i, 1, 1)
                have(dve, d_xr, i, 16, 16)
                freed(dve, v_x1, i, 1, 1)
                dve.tensor_tensor(r1[:], x_res[:], ob[:, 0:D], ALU.add).then_inc(v_l1, 1)
                have(dve, v_l1, i, 3, 1)
                dve.bn_stats(st1[:], r1[:]).then_inc(v_l1, 1)
                have(dve, v_l1, i, 3, 2)
                freed(dve, g_l1, i, 2, 2)
                dve.tensor_copy(carry[:], st1[:, 0:1])
                dve.bn_aggr(mv1[:], st1[:]).then_inc(v_l1, 1)

            def mla_norm(i):
                have(dve, g_l1, i, 2, 2)
                freed(dve, q_xT, i, 1, 1)
                freed(dve, g_x1, i, 1, 1)
                dve.tensor_scalar(x1[:], r1[:], mv1[:, 0:1], rs1[:], ALU.subtract, ALU.mult).then_inc(v_x1, 1)

            def xat_split_ctx(i):
                have(dve, b_xs, i, 2, 1)
                dve.tensor_tensor(xcl[:, 2:4, :], ctxT[:], f32(xch[:, 2:4, :]), ALU.subtract).then_inc(w_xs, 1)

            def xat_split_x(i):
                have(dve, b_xs, i, 2, 2)
                dve.tensor_tensor(xcl[:, 0:2, :].rearrange("p k t -> p (k t)"), mb[:, 0:256],
                                  f32(xch[:, 0:2, :].rearrange("p k t -> p (k t)")), ALU.subtract).then_inc(w_xs, 1)

            def xat_bias(i):
                have(dve, q_qkv, i, 1, 1)
                freed(dve, b_ar, i, 2, 2)
                freed(dve, g_ar, i, 2, 2)
                freed(dve, g_vx, i, 1, 1)
                dve.tensor_tensor(qkv[:], mb[:, 0:384], bqkv[:], ALU.add).then_inc(w_qkv, 1)

            def xat_mask(i):
                have(dve, d_p, i, 16, 16)
                freed(dve, q_s, i, NCX, NCX)
                dve.scalar_tensor_tensor(comb[:], pad8[:], -BIG, ssmask[:], ALU.mult, ALU.add).then_inc(w_cm, 1)

            def xat_keys(i, half):
                have(dve, q_kT, i, 1, 1)
                freed(dve, q_s, i, NCX, (half + 1) * HC)
                dve.tensor_tensor(KX[:, half], mb[:, half * 128:(half + 1) * 128].unsqueeze(1).to_broadcast([128, HALF, 128]),
                                  groupsel[:].unsqueeze(2).to_broadcast([128, HALF, 128]), ALU.mult).then_inc(w_kx, 1)

            def xat_max(i, n):
                have(dve, q_s, i, NCX, n + 1)
                if n == NCX - 1:
                    freed(dve, w_o, i, 3, 1)
                bank = sx[n % 2][:].rearrange("p (h s) -> p h s", h=HC)
                dve.tensor_reduce(mxx[:, n, :], bank, AX.X, ALU.max).then_inc(w_mx, 1)
                have(dve, w_mx, i, NCX, n + 1)
                dve.tensor_tensor(Px[:, n % 2, :].rearrange("p (h s) -> p h s", h=HC), bank,
                                  mxx[:, n, :].unsqueeze(2).to_broadcast([128, HC, 128]), ALU.subtract).then_inc(w_sub, 1)

            def xat_out_norm(i):
                have(dve, q_pv, i, NCX, NCX)
                o = xo[:, 0:XH * (HD + 1)].rearrange("p (h c) -> p h c", h=XH)
                dve.scalar_tensor_tensor(den[:].unsqueeze(2), mxx[:, NCX - 1, 0:1].unsqueeze(1).to_broadcast([128, XH, 1]), -BIG / 2,
                                         o[:, :, HD:HD + 1], ALU.is_gt, ALU.mult).then_inc(w_o, 1)
                have(dve, w_o, i, 3, 1)
                dve.reciprocal(recx[:], den[:]).then_inc(w_o, 1)
                have(dve, w_o, i, 3, 2)
                freed(dve, q_oT, i, 1, 1)
                dve.tensor_tensor(Ox[:], o[:, :, 0:HD], recx[:].unsqueeze(2).to_broadcast([128, XH, HD]), ALU.mult)\
                   .then_inc(w_o, 1)

            def xat_out_lo(i):
                have(dve, b_oT, i, 1, 1)
                dve.tensor_tensor(OTxl[:].rearrange("p k t -> p (k t)"), mb[:, 0:256],
                                  f32(OTxh[:].rearrange("p k t -> p (k t)")), ALU.subtract).then_inc(w_oT, 1)

            def xat_norm_stats(i):
                have(dve, q_y, i, 1, 1)
                have(dve, g_xb, i, 1, 1)
                freed(dve, w_x2, i, 1, 1)
                dve.tensor_tensor(r2[:], x1b[:], mb[:, 0:D], ALU.add).then_inc(w_l2, 1)
                have(dve, w_l2, i, 3, 1)
                dve.bn_stats(st2[:], r2[:]).then_inc(w_l2, 1)
                have(dve, w_l2, i, 3, 2)
                freed(dve, g_l2, i, 2, 2)
                dve.tensor_copy(carry[:], st2[:, 0:1])
                dve.bn_aggr(mv2[:], st2[:]).then_inc(w_l2, 1)

            def xat_norm(i):
                have(dve, g_l2, i, 2, 2)
                freed(dve, d_x2, i, 16, 16)
                dve.tensor_scalar(x2[:], r2[:], mv2[:, 0:1], rs2[:], ALU.subtract, ALU.mult).then_inc(w_x2, 1)

            def step(j):
                for n in range(NCA):
                    if n == 0 and there(j - 1): mla_norm_stats(j - 1)
                    if n == 1 and there(j + 1): mla_normalise(j + 1)
                    if n == 1 and there(j - 3): xat_norm(j - 3)
                    if there(mla_chunk(j, n + 1)[0]): mla_max(*mla_chunk(j, n + 1))
                    if n == 2 and there(j + 1): mla_latents_lo(j + 1)
                    if there(xat_chunk(j - 2, 2 * n + 2)[0]): xat_max(*xat_chunk(j - 2, 2 * n + 2))
                    if n == 0 and there(j - 1): mla_norm(j - 1)
                    if n == 0 and there(j - 3): xat_out_lo(j - 3)
                    if n == 1 and there(j - 1): xat_split_x(j - 1)
                    if there(mla_chunk(j, n + 2)[0]): mla_rotate_sine(*mla_chunk(j, n + 2))
                    if n == 2 and there(j - 1): xat_keys(j - 1, 0)
                    if there(j): mla_out_norm(j, n)
                    if there(xat_chunk(j - 2, 2 * n + 3)[0]): xat_max(*xat_chunk(j - 2, 2 * n + 3))
                    if n == 0 and there(j - 3): xat_norm_stats(j - 3)
                    if n == 1 and there(j - 1): xat_bias(j - 1)
                    if n == 2 and there(j - 1):
                        xat_keys(j - 1, 1)
                        xat_mask(j - 1)
                    if n == 3 and there(j - 2): xat_out_norm(j - 2)
                    if there(mla_chunk(j, n + 2)[0]): mla_query_T_take(*mla_chunk(j, n + 2))
                    if n == 3 and there(j): xat_split_ctx(j)
                    if n == 3 and there(j + 2): mla_split(j + 2)

            mla_split(0)
            pipeline(dve, step)

            def chunk(c):
                def after(k):
                    dve.wait_ge(f_v, c * F_V + k)

                for k in range(KT_D):
                    dve.wait_ge(f_hi, c * (2 * KT_D) + (2 * k + 2))
                    dve.tensor_tensor(x2Tl[:, k, :], x2T[:, k, :], f32(x2Th[:, k, :]), ALU.subtract).then_inc(f_lo, 1)
                dve.wait_ge(f_lg, c * TC + TC)
                dve.tensor_copy(lg[:].rearrange("p t e -> p (t e)"), ob[:, 0:TC * E]).then_inc(f_v, 1)
                after(1)
                if not isinstance(c, int):
                    dve.wait_ge(f_st, c * 16)
                dve.tensor_copy(acc[:], x2c[:]).then_inc(f_ac, 1)
                for t in range(TC):
                    last = dve.max(top[:, t, :], lg[:, t, :])
                last.then_inc(f_v, 1)
                after(2)
                dve.tensor_tensor(dd[:].unsqueeze(2), top[:, :, 1:2], top[:, :, 0:1], ALU.subtract).then_inc(f_v, 1)
                for t in range(TC):
                    last = dve.max_index(topi[:, t, :], top[:, t, :], lg[:, t, :])
                last.then_inc(f_v, 1)
                after(4)
                dve.tensor_copy(topf[:], topi[:, :, 0:2]).then_inc(f_v, 1)
                dve.wait_ge(f_p2, c + 1)
                dve.tensor_scalar(p2d[:], p2e[:], 1.0, None, ALU.add).then_inc(f_v, 1)
                after(6)
                dve.reciprocal(pr[:, :, 0:1].rearrange("p t a -> p (t a)"), p2d[:]).then_inc(f_v, 1)
                after(7)
                dve.tensor_tensor(pr[:, :, 1:2].rearrange("p t a -> p (t a)"), p2e[:],
                                  pr[:, :, 0:1].rearrange("p t a -> p (t a)"), ALU.mult).then_inc(f_v, 1)
                after(8)
                for oh, a in ((oh1, 0), (oh2, 1)):
                    dve.tensor_tensor(oh[:], eidx[:].unsqueeze(1).to_broadcast([128, TC, E]),
                                      topf[:, :, a:a + 1].to_broadcast([128, TC, E]), ALU.is_equal).then_inc(f_v, 1)
                after(10)
                for oh, a in ((oh1, 0), (oh2, 1)):
                    dve.tensor_tensor(oh[:], oh[:], pr[:, :, a:a + 1].to_broadcast([128, TC, E]), ALU.mult).then_inc(f_v, 1)
                after(12)
                dve.tensor_tensor(wt[:], oh1[:], oh2[:], ALU.add).then_inc(f_v, 1)
                after(13)
                for e in range(E):
                    for t in range(TC):
                        if t % 2 == 0:
                            dve.wait_ge(f_y, c * (2 * E) + (2 * e + t // 2 + 1))
                        dve.wait_ge(f_ac, c * F_AC + (1 if e == 0 else (e - 1) * TC + t + 2))
                        dve.scalar_tensor_tensor(acc[:, t, :], (sx[0], sx[1])[t // 2][:, (t % 2) * D:(t % 2 + 1) * D],
                                                 wt[:, t, e:e + 1], acc[:, t, :], ALU.mult, ALU.add).then_inc(f_ac, 1)
                dve.wait_ge(f_ac, c * F_AC + F_AC)
                for t in range(TC):
                    dve.bn_stats(st3[:, t, :], acc[:, t, :]).then_inc(f_ln, 1)
                dve.wait_ge(f_ln, c * F_LN + TC)
                dve.tensor_copy(carry[:], st3[:, 0, 0:1])
                for t in range(TC):
                    dve.bn_aggr(mv3[:, t, :], st3[:, t, :]).then_inc(f_ln, 1)
                dve.wait_ge(f_gl, c * 2 + 2)
                for t in range(TC):
                    dve.tensor_scalar(acc[:, t, :], acc[:, t, :], mv3[:, t, 0:1], rs3[:, t:t + 1],
                                      ALU.subtract, ALU.mult).then_inc(f_ln, 1)

            chunk(0)
            with dve.Fori(1, NCH) as c:
                chunk(c)

        @block.gpsimd
        def _(gp):
            gp.wait_ge(c_ok, N_CONST)

            def power(dst, var, tmp, eps, s, i, per=2):
                gp.tensor_tensor(tmp, var, eps.to_broadcast(list(tmp.shape)), ALU.add).then_inc(s, 1)
                gp.wait_ge(s, i * per + 1)
                gp.tensor_tensor(dst, tmp, mhalf[:, 0:1].to_broadcast(list(tmp.shape)), ALU.pow).then_inc(s, 1)

            def mla_rstd(i):
                have(gp, a_sq, i, 2, 2)
                freed(gp, v_qk, i, 5, 5)
                power(rstd[:], ms[:], mse[:], rms_eps[:], g_rs, i)

            def mla_rest(i):
                have(gp, v_qk, i, 5, 3)
                freed(gp, p_aT, i, 1, 1)
                gp.tensor_tensor(kvn[:, 0:64], kc[:], ks[:], ALU.add).then_inc(g_qk, 1)
                gp.tensor_copy(qn[:, 128:192].bitcast(F32R), qraw[:]).then_inc(g_qk, 1)
                have(gp, g_qk, i, 3, 2)
                gp.tensor_tensor(qn[:, 192:256], qraw[:], qn[:, 128:192], ALU.subtract).then_inc(g_qk, 1)

            def mla_keep_values(i):
                have(gp, v_qk, i, 5, 5)
                freed(gp, p_pv, i, NCA, NCA)
                gp.tensor_tensor(kv[:, 0:KL], kvn[:, 64:128], zero[:].to_broadcast([128, KL]), ALU.add).then_inc(g_kv, 1)

            def mla_rotate(i, n):
                have(gp, a_q, i, NCA, n + 1)
                gp.tensor_tensor(rcos[:], Qs[:, :, 0:DR], cosine[:].unsqueeze(1).to_broadcast([128, HC, DR]), ALU.mult)\
                  .then_inc(g_rp, 1)
                have(gp, g_rp, i, 2 * NCA, 2 * n + 1)
                have(gp, v_rp, i, NCA, n + 1)
                gp.tensor_tensor(Qs[:, :, 0:DR], rcos[:], rsin[:], ALU.add).then_inc(g_rp, 1)

            def mla_norm(i):
                have(gp, v_l1, i, 3, 3)
                freed(gp, v_x1, i, 1, 1)
                power(rs1[:], mv1[:, 1:2], ve1[:], ln_eps[:], g_l1, i)

            def xat_keep(i):
                have(gp, v_x1, i, 1, 1)
                freed(gp, g_xb, i, 1, 1)
                gp.tensor_tensor(x1k[:], x1[:], zero[:].to_broadcast([128, D]), ALU.add).then_inc(g_x1, 1)

            def xat_keep_biased(i):
                have(gp, g_x1, i, 1, 1)
                freed(gp, w_l2, i, 3, 1)
                gp.tensor_tensor(x1b[:], x1k[:], bo[:], ALU.add).then_inc(g_xb, 1)

            def xat_arrange_lo(i):
                have(gp, b_ar, i, 2, 2)
                gp.tensor_tensor(karr[:, :, :, 1, :],
                                 qkv[:, 256:320].rearrange("p (n c) -> p n c", n=2).unsqueeze(2).to_broadcast([128, 2, 2, SLOT]),
                                 karr[:, :, :, 0, :], ALU.subtract).then_inc(g_ar, 1)
                gp.tensor_tensor(qarr[:, :, 2:4, :],
                                 qkv[:, 0:256].rearrange("p (n c) -> p n c", n=NCX).unsqueeze(2).to_broadcast([128, NCX, 2, SLOT]),
                                 qarr[:, :, 0:2, :], ALU.subtract).then_inc(g_ar, 1)

            def xat_keep_values(i):
                have(gp, w_qkv, i, 1, 1)
                freed(gp, q_pv, i, NCX, NCX)
                gp.tensor_tensor(vx[:, :, 0:HD], qkv[:, 320:384].rearrange("p (g d) -> p g d", g=G),
                                 zero[:].unsqueeze(2).to_broadcast([128, G, HD]), ALU.add).then_inc(g_vx, 1)

            def xat_norm(i):
                have(gp, w_l2, i, 3, 3)
                freed(gp, w_x2, i, 1, 1)
                power(rs2[:], mv2[:, 1:2], ve2[:], ln_eps[:], g_l2, i)

            def step(j):
                for n in range(NCA):
                    if n == 0 and there(j - 1): mla_norm(j - 1)
                    if n == 1 and there(j - 2): xat_keep_biased(j - 2)
                    if n == 1 and there(j - 1): xat_keep(j - 1)
                    if n == 1 and there(j + 1): mla_rest(j + 1)
                    if n == 2 and there(j - 1): xat_arrange_lo(j - 1)
                    if there(mla_chunk(j, n + 2)[0]): mla_rotate(*mla_chunk(j, n + 2))
                    if n == 0 and there(j - 3): xat_norm(j - 3)
                    if n == 0 and there(j + 1): mla_rstd(j + 1)
                    if n == 3 and there(j - 1): xat_keep_values(j - 1)
                    if n == 3 and there(j + 1): mla_keep_values(j + 1)
                if isinstance(j, int) and j == 0:
                    gp.wait_ge(wf_ld, 32)
                    gp.tensor_copy(wfch[:], wfc).then_inc(wf_ok, 1)
                    gp.wait_ge(wf_ok, 1)
                    gp.tensor_tensor(wfcl[:], wfc, f32(wfch[:]), ALU.subtract).then_inc(wf_ok, 1)

            pipeline(gp, step)

            def chunk(c):
                for e in range(E):
                    for m in range(2):
                        gp.wait_ge(f_r, c * (2 * E) + (2 * e + m + 1))
                        earlier(gp, f_y, c, 2 * E, 2 * (e - 1))
                        gp.tensor_tensor(h2[:, e % 2, m, :], hr[:, m, :], hr[:, m, :], ALU.mult).then_inc(f_sq, 1)
                gp.wait_ge(f_ln, c * F_LN + 2 * TC)
                power(rs3[:], mv3[:, :, 1:2].rearrange("p t a -> p (t a)"), ve3[:], ln_eps[:], f_gl, c)

            chunk(0)
            with gp.Fori(1, NCH) as c:
                chunk(c)


def kernel(**inputs):
    import concourse.bacc as bacc
    from concourse.bass_utils import run_bass_kernel_spmd

    a = {k: np.asarray(v) for k, v in inputs.items()}
    x, ctx = a["x"], a["ctx_2048"]
    wq_b = a["L0_attn_wq_b"].reshape(QL, H, DN + DR)
    wkv_b = a["L0_attn_wkv_b"].reshape(KL, H, DN + DV)
    rest = slice(128, QL)
    nopeT = wq_b[:, :, :DN].transpose(2, 1, 0)
    qln = a["L0_attn_q_a_ln_w"]

    def group_order(w, axis):
        w = np.moveaxis(w, axis, -1)
        lead = w.shape[:-1]
        w = w.reshape(*lead, 2, HALF, HC, HD).swapaxes(-3, -2).reshape(*lead, XH * HD)
        return np.moveaxis(w, -1, axis)

    def tokens_last(v):
        return v.reshape(B * S, KT_D, 128).transpose(2, 1, 0)

    inv = 1.0 / np.float32(10000.0) ** (np.arange(0, DR, 2, dtype=np.float32) / np.float32(DR))
    angle = np.outer(np.arange(S, dtype=np.float32), inv.astype(np.float32)).astype(np.float32)
    cos, sin = np.cos(angle), np.sin(angle)
    row = np.arange(128)
    arrays = {
        "x": x, "xT": tokens_last(x), "ctxT": tokens_last(ctx),
        "ssmask": a["mask_SxS2_bc0"], "padmask": a["mask_BxS2_bk0"],
        "wa": np.concatenate([a["L0_attn_wq_a"], a["L0_attn_wkv_a"]], axis=1),
        "wqnT": np.concatenate([nopeT, nopeT[:, :, rest]], axis=2),
        "wkvT": np.stack([wkv_b[:, :, :DN].transpose(2, 1, 0), wkv_b[:, :, DN:].transpose(2, 1, 0)], axis=1),
        "wpe": np.stack([wq_b[:128, :, DN:], np.concatenate([wq_b[rest, :, DN:]] * 2)], axis=1),
        "wo": a["L0_attn_wo"],
        "qln": np.stack([qln[:128], np.concatenate([qln[rest]] * 2)], axis=1),
        "kvln": a["L0_attn_kv_a_ln_w"],
        "xw": np.concatenate([group_order(a["L0_xattn_Wq"], 0).T, a["L0_xattn_Wk"].T, a["L0_xattn_Wv"].T,
                              group_order(a["L0_xattn_Wo"], 1).T], axis=1),
        "bqkv": np.concatenate([group_order(a["L0_xattn_bq"], 0), a["L0_xattn_bk"], a["L0_xattn_bv"]]),
        "bo": a["L0_xattn_bo"],
        "wr": a["L0_ffn_w_router"], 
        "wfc": a["L0_ffn_w_fc"].reshape(E, KT_D, 128, D).transpose(2, 1, 0, 3),
        "wpj": a["L0_ffn_w_proj"].reshape(E, KT_D, 128, D).transpose(2, 0, 1, 3),
        "c_ident": np.eye(128, dtype=np.float32),
        "c_causal": np.where(row[None, :] > row[:, None], np.float32(-BIG), np.float32(0)),
        "c_cos": np.concatenate([cos, cos], axis=1), "c_sin": np.concatenate([-sin, sin], axis=1),
        "c_groupsel": (row[:, None] % SLOT // HD == np.arange(HALF)).astype(np.float32),
        "c_eidx": np.tile(np.arange(E, dtype=np.float32), (128, 1)),
    }
    arrays = {k: np.ascontiguousarray(v) for k, v in arrays.items()}
    nc = bacc.Bacc("TRN2", target_bir_lowering=False, num_devices=1)
    io = {k: nc.dram_tensor(f"in_{k}", v.shape, mybir.dt.from_np(v.dtype), kind="ExternalInput").ap()
          for k, v in arrays.items()}
    io["out"] = nc.dram_tensor("out_x", (B, S, D), F32, kind="ExternalOutput").ap()
    decoder_layer(nc, io)
    r = run_bass_kernel_spmd(nc, [{f"in_{k}": v for k, v in arrays.items()}], core_ids=[0])
    return r.results[0]["out_x"]
```

```python
from contextlib import ExitStack

import numpy as np

import concourse.bass as bass
from concourse import mybir

F32 = mybir.dt.float32
F32R = mybir.dt.float32r
BF16 = mybir.dt.bfloat16
U8 = mybir.dt.uint8
U32 = mybir.dt.uint32
ALU = mybir.AluOpType
ACT = mybir.ActivationFunctionType
AX = mybir.AxisListType

B, S, D = 16, 128, 256
KT_D = D // 128
H, QL, KL, DR, DN, DV = 16, 192, 64, 64, 128, 128
QB = QL - 128
HC = 4
NCA = H // HC
XH, G, HD = 32, 8, 8
NCX = XH // HC
HALF = G // 2
SLOT = HALF * HD
E, TOPK = 8, 2
TC = 4
NCH = B // TC
NPX = 4
BIG = 1e30
MLA_SCALE = float((DN + DR) ** -0.5)
XAT_SCALE = float(HD ** -0.5)
RMS_EPS, LN_EPS = 1e-6, 1e-5


def decoder_layer(nc, io):
    with ExitStack() as ctx:
        def sb(name, shape, dt=F32):
            return ctx.enter_context(nc.sbuf_tensor(name, shape, dt))

        def ps(name):
            return ctx.enter_context(nc.psum_tensor(name, [128, 512], F32))

        def sem(name):
            return ctx.enter_context(nc.semaphore(name))

        def f32(t):
            return t.bitcast(F32)

        x2_hbm = nc.dram_tensor("x2_hbm", (B, S, D), F32).ap()

        ident = sb("ident", [128, 128])
        causal = sb("causal", [128, 128])
        cosine = sb("cosine", [128, DR])
        sine = sb("sine", [128, DR])
        groupsel = sb("groupsel", [128, HALF])
        eidx = sb("eidx", [128, E])
        mhalf = sb("mhalf", [128, 1])
        zero = sb("zero", [128, 1])
        rms_eps = sb("rms_eps", [128, 1])
        ln_eps = sb("ln_eps", [128, 1])
        carry = sb("carry", [128, 1])
        wah = sb("wah", [128, KT_D, 320], F32R)
        wal = sb("wal", [128, KT_D, 320], F32R)
        with nc.sbuf_tensor("stage1", [128, 4096], F32) as stage1:
            pass
        wfcl = sb("wfcl", [128, KT_D, E, D], F32R)
        stage2 = sb("stage2", [128, 4096])
        wqnT = stage1[:].rearrange("p (h a) -> p h a", h=H)
        wo_s = stage2[:].rearrange("p (h c) -> p h c", h=H)
        qln = sb("qln", [128, 2])
        kvln = sb("kvln", [128, KL])
        with nc.sbuf_tensor("WQh", [128, 2, H, 128], F32R) as WQh:
            pass
        h2 = sb("h2", [128, 2, KT_D, 512])
        acc = sb("acc", [128, TC, D])
        y3 = sb("y3", [128, TC, D])
        WQl = sb("WQl", [128, 2, H, 128], F32R)
        VO = sb("VO", [128, H // 2, D])
        xwh = sb("xwh", [128, KT_D, 640], F32R)
        xwl = sb("xwl", [128, KT_D, 640], F32R)
        bqkv = sb("bqkv", [128, 384])
        bo = sb("bo", [128, D])
        ssmask8 = sb("ssmask8", [128, 128], U8)
        ssmask = sb("ssmask", [128, 128], BF16)
        wr = sb("wr", [128, KT_D, E])
        wfch = sb("wfch", [128, KT_D, E, D], F32R)
        wfc = stage1[:].rearrange("p (k e d) -> p k e d", k=KT_D, e=E)
        wpj = stage2[:].rearrange("p (e k c) -> p e k c", e=E, k=KT_D)
        xT = sb("xT", [128, KT_D, 128])
        xTh = sb("xTh", [128, KT_D, 128], F32R)
        xTl = sb("xTl", [128, KT_D, 128], F32R)
        x_res = sb("x_res", [128, D])
        sqj = sb("sqj", [128, QL])
        ms = sb("ms", [128, 2])
        mse = sb("mse", [128, 2])
        rstd = sb("rstd", [128, 2])
        qn = sb("qn", [128, 256])
        qraw = sb("qraw", [128, QB])
        kvn = sb("kvn", [128, 128])
        kv = sb("kv", [128, KL + 1])
        kc = sb("kc", [128, DR])
        ks = sb("ks", [128, DR])
        qAh = sb("qAh", [128, 128], F32R)
        qAl = sb("qAl", [128, 128], F32R)
        qBs = sb("qBs", [128, 128], F32R)
        KT = sb("KT", [128, 128])
        Qs = sb("Qs", [128, HC, 128])
        rsin = sb("rsin", [128, HC, DR])
        rcos = sb("rcos", [128, HC, DR])
        QT = sb("QT", [128, HC * 128])
        mxa = sb("mxa", [128, HC])
        Pa = sb("Pa", [128, 2, 512])
        PTa = sb("PTa", [128, 2, 512])
        rec = sb("rec", [128, HC])
        Oa = sb("Oa", [128, HC, KL])
        OTa = sb("OTa", [128, H // 2, 128])
        r1 = sb("r1", [128, D])
        st1 = sb("st1", [128, 6])
        mv1 = sb("mv1", [128, 2])
        ve1 = sb("ve1", [128, 1])
        rs1 = sb("rs1", [128, 1])
        x1 = sb("x1", [128, D])
        ctxT = sb("ctxT", [128, KT_D, 128])
        xch = sb("xch", [128, 4, 128], F32R)
        xcl = sb("xcl", [128, 4, 128], F32R)
        x1b = sb("x1b", [128, D])
        x1k = sb("x1k", [128, D])
        qkv = sb("qkv", [128, 384])
        qarr = sb("qarr", [128, NCX, 4, SLOT])
        karr = sb("karr", [128, 2, 2, 2, SLOT])
        vx = sb("vx", [128, G, HD + 1])
        QX = sb("QX", [128, NCX, 128], F32R)
        KX = sb("KX", [128, 2, HALF, 128], F32R)
        pad8 = sb("pad8", [128, 128], U8)
        comb = sb("comb", [128, 128], BF16)
        mxx = sb("mxx", [128, NCX, HC])
        Px = sb("Px", [128, NPX, 512])
        PTx = sb("PTx", [128, 2, 512])
        den = sb("den", [128, XH])
        recx = sb("recx", [128, XH])
        Ox = sb("Ox", [128, XH, HD])
        OTxh = sb("OTxh", [128, KT_D, 128], F32R)
        OTxl = sb("OTxl", [128, KT_D, 128], F32R)
        r2 = sb("r2", [128, D])
        st2 = sb("st2", [128, 6])
        mv2 = sb("mv2", [128, 2])
        ve2 = sb("ve2", [128, 1])
        rs2 = sb("rs2", [128, 1])
        x2 = sb("x2", [128, D])
        setup_only = ExitStack()

        def loaded(name, shape, dt=F32):
            return setup_only.enter_context(nc.sbuf_tensor(name, shape, dt))

        stage3 = loaded("stage3", [128, 4096])
        wkT = stage3[:, 0:1024].rearrange("p (h c) -> p h c", h=H)
        wvT = stage3[:, 1024:2048].rearrange("p (h c) -> p h c", h=H)
        wpe = stage3[:, 2048:4096].rearrange("p (k h c) -> p k h c", k=2, h=H)
        wa = loaded("wa", [128, KT_D, 320])
        xw = loaded("xw", [128, KT_D, 640])
        setup_only.close()
        x2c = sb("x2c", [128, TC, D])
        x2T = sb("x2T", [128, KT_D, TC * 128])
        x2Th = sb("x2Th", [128, KT_D, TC * 128], F32R)
        x2Tl = sb("x2Tl", [128, KT_D, TC * 128], F32R)
        lg = sb("lg", [128, TC, E])
        top = sb("top", [128, TC, E])
        topi = sb("topi", [128, TC, E], U32)
        topf = sb("topf", [128, TC, 2])
        dd = sb("dd", [128, TC])
        p2e = sb("p2e", [128, TC])
        p2d = sb("p2d", [128, TC])
        pr = sb("pr", [128, TC, 2])
        oh1 = sb("oh1", [128, TC, E])
        oh2 = sb("oh2", [128, TC, E])
        wt = sb("wt", [128, TC, E])
        hr = sb("hr", [128, 2, 512])
        st3 = sb("st3", [128, TC, 6])
        mv3 = sb("mv3", [128, TC, 2])
        ve3 = sb("ve3", [128, TC])
        rs3 = sb("rs3", [128, TC])

        qb, ob = ps("qb"), ps("ob")
        sa = [ps("sa0"), ps("sa1")]
        mb, xo = ps("mb"), ps("xo")
        sx = [ps("sx0"), ps("sx1")]

        d_fold = sem("d_fold")
        d_ld = sem("d_ld")
        k_ok = sem("k_ok")
        c_ok = sem("c_ok")
        c_lo = sem("c_lo")
        s_p = sem("s_p")
        s_hi = sem("s_hi")
        o_p = sem("o_p")
        o_ok = sem("o_ok")
        s_lo = sem("s_lo")
        wf_ld = sem("wf_ld")
        wf_hi = sem("wf_hi")
        wf_lo = sem("wf_lo")
        d_x = sem("d_x")
        d_xr = sem("d_xr")
        d_c = sem("d_c")
        d_p = sem("d_p")
        d_x2 = sem("d_x2")
        a_xs = sem("a_xs")
        p_a = sem("p_a")
        a_sq = sem("a_sq")
        g_rs = sem("g_rs")
        v_qk = sem("v_qk")
        g_qk = sem("g_qk")
        g_kv = sem("g_kv")
        p_aT = sem("p_aT")
        a_aT = sem("a_aT")
        v_aT = sem("v_aT")
        p_q = sem("p_q")
        a_q = sem("a_q")
        v_rp = sem("v_rp")
        g_rp = sem("g_rp")
        p_qT = sem("p_qT")
        v_qT = sem("v_qT")
        p_s = sem("p_s")
        v_ms = sem("v_ms")
        v_mx = sem("v_mx")
        g_sub = sem("g_sub")
        a_ex = sem("a_ex")
        p_pT = sem("p_pT")
        a_pT = sem("a_pT")
        p_pv = sem("p_pv")
        v_rc = sem("v_rc")
        v_o = sem("v_o")
        p_oT = sem("p_oT")
        a_oT = sem("a_oT")
        p_y = sem("p_y")
        v_l1 = sem("v_l1")
        g_l1 = sem("g_l1")
        v_x1 = sem("v_x1")
        q_xT = sem("q_xT")
        b_xs = sem("b_xs")
        w_xs = sem("w_xs")
        g_x1 = sem("g_x1")
        g_xb = sem("g_xb")
        q_qkv = sem("q_qkv")
        w_qkv = sem("w_qkv")
        b_ar = sem("b_ar")
        g_ar = sem("g_ar")
        g_vx = sem("g_vx")
        q_kT = sem("q_kT")
        w_kx = sem("w_kx")
        q_qx = sem("q_qx")
        b_qx = sem("b_qx")
        w_cm = sem("w_cm")
        q_s = sem("q_s")
        w_ms = sem("w_ms")
        w_mx = sem("w_mx")
        h_sub = sem("h_sub")
        b_ex = sem("b_ex")
        q_pT = sem("q_pT")
        b_pT = sem("b_pT")
        q_pv = sem("q_pv")
        w_o = sem("w_o")
        q_oT = sem("q_oT")
        b_oT = sem("b_oT")
        w_oT = sem("w_oT")
        q_y = sem("q_y")
        w_l2 = sem("w_l2")
        g_l2 = sem("g_l2")
        w_x2 = sem("w_x2")
        f_ld = sem("f_ld")
        f_T = sem("f_T")
        f_ev = sem("f_ev")
        f_hi = sem("f_hi")
        f_lo = sem("f_lo")
        f_lg = sem("f_lg")
        f_v = sem("f_v")
        f_p2 = sem("f_p2")
        f_h = sem("f_h")
        f_r = sem("f_r")
        f_sq = sem("f_sq")
        f_y = sem("f_y")
        f_ac = sem("f_ac")
        f_ln = sem("f_ln")
        f_gl = sem("f_gl")
        f_st = sem("f_st")

        def there(i):
            return not isinstance(i, int) or 0 <= i < B

        def have(eng, s, i, per, k):
            if there(i):
                eng.wait_ge(s, i * per + k)

        def freed(eng, s, i, per, k):
            have(eng, s, i - 1, per, k)

        def mla_chunk(j, c):
            return j + c // NCA, c % NCA

        def xat_chunk(x, c):
            return x + c // NCX, c % NCX

        def pipeline(eng, step):
            for j in range(-1, LOOP_FROM):
                step(j)
            with eng.Fori(LOOP_FROM, B - 2) as j:
                step(j)
            for j in range(B - 2, B + 3):
                step(j)

        def phase_b_begins(j):
            return isinstance(j, int) and j == B

        def early_expert(j, n):
            e = (j - B) * NCA + n - 1 if isinstance(j, int) else -1
            return [e] if 0 <= e < E - 1 else []

        def first(c):
            return isinstance(c, int) and c == 0

        def final(c):
            return isinstance(c, int) and c == NCH - 1

        def prepare_at(c):
            return E - 1 if first(c) else E - 3

        def route_at(c):
            return E - 1 if first(c) else E - 2

        def chunks(eng, expert):
            expert(0, E - 1)
            with eng.Fori(1, NCH - 1) as c:
                for e in range(E):
                    expert(c, e)
            for e in range(E):
                expert(NCH - 1, e)

        def earlier(eng, s, c, per, k):
            if not first(c) or k > 0:
                eng.wait_ge(s, c * per + k)

        LOOP_FROM = 4
        N_CONST, N_LO = 11, 4
        WF_PARTS = 4
        F_V, F_LN, F_AC = 13, 3 * TC, TC * E
        N_FOLD_LOADS, N_LOADS = 4, 14

        block = ctx.enter_context(nc.Block())

        @block.sync
        def _(sp):
            def bc(ap, n):
                return ap.partition_broadcast(128)
            fold_loads = [
                (qln[:], io["qln"]), (kvln[:], bc(io["kvln"], KL)),
                (stage3[:, 0:2048].rearrange("p (k h c) -> p k h c", k=2, h=H), io["wkvT"]), (wqnT, io["wqnT"]),
            ]
            loads = [
                (wa[:], io["wa"].rearrange("(k p) n -> p k n", p=128)),
                (ident[:], io["c_ident"]), (causal[:], io["c_causal"]), (cosine[:], io["c_cos"]),
                (sine[:], io["c_sin"]), (groupsel[:], io["c_groupsel"]), (eidx[:], io["c_eidx"]),
                (wo_s, io["wo"].rearrange("(h p) c -> p h c", p=128)), (wpe, io["wpe"]),
                (xw[:], io["xw"].rearrange("(k p) n -> p k n", p=128)),
                (bqkv[:], bc(io["bqkv"], 384)), (bo[:], bc(io["bo"], D)),
                (ssmask8[:], io["ssmask"]), (wr[:], io["wr"].rearrange("(k p) n -> p k n", p=128)),
            ]
            assert (len(fold_loads), len(loads)) == (N_FOLD_LOADS, N_LOADS)
            for dst, src in fold_loads:
                sp.dma_start(dst, src).then_inc(d_fold, 16)
            for dst, src in loads:
                sp.dma_start(dst, src).then_inc(d_ld, 16)

            def load_xT(i):
                freed(sp, a_xs, i, 2, 2)
                sp.dma_start(xT[:], io["xT"][:, :, bass.ds(i * S, S)]).then_inc(d_x, 16)

            def load_x_res(i):
                freed(sp, v_l1, i, 3, 1)
                sp.dma_start(x_res[:], io["x"][i]).then_inc(d_xr, 16)

            def load_ctx(i):
                freed(sp, b_xs, i, 2, 1)
                freed(sp, w_xs, i, 2, 1)
                sp.dma_start(ctxT[:], io["ctxT"][:, :, bass.ds(i * S, S)]).then_inc(d_c, 16)

            def load_pad(i):
                freed(sp, w_cm, i, 1, 1)
                sp.dma_start(pad8[:], io["padmask"][i].partition_broadcast(128)).then_inc(d_p, 16)

            def store_x2(i):
                have(sp, w_x2, i, 1, 1)
                sp.dma_start(x2_hbm[i], x2[:]).then_inc(d_x2, 16)

            def step(j):
                if phase_b_begins(j): load_chunk(0)
                if isinstance(j, int) and j == B + 1: load_chunk(1)
                if there(j + 2): load_xT(j + 2)
                if there(j): load_x_res(j)
                if there(j - 3): store_x2(j - 3)
                if there(j): load_ctx(j)
                if there(j): load_pad(j)
                if isinstance(j, int) and j == -1:
                    sp.wait_ge(s_p, NCA)
                    sp.wait_ge(o_p, NCA)
                    sp.dma_start(wfc, io["wfc"]).then_inc(wf_ld, 16)
                    sp.dma_start(wpj, io["wpj"]).then_inc(wf_ld, 16)

            def load_chunk(c):
                if not first(c):
                    sp.wait_ge(f_ac, c * F_AC + (TC - F_AC))
                sp.wait_ge(d_x2, 16 * min(B, TC * (c + 1)) if isinstance(c, int) else 16 * B)
                sp.dma_start(x2c[:], x2_hbm[bass.ds(c * TC, TC)].rearrange("t p d -> p t d")).then_inc(f_ld, 16)

            def store_chunk(c):
                sp.wait_ge(f_ln, c * F_LN + F_LN)
                sp.dma_start(io["out"][bass.ds(c * TC, TC)].rearrange("t p d -> p t d"), y3[:]).then_inc(f_st, 16)

            load_xT(0)
            pipeline(sp, step)
            store_chunk(0)
            with sp.Fori(1, NCH - 1) as c:
                load_chunk(c + 1)
                store_chunk(c)
            store_chunk(NCH - 1)
            sp.wait_ge(f_st, 16 * NCH)

        @block.tensor
        def _(pe):
            pe.wait_ge(d_fold, 16 * N_FOLD_LOADS)
            pe.wait_ge(k_ok, 1)
            for n in range(NCA):
                if n >= 2:
                    pe.wait_ge(s_lo, 2 * (n - 2) + 2)
                bank = sa[n % 2]
                for j in range(HC):
                    h = HC * n + j
                    pe.matmul(bank[:, j * KL:(j + 1) * KL], wqnT[:, h, 0:128], wkT[:, h, :], start=True, stop=True)
                    last = pe.matmul(bank[:, 256 + j * KL:256 + (j + 1) * KL], wqnT[:, h, 128:256], wkT[:, h, :],
                                     start=True, stop=True)
                last.then_inc(s_p, 1)
            pe.wait_ge(d_ld, 16 * N_LOADS)
            for n in range(NCA):
                if n >= 2:
                    pe.wait_ge(o_ok, n - 1)
                bank = sx[n % 2]
                for j in range(HC):
                    h = HC * n + j
                    last = pe.matmul(bank[64 * (j % 2):64 * (j % 2) + 64, (j // 2) * D:(j // 2 + 1) * D],
                                     wvT[:, h, :], wo_s[:, h, :], start=True, stop=True)
                last.then_inc(o_p, 1)
            pe.wait_ge(c_ok, N_CONST)
            pe.wait_ge(s_lo, 2 * NCA)
            pe.wait_ge(o_ok, NCA)
            pe.wait_ge(c_lo, N_LO)

            def split_matmul(out, terms):
                for k, (w, m) in enumerate(terms):
                    last = pe.matmul(out, w, m, start=(k == 0), stop=(k == len(terms) - 1))
                return last

            def mla_latents(i):
                have(pe, a_xs, i, 2, 2)
                freed(pe, a_oT, i, NCA, 1)
                terms = []
                for k in range(KT_D):
                    terms += [(xTh[:, k, :], wah[:, k, :]), (xTh[:, k, :], wal[:, k, :]), (xTl[:, k, :], wah[:, k, :])]
                split_matmul(ob[:, 0:320], terms).then_inc(p_a, 1)

            def mla_latents_T(i):
                have(pe, g_qk, i, 3, 3)
                have(pe, v_qk, i, 5, 5)
                freed(pe, v_qT, i, NCA, NCA)
                pe.transpose(qb[:, 0:128], qn[:, 0:128], ident[:])
                pe.transpose(qb[:, 128:256], qn[:, 128:256], ident[:])
                pe.transpose(qb[:, 256:384], kvn[:], ident[:]).then_inc(p_aT, 1)

            def mla_query(i, n):
                if n == 0:
                    have(pe, a_aT, i, 3, 3)
                    have(pe, v_aT, i, 1, 1)
                else:
                    have(pe, v_qT, i, NCA, n)
                hs = slice(HC * n, HC * n + HC)
                split_matmul(qb[:], [(qAh[:], WQh[:, 0, hs, :]), (qAh[:], WQl[:, 0, hs, :]), (qAl[:], WQh[:, 0, hs, :]),
                                     (qBs[:], WQh[:, 1, hs, :]), (qBs[:], WQl[:, 1, hs, :])]).then_inc(p_q, 1)

            def mla_query_T(i, n):
                have(pe, g_rp, i, 2 * NCA, 2 * n + 2)
                for j in range(HC):
                    last = pe.transpose(qb[:, j * 128:(j + 1) * 128], Qs[:, j, :], ident[:])
                last.then_inc(p_qT, 1)

            def mla_scores(i, n):
                have(pe, v_qT, i, NCA, n + 1)
                if n >= 2:
                    have(pe, a_pT, i, NCA, n - 1)
                else:
                    freed(pe, a_pT, i, NCA, n + 3)
                bank = sa[n % 2]
                for j in range(HC):
                    last = pe.matmul(bank[:, j * 128:(j + 1) * 128], QT[:, j * 128:(j + 1) * 128], KT[:],
                                     start=True, stop=True)
                last.then_inc(p_s, 1)

            def mla_probs_T(i, n):
                have(pe, a_ex, i, NCA, n + 1)
                for j in range(HC):
                    last = pe.transpose(sa[n % 2][:, j * 128:(j + 1) * 128], Pa[:, n % 2, j * 128:(j + 1) * 128], ident[:])
                last.then_inc(p_pT, 1)

            def mla_values(i, n):
                have(pe, a_pT, i, NCA, n + 1)
                if n == 0:
                    have(pe, g_kv, i, 1, 1)
                    freed(pe, v_l1, i, 3, 1)
                elif n == 1:
                    have(pe, a_oT, i, NCA, n)
                    have(pe, v_qk, i + 1, 5, 5)
                else:
                    have(pe, a_oT, i, NCA, n)
                for j in range(HC):
                    last = pe.matmul(ob[:, j * 65:(j + 1) * 65], PTa[:, n % 2, j * 128:(j + 1) * 128], kv[:],
                                     start=True, stop=True)
                last.then_inc(p_pv, 1)

            def mla_out_T(i, n):
                have(pe, v_o, i, NCA, n + 1)
                for k in range(2):
                    last = pe.transpose(ob[:, k * 128:(k + 1) * 128],
                                        Oa[:, 2 * k:2 * k + 2, :].rearrange("p h c -> p (h c)"), ident[:])
                last.then_inc(p_oT, 1)

            def mla_project(i):
                have(pe, a_oT, i, NCA, NCA)
                split_matmul(ob[:, 0:D], [(OTa[:, k, :], VO[:, k, :]) for k in range(H // 2)]).then_inc(p_y, 1)

            def xat_x_T(i):
                have(pe, v_x1, i, 1, 1)
                have(pe, w_l2, i - 2, 3, 1)
                for k in range(KT_D):
                    last = pe.transpose(mb[:, k * 128:(k + 1) * 128], x1[:, k * 128:(k + 1) * 128], ident[:])
                last.then_inc(q_xT, 1)

            def xat_qkv(i):
                have(pe, b_xs, i, 2, 2)
                have(pe, w_xs, i, 2, 2)
                for lo, hi, t0 in ((0, 256, 0), (256, 384, 2)):
                    terms = []
                    for k in range(KT_D):
                        terms += [(xch[:, t0 + k, :], xwh[:, k, lo:hi]), (xch[:, t0 + k, :], xwl[:, k, lo:hi]),
                                  (xcl[:, t0 + k, :], xwh[:, k, lo:hi])]
                    last = split_matmul(mb[:, lo:hi], terms)
                last.then_inc(q_qkv, 1)

            def xat_keys_T(i):
                have(pe, b_ar, i, 2, 2)
                have(pe, g_ar, i, 2, 1)
                for k in range(2):
                    last = pe.transpose(mb[:, k * 128:(k + 1) * 128],
                                        karr[:, k].rearrange("p a b c -> p (a b c)"), ident[:])
                last.then_inc(q_kT, 1)

            def xat_queries_T(i, half):
                have(pe, g_ar, i, 2, 2)
                if half == 0:
                    have(pe, w_kx, i, 2, 2)
                else:
                    have(pe, b_qx, i, 2, 1)
                for r in range(HC):
                    last = pe.transpose(mb[:, r * 128:(r + 1) * 128],
                                        qarr[:, half * HC + r].rearrange("p a b -> p (a b)"), ident[:])
                last.then_inc(q_qx, 1)

            def xat_scores(i, n):
                if n == 0:
                    have(pe, w_kx, i, 2, 2)
                    freed(pe, w_ms, i, NCX, NCX)
                else:
                    have(pe, w_ms, i, NCX, n)
                if n % HC == 0:
                    have(pe, b_qx, i, 2, n // HC + 1)
                pe.matmul(sx[0][:], QX[:, n, :], KX[:, n // HC].rearrange("p g s -> p (g s)"), start=True, stop=True)\
                  .then_inc(q_s, 1)

            def xat_probs_T(i, n):
                have(pe, b_ex, i, NCX, n + 1)
                if n == 0:
                    freed(pe, b_pT, i, NCX, NCX)
                else:
                    have(pe, b_pT, i, NCX, n)
                for j in range(HC):
                    last = pe.transpose(sx[1][:, j * 128:(j + 1) * 128], Px[:, n % NPX, j * 128:(j + 1) * 128], ident[:])
                last.then_inc(q_pT, 1)

            def xat_values(i, n):
                have(pe, b_pT, i, NCX, n + 1)
                if n == 0:
                    have(pe, g_vx, i, 1, 1)
                    freed(pe, w_o, i, 3, 3)
                for j in range(HC):
                    c = (n * HC + j) * (HD + 1)
                    last = pe.matmul(xo[:, c:c + HD + 1], PTx[:, n % 2, j * 128:(j + 1) * 128],
                                     vx[:, (n // HC) * HALF + j, :], start=True, stop=True)
                last.then_inc(q_pv, 1)

            def xat_out_T(i):
                have(pe, w_o, i, 3, 3)
                have(pe, b_qx, i + 1, 2, 2)
                for k in range(KT_D):
                    last = pe.transpose(mb[:, k * 128:(k + 1) * 128],
                                        Ox[:, k * 16:(k + 1) * 16, :].rearrange("p h c -> p (h c)"), ident[:])
                last.then_inc(q_oT, 1)

            def xat_project(i):
                have(pe, b_oT, i, 1, 1)
                have(pe, w_oT, i, 1, 1)
                terms = []
                for k in range(KT_D):
                    terms += [(OTxh[:, k, :], xwh[:, k, 384:640]), (OTxh[:, k, :], xwl[:, k, 384:640]),
                              (OTxl[:, k, :], xwh[:, k, 384:640])]
                split_matmul(mb[:, 0:D], terms).then_inc(q_y, 1)

            def piece(x, c):
                late = c + 3 == NCX + 1
                if c + 3 != NCX and not late and there(xat_chunk(x, c + 3)[0]): xat_scores(*xat_chunk(x, c + 3))
                if there(xat_chunk(x, c + 1)[0]): xat_probs_T(*xat_chunk(x, c + 1))
                if there(x): xat_values(x, c)
                if late and there(x + 1): xat_scores(x + 1, 1)

            def step(j):
                if there(j - 1): mla_query_T(j - 1, 3)
                if there(j - 3): xat_probs_T(j - 3, 3)
                if there(j - 3): xat_values(j - 3, 2)
                if there(j - 1): mla_scores(j - 1, 3)
                for e in early_expert(j, 0): expert(0, e)
                if there(j - 3): xat_probs_T(j - 3, 4)
                if there(j): mla_latents_T(j)
                if there(j - 3): xat_scores(j - 3, 7)
                if there(j - 1): mla_values(j - 1, 1)
                if there(j - 2): xat_keys_T(j - 2)
                if there(j - 3): xat_probs_T(j - 3, 5)
                if there(j): mla_query(j, 0)
                if there(j - 1): mla_probs_T(j - 1, 2)
                if there(j - 2): xat_queries_T(j - 2, 0)
                if there(j - 3): xat_values(j - 3, 3)
                if there(j - 1): mla_out_T(j - 1, 1)
                if there(j - 3): xat_values(j - 3, 4)
                if there(j - 2): xat_scores(j - 2, 0)
                if there(j - 1): mla_probs_T(j - 1, 3)
                if there(j): mla_query_T(j, 0)
                if there(j - 1): mla_values(j - 1, 2)
                if there(j - 3): xat_probs_T(j - 3, 6)
                if there(j): mla_scores(j, 0)
                if there(j): mla_query(j, 1)
                if there(j - 2): xat_scores(j - 2, 1)
                if there(j - 1): mla_out_T(j - 1, 2)
                if there(j - 3): xat_probs_T(j - 3, 7)
                if there(j - 3): xat_values(j - 3, 5)
                if there(j - 2): xat_queries_T(j - 2, 1)
                if there(j - 1): mla_values(j - 1, 3)
                if there(j - 3): xat_values(j - 3, 6)
                if there(j - 3): xat_values(j - 3, 7)
                if there(j - 1): mla_out_T(j - 1, 3)
                if there(j - 2): xat_scores(j - 2, 2)
                if there(j): mla_probs_T(j, 0)
                if there(j): mla_query_T(j, 1)
                if there(j - 1): mla_project(j - 1)
                if phase_b_begins(j): prepare_T(0)
                if there(j - 2): xat_scores(j - 2, 3)
                if there(j): mla_query(j, 2)
                if there(j - 2): xat_probs_T(j - 2, 0)
                if there(j): mla_values(j, 0)
                if there(j): mla_scores(j, 1)
                if phase_b_begins(j): route(0)
                if there(j - 3): xat_out_T(j - 3)
                if there(j - 2): xat_values(j - 2, 0)
                if there(j): mla_out_T(j, 0)
                if there(j - 2): xat_probs_T(j - 2, 1)
                if there(j - 2): xat_scores(j - 2, 4)
                if there(j): mla_query_T(j, 2)
                if there(j + 1): mla_latents(j + 1)
                if there(j - 3): xat_project(j - 3)
                for e in early_expert(j, 1): expert(0, e)
                if there(j - 2): xat_scores(j - 2, 5)
                if there(j - 2): xat_values(j - 2, 1)
                if there(j): mla_query(j, 3)
                for e in early_expert(j, 2): expert(0, e)
                if there(j - 2): xat_probs_T(j - 2, 2)
                if there(j - 1): xat_x_T(j - 1)
                if there(j - 2): xat_scores(j - 2, 6)
                if there(j): mla_scores(j, 2)
                for e in early_expert(j, 3): expert(0, e)
                if there(j): mla_probs_T(j, 1)
                if there(j - 1): xat_qkv(j - 1)

            def prepare_T(c):
                pe.wait_ge(f_ld, c * 16 + 16)
                if isinstance(c, int) and c == 0:
                    pe.wait_ge(a_pT, B * NCA)
                    pe.wait_ge(wf_lo, WF_PARTS)
                elif isinstance(c, int) and c == 1:
                    pe.wait_ge(b_pT, B * NCX)
                for k in range(KT_D):
                    bank = (sa if isinstance(c, int) and c == 0 else sx)[k]
                    for t in range(TC):
                        last = pe.transpose(bank[:, t * 128:(t + 1) * 128], x2c[:, t, k * 128:(k + 1) * 128], ident[:])
                    last.then_inc(f_T, 1)

            def route(c):
                pe.wait_ge(f_ev, c * KT_D + KT_D)
                if isinstance(c, int) and c == 0:
                    pe.wait_ge(v_qT, B * NCA)
                elif isinstance(c, int) and c == 1:
                    pe.wait_ge(w_l2, B * 3)
                bank = qb if isinstance(c, int) and c == 0 else mb
                for t in range(TC):
                    last = split_matmul(bank[:, t * E:(t + 1) * E],
                                        [(x2T[:, k, t * 128:(t + 1) * 128], wr[:, k, :]) for k in range(KT_D)])
                last.then_inc(f_lg, 1)

            def hidden(c, e):
                if e == 0:
                    pe.wait_ge(f_lo, c * KT_D + KT_D)
                for m in range(2):
                    earlier(pe, f_r, c, 2 * E, 2 * (e - 1) + m + 1)
                    terms = []
                    for k in range(KT_D):
                        w = slice(m * 128, (m + 1) * 128)
                        terms += [(wfch[:, k, e, w], x2Th[:, k, :]), (wfcl[:, k, e, w], x2Th[:, k, :]),
                                  (wfch[:, k, e, w], x2Tl[:, k, :])]
                    split_matmul(sa[m][:], terms).then_inc(f_h, 1)

            def project(c, e):
                if isinstance(c, int) and (c, e) == (0, 0):
                    pe.wait_ge(f_v, 1)
                    pe.wait_ge(v_l1, B * 3)
                pe.wait_ge(f_sq, c * (2 * E) + (2 * e + 2))
                for q in range(2):
                    earlier(pe, f_ac, c, F_AC, (e - 1) * TC + 2 * q + 2)
                    for u in range(2):
                        t = 2 * q + u
                        last = split_matmul((qb, ob)[q][:, u * D:(u + 1) * D],
                                            [(h2[:, e % 2, k, t * 128:(t + 1) * 128], wpj[:, e, k, :]) for k in range(KT_D)])
                    last.then_inc(f_y, 1)

            def expert(c, e):
                if e == 0:
                    if not first(c): project(c - 1, E - 1)
                    hidden(c, 0)
                else:
                    hidden(c, e)
                    project(c, e - 1)
                if e == prepare_at(c) and not final(c): prepare_T(c + 1)
                if e == route_at(c) and not final(c): route(c + 1)

            pipeline(pe, step)
            chunks(pe, expert)
            project(NCH - 1, E - 1)

        @block.scalar
        def _(act):
            act.wait_ge(d_fold, 16 * N_FOLD_LOADS)
            for n in range(NCA):
                act.wait_ge(s_p, n + 1)
                for k in range(2):
                    act.activation(WQh[:, k, HC * n:HC * n + HC, DR:128],
                                   sa[n % 2][:, k * 256:(k + 1) * 256].rearrange("p (h c) -> p h c", h=HC),
                                   ACT.Copy, scale=qln[:, k:k + 1]).then_inc(s_hi, 1)
            act.wait_ge(d_ld, 16 * N_LOADS)
            act.activation(wah[:], wa[:], ACT.Copy).then_inc(c_ok, 1)
            for k in range(2):
                act.activation(WQh[:, k, :, 0:DR], wpe[:, k], ACT.Copy, scale=qln[:, k:k + 1]).then_inc(c_ok, 1)
            act.activation(xwh[:], xw[:], ACT.Copy).then_inc(c_ok, 1)
            act.activation(ssmask[:], ssmask8[:], ACT.Copy, scale=-BIG).then_inc(c_ok, 1)
            for n in range(NCA):
                act.wait_ge(o_p, n + 1)
                act.activation(VO[:, 2 * n:2 * n + 2, :], sx[n % 2][:].rearrange("p (k c) -> p k c", k=2), ACT.Copy)\
                   .then_inc(o_ok, 1)

            def mla_split(i):
                have(act, d_x, i, 16, 16)
                freed(act, p_a, i, 1, 1)
                act.activation(xTh[:], xT[:], ACT.Copy).then_inc(a_xs, 1)

            def experts_split(q):
                act.wait_ge(wf_ld, 32)
                es = slice(q * E // WF_PARTS, (q + 1) * E // WF_PARTS)
                act.activation(wfch[:, :, es, :], wfc[:, :, es, :], ACT.Copy).then_inc(wf_hi, 1)

            def mla_squares(i):
                have(act, p_a, i, 1, 1)
                freed(act, g_rs, i, 2, 2)
                act.activation(sqj[:], ob[:, 0:QL], ACT.Square, scale=float(QL ** -0.5), accum_out=ms[:, 0:1]).then_inc(a_sq, 1)
                act.wait_ge(a_sq, i * 2 + 1)
                act.activation(sqj[:, 0:KL], ob[:, QL:QL + KL], ACT.Square, scale=float(KL ** -0.5),
                               accum_out=ms[:, 1:2]).then_inc(a_sq, 1)

            def mla_latents_take(i):
                have(act, p_aT, i, 1, 1)
                act.activation(qAh[:], qb[:, 0:128], ACT.Copy).then_inc(a_aT, 1)
                act.activation(qBs[:], qb[:, 128:256], ACT.Copy).then_inc(a_aT, 1)
                act.activation(KT[:], qb[:, 256:384], ACT.Copy).then_inc(a_aT, 1)

            def mla_query_take(i, n):
                have(act, p_q, i, NCA, n + 1)
                act.activation(Qs[:].rearrange("p h c -> p (h c)"), qb[:], ACT.Copy).then_inc(a_q, 1)

            def mla_exp(i, n):
                have(act, g_sub, i, NCA, n + 1)
                act.activation(Pa[:, n % 2, :], Pa[:, n % 2, :], ACT.Exp, scale=MLA_SCALE).then_inc(a_ex, 1)

            def mla_probs_take(i, n):
                have(act, p_pT, i, NCA, n + 1)
                if n >= 2:
                    have(act, p_pv, i, NCA, n - 1)
                else:
                    freed(act, p_pv, i, NCA, n + 3)
                act.activation(PTa[:, n % 2, :], sa[n % 2][:], ACT.Copy).then_inc(a_pT, 1)

            def mla_out_take(i, n):
                have(act, p_oT, i, NCA, n + 1)
                act.activation(OTa[:, 2 * n:2 * n + 2, :].rearrange("p k t -> p (k t)"), ob[:, 0:256], ACT.Copy)\
                   .then_inc(a_oT, 1)

            def xat_split_ctx(i):
                have(act, d_c, i, 16, 16)
                freed(act, q_qkv, i, 1, 1)
                act.activation(xch[:, 2:4, :], ctxT[:], ACT.Copy).then_inc(b_xs, 1)

            def xat_split_x(i):
                have(act, q_xT, i, 1, 1)
                act.activation(xch[:, 0:2, :].rearrange("p k t -> p (k t)"), mb[:, 0:256], ACT.Copy).then_inc(b_xs, 1)

            def xat_arrange_hi(i):
                have(act, w_qkv, i, 1, 1)
                freed(act, q_qx, i, 2, 2)
                act.activation(qarr[:, :, 0:2, :].bitcast(F32R),
                               qkv[:, 0:256].rearrange("p (n c) -> p n c", n=NCX).unsqueeze(2).to_broadcast([128, NCX, 2, SLOT]),
                               ACT.Copy).then_inc(b_ar, 1)
                act.activation(karr[:, :, :, 0, :].bitcast(F32R),
                               qkv[:, 256:320].rearrange("p (n c) -> p n c", n=2).unsqueeze(2).to_broadcast([128, 2, 2, SLOT]),
                               ACT.Copy).then_inc(b_ar, 1)

            def xat_queries_take(i, half):
                have(act, q_qx, i, 2, half + 1)
                freed(act, q_s, i, NCX, (half + 1) * HC)
                act.activation(QX[:, half * HC:(half + 1) * HC, :].rearrange("p n t -> p (n t)"), mb[:], ACT.Copy)\
                   .then_inc(b_qx, 1)

            def xat_exp(i, n):
                have(act, h_sub, i, NCX, n + 1)
                act.activation(Px[:, n % NPX, :], Px[:, n % NPX, :], ACT.Exp, scale=XAT_SCALE).then_inc(b_ex, 1)

            def xat_probs_take(i, n):
                have(act, q_pT, i, NCX, n + 1)
                if n >= 2:
                    have(act, q_pv, i, NCX, n - 1)
                else:
                    freed(act, q_pv, i, NCX, n + NCX - 1)
                act.activation(PTx[:, n % 2, :], sx[1][:], ACT.Copy).then_inc(b_pT, 1)

            def xat_out_take(i):
                have(act, q_oT, i, 1, 1)
                act.activation(OTxh[:].rearrange("p k t -> p (k t)"), mb[:, 0:256], ACT.Copy).then_inc(b_oT, 1)

            def step(j):
                for e in early_expert(j, 0): expert(0, e)
                if there(j - 3): xat_probs_take(j - 3, 5)
                if there(j - 1): xat_split_ctx(j - 1)
                if there(j - 3): xat_exp(j - 3, 7)
                if there(j - 3): xat_probs_take(j - 3, 6)
                if there(j): mla_query_take(j, 1)
                if there(j - 1): mla_probs_take(j - 1, 3)
                if there(j - 1): mla_out_take(j - 1, 2)
                if there(j - 3): xat_probs_take(j - 3, 7)
                if there(j - 2): xat_queries_take(j - 2, 1)
                if there(j - 2): xat_exp(j - 2, 0)
                if there(j): mla_exp(j, 0)
                if there(j - 1): mla_out_take(j - 1, 3)
                if there(j): mla_probs_take(j, 0)
                if there(j - 2): xat_exp(j - 2, 1)
                if phase_b_begins(j): prepare_T(0)
                if there(j): mla_query_take(j, 2)
                if there(j - 2): xat_probs_take(j - 2, 0)
                if there(j - 3): xat_out_take(j - 3)
                if phase_b_begins(j):
                    route(0)
                    split(0)
                if there(j): mla_out_take(j, 0)
                if there(j - 2): xat_probs_take(j - 2, 1)
                if there(j + 1): mla_squares(j + 1)
                if there(j - 2): xat_exp(j - 2, 2)
                if there(j): mla_exp(j, 1)
                for e in early_expert(j, 1): expert(0, e)
                if there(j): mla_query_take(j, 3)
                if there(j - 1): xat_split_x(j - 1)
                for e in early_expert(j, 2): expert(0, e)
                if there(j - 2): xat_probs_take(j - 2, 2)
                if there(j - 2): xat_exp(j - 2, 3)
                if there(j - 2): xat_exp(j - 2, 4)
                if there(j): mla_probs_take(j, 1)
                for e in early_expert(j, 3): expert(0, e)
                if isinstance(j, int) and 0 <= j < WF_PARTS: experts_split(j)
                if there(j - 2): xat_probs_take(j - 2, 3)
                if there(j - 2): xat_exp(j - 2, 5)
                if there(j - 1): xat_arrange_hi(j - 1)
                if there(j - 2): xat_probs_take(j - 2, 4)
                if there(j + 1): mla_latents_take(j + 1)
                if there(j): mla_exp(j, 2)
                if there(j + 1): mla_query_take(j + 1, 0)
                if there(j + 2): mla_split(j + 2)
                if there(j): mla_probs_take(j, 2)
                if there(j - 1): xat_queries_take(j - 1, 0)
                if there(j): mla_exp(j, 3)
                if there(j): mla_out_take(j, 1)
                if there(j - 2): xat_exp(j - 2, 6)

            def prepare_T(c):
                for k in range(KT_D):
                    act.wait_ge(f_T, c * KT_D + (k + 1))
                    if k == 0 and not first(c):
                        act.wait_ge(f_lo, c * KT_D)
                    bank = (sa if isinstance(c, int) and c == 0 else sx)[k]
                    act.activation(x2T[:, k, :], bank[:], ACT.Copy).then_inc(f_ev, 1)

            def route(c):
                act.wait_ge(f_v, c * F_V + 3)
                act.activation(p2e[:], dd[:], ACT.Exp).then_inc(f_p2, 1)

            def split(c):
                act.wait_ge(f_ev, c * KT_D + KT_D)
                if not first(c):
                    act.wait_ge(f_h, c * (2 * E))
                for k in range(KT_D):
                    act.activation(x2Th[:, k, :], x2T[:, k, :], ACT.Copy).then_inc(f_hi, 1)

            def expert(c, e):
                if e == 0 and not first(c): split(c)
                for m in range(2):
                    act.wait_ge(f_h, c * (2 * E) + (2 * e + m + 1))
                    earlier(act, f_sq, c, 2 * E, 2 * (e - 1) + m + 1)
                    act.activation(hr[:, m, :], sa[m][:], ACT.Relu).then_inc(f_r, 1)
                if e == prepare_at(c) and not final(c): prepare_T(c + 1)
                if e == E - 1 and not final(c): route(c + 1)

            mla_split(0)
            pipeline(act, step)
            chunks(act, expert)

        @block.vector
        def _(dve):
            dve.memset(mhalf[:], -0.5).then_inc(c_ok, 1)
            dve.memset(zero[:], 0.0).then_inc(c_ok, 1)
            dve.memset(rms_eps[:], RMS_EPS).then_inc(c_ok, 1)
            dve.memset(ln_eps[:], LN_EPS).then_inc(c_ok, 1)
            dve.memset(kv[:, KL:KL + 1], 1.0).then_inc(c_ok, 1)
            dve.memset(vx[:, :, HD:HD + 1], 1.0).then_inc(c_ok, 1)
            dve.wait_ge(d_fold, 16 * N_FOLD_LOADS)
            dve.tensor_tensor(stage3[:, 0:2048].rearrange("p (h c) -> p h c", c=KL),
                              stage3[:, 0:2048].rearrange("p (h c) -> p h c", c=KL),
                              kvln[:].unsqueeze(1).to_broadcast([128, 2 * H, KL]), ALU.mult).then_inc(k_ok, 1)
            for n in range(NCA):
                for k in range(2):
                    dve.wait_ge(s_hi, 2 * n + 2)
                    dve.scalar_tensor_tensor(WQl[:, k, HC * n:HC * n + HC, DR:128],
                                             sa[n % 2][:, k * 256:(k + 1) * 256].rearrange("p (h c) -> p h c", h=HC),
                                             qln[:, k:k + 1], f32(WQh[:, k, HC * n:HC * n + HC, DR:128]),
                                             ALU.mult, ALU.subtract).then_inc(s_lo, 1)
            dve.wait_ge(d_ld, 16 * N_LOADS)
            dve.wait_ge(c_ok, N_CONST)
            dve.tensor_tensor(wal[:], wa[:], f32(wah[:]), ALU.subtract).then_inc(c_lo, 1)
            for k in range(2):
                dve.scalar_tensor_tensor(WQl[:, k, :, 0:DR], wpe[:, k], qln[:, k:k + 1], f32(WQh[:, k, :, 0:DR]),
                                         ALU.mult, ALU.subtract).then_inc(c_lo, 1)
            dve.tensor_tensor(xwl[:], xw[:], f32(xwh[:]), ALU.subtract).then_inc(c_lo, 1)

            def mla_split(i):
                have(dve, a_xs, i, 2, 1)
                dve.tensor_tensor(xTl[:], xT[:], f32(xTh[:]), ALU.subtract).then_inc(a_xs, 1)

            def mla_normalise(i):
                have(dve, g_rs, i, 2, 2)
                freed(dve, p_aT, i, 1, 1)
                freed(dve, g_qk, i, 3, 3)
                freed(dve, g_kv, i, 1, 1)
                dve.tensor_scalar(qraw[:], ob[:, 128:QL], rstd[:, 0:1], None, ALU.mult).then_inc(v_qk, 1)
                dve.tensor_tensor(kc[:], ob[:, 256:320], cosine[:], ALU.mult).then_inc(v_qk, 1)
                dve.tensor_tensor(ks[:].rearrange("p (a c) -> p a c", a=2),
                                  ob[:, 256:320].rearrange("p (a c) -> p a c", a=2)[:, ::-1, :],
                                  sine[:].rearrange("p (a c) -> p a c", a=2), ALU.mult).then_inc(v_qk, 1)
                dve.tensor_scalar(qn[:, 0:128], ob[:, 0:128], rstd[:, 0:1], None, ALU.mult).then_inc(v_qk, 1)
                dve.tensor_scalar(kvn[:, 64:128], ob[:, QL:QL + KL], rstd[:, 1:2], None, ALU.mult).then_inc(v_qk, 1)

            def mla_latents_lo(i):
                have(dve, a_aT, i, 3, 3)
                dve.tensor_tensor(qAl[:], qb[:, 0:128], f32(qAh[:]), ALU.subtract).then_inc(v_aT, 1)

            def mla_rotate_sine(i, n):
                have(dve, a_q, i, NCA, n + 1)
                if n > 0:
                    have(dve, g_rp, i, 2 * NCA, 2 * n)
                else:
                    freed(dve, g_rp, i, 2 * NCA, 2 * NCA)
                dve.tensor_tensor(rsin[:].rearrange("p h (a c) -> p h a c", a=2),
                                  Qs[:, :, 0:DR].rearrange("p h (a c) -> p h a c", a=2)[:, :, ::-1, :],
                                  sine[:].rearrange("p (a c) -> p a c", a=2).unsqueeze(1).to_broadcast([128, HC, 2, DR // 2]),
                                  ALU.mult).then_inc(v_rp, 1)

            def mla_query_T_take(i, n):
                have(dve, p_qT, i, NCA, n + 1)
                if n > 0:
                    have(dve, p_s, i, NCA, n)
                else:
                    freed(dve, p_s, i, NCA, NCA)
                dve.tensor_copy(QT[:], qb[:]).then_inc(v_qT, 1)

            def mla_max(i, n):
                have(dve, p_s, i, NCA, n + 1)
                masked = Pa[:, n % 2, :].rearrange("p (h s) -> p h s", h=HC)
                dve.tensor_tensor(masked, sa[n % 2][:].rearrange("p (h s) -> p h s", h=HC),
                                  causal[:].unsqueeze(1).to_broadcast([128, HC, 128]), ALU.add).then_inc(v_ms, 1)
                if n > 0:
                    have(dve, g_sub, i, NCA, n)
                else:
                    freed(dve, g_sub, i, NCA, NCA)
                have(dve, v_ms, i, NCA, n + 1)
                dve.tensor_reduce(mxa[:], masked, AX.X, ALU.max).then_inc(v_mx, 1)

            def mla_out_norm(i, n):
                have(dve, p_pv, i, NCA, n + 1)
                if n > 0:
                    have(dve, v_o, i, NCA, n)
                else:
                    freed(dve, v_o, i, NCA, NCA)
                o = ob[:, 0:HC * 65].rearrange("p (h c) -> p h c", h=HC)
                dve.reciprocal(rec[:].unsqueeze(2), o[:, :, KL:KL + 1]).then_inc(v_rc, 1)
                have(dve, v_rc, i, NCA, n + 1)
                dve.tensor_tensor(Oa[:], o[:, :, 0:KL], rec[:].unsqueeze(2).to_broadcast([128, HC, KL]), ALU.mult)\
                   .then_inc(v_o, 1)

            def mla_norm_stats(i):
                have(dve, p_y, i, 1, 1)
                have(dve, d_xr, i, 16, 16)
                freed(dve, v_x1, i, 1, 1)
                dve.tensor_tensor(r1[:], x_res[:], ob[:, 0:D], ALU.add).then_inc(v_l1, 1)
                have(dve, v_l1, i, 3, 1)
                dve.bn_stats(st1[:], r1[:]).then_inc(v_l1, 1)
                have(dve, v_l1, i, 3, 2)
                freed(dve, g_l1, i, 2, 2)
                dve.tensor_copy(carry[:], st1[:, 0:1])
                dve.bn_aggr(mv1[:], st1[:]).then_inc(v_l1, 1)

            def mla_norm(i):
                have(dve, g_l1, i, 2, 2)
                freed(dve, q_xT, i, 1, 1)
                freed(dve, g_x1, i, 1, 1)
                dve.tensor_scalar(x1[:], r1[:], mv1[:, 0:1], rs1[:], ALU.subtract, ALU.mult).then_inc(v_x1, 1)

            def xat_split_ctx(i):
                have(dve, b_xs, i, 2, 1)
                dve.tensor_tensor(xcl[:, 2:4, :], ctxT[:], f32(xch[:, 2:4, :]), ALU.subtract).then_inc(w_xs, 1)

            def xat_split_x(i):
                have(dve, b_xs, i, 2, 2)
                dve.tensor_tensor(xcl[:, 0:2, :].rearrange("p k t -> p (k t)"), mb[:, 0:256],
                                  f32(xch[:, 0:2, :].rearrange("p k t -> p (k t)")), ALU.subtract).then_inc(w_xs, 1)

            def xat_bias(i):
                have(dve, q_qkv, i, 1, 1)
                freed(dve, b_ar, i, 2, 2)
                freed(dve, g_ar, i, 2, 2)
                freed(dve, g_vx, i, 1, 1)
                dve.tensor_tensor(qkv[:], mb[:, 0:384], bqkv[:], ALU.add).then_inc(w_qkv, 1)

            def xat_mask(i):
                have(dve, d_p, i, 16, 16)
                freed(dve, q_s, i, NCX, NCX)
                dve.scalar_tensor_tensor(comb[:], pad8[:], -BIG, ssmask[:], ALU.mult, ALU.add).then_inc(w_cm, 1)

            def xat_keys(i, half):
                have(dve, q_kT, i, 1, 1)
                freed(dve, q_s, i, NCX, (half + 1) * HC)
                dve.tensor_tensor(KX[:, half], mb[:, half * 128:(half + 1) * 128].unsqueeze(1).to_broadcast([128, HALF, 128]),
                                  groupsel[:].unsqueeze(2).to_broadcast([128, HALF, 128]), ALU.mult).then_inc(w_kx, 1)

            def xat_max(i, n):
                have(dve, q_s, i, NCX, n + 1)
                if n == 0:
                    have(dve, w_cm, i, 1, 1)
                if n == NCX - 1:
                    freed(dve, w_o, i, 3, 1)
                masked = Px[:, n % NPX, :].rearrange("p (h s) -> p h s", h=HC)
                dve.tensor_tensor(masked, sx[0][:].rearrange("p (h s) -> p h s", h=HC),
                                  comb[:].unsqueeze(1).to_broadcast([128, HC, 128]), ALU.add).then_inc(w_ms, 1)
                have(dve, w_ms, i, NCX, n + 1)
                dve.tensor_reduce(mxx[:, n, :], masked, AX.X, ALU.max).then_inc(w_mx, 1)

            def xat_out_norm(i):
                have(dve, q_pv, i, NCX, NCX)
                o = xo[:, 0:XH * (HD + 1)].rearrange("p (h c) -> p h c", h=XH)
                dve.scalar_tensor_tensor(den[:].unsqueeze(2), mxx[:, NCX - 1, 0:1].unsqueeze(1).to_broadcast([128, XH, 1]), -BIG / 2,
                                         o[:, :, HD:HD + 1], ALU.is_gt, ALU.mult).then_inc(w_o, 1)
                have(dve, w_o, i, 3, 1)
                dve.reciprocal(recx[:], den[:]).then_inc(w_o, 1)
                have(dve, w_o, i, 3, 2)
                freed(dve, q_oT, i, 1, 1)
                dve.tensor_tensor(Ox[:], o[:, :, 0:HD], recx[:].unsqueeze(2).to_broadcast([128, XH, HD]), ALU.mult)\
                   .then_inc(w_o, 1)

            def xat_out_lo(i):
                have(dve, b_oT, i, 1, 1)
                dve.tensor_tensor(OTxl[:].rearrange("p k t -> p (k t)"), mb[:, 0:256],
                                  f32(OTxh[:].rearrange("p k t -> p (k t)")), ALU.subtract).then_inc(w_oT, 1)

            def xat_norm_stats(i):
                have(dve, q_y, i, 1, 1)
                have(dve, g_xb, i, 1, 1)
                freed(dve, w_x2, i, 1, 1)
                dve.tensor_tensor(r2[:], x1b[:], mb[:, 0:D], ALU.add).then_inc(w_l2, 1)
                have(dve, w_l2, i, 3, 1)
                dve.bn_stats(st2[:], r2[:]).then_inc(w_l2, 1)
                have(dve, w_l2, i, 3, 2)
                freed(dve, g_l2, i, 2, 2)
                dve.tensor_copy(carry[:], st2[:, 0:1])
                dve.bn_aggr(mv2[:], st2[:]).then_inc(w_l2, 1)

            def xat_norm(i):
                have(dve, g_l2, i, 2, 2)
                freed(dve, d_x2, i, 16, 16)
                dve.tensor_scalar(x2[:], r2[:], mv2[:, 0:1], rs2[:], ALU.subtract, ALU.mult).then_inc(w_x2, 1)

            def step(j):
                for e in early_expert(j, 0): expert(0, e)
                if there(j): mla_rotate_sine(j, 1)
                if there(j - 3): xat_out_norm(j - 3)
                if there(j): mla_query_T_take(j, 1)
                if there(j - 2): xat_max(j - 2, 2)
                if there(j - 1): xat_split_ctx(j - 1)
                if there(j - 1): mla_norm_stats(j - 1)
                if there(j - 2): xat_max(j - 2, 3)
                if there(j): mla_out_norm(j, 0)
                if there(j): mla_rotate_sine(j, 2)
                if there(j): mla_max(j, 1)
                if phase_b_begins(j):
                    route(0)
                    route_weights(0)
                    split(0)
                if there(j - 3): xat_out_lo(j - 3)
                if there(j - 2): xat_max(j - 2, 4)
                if there(j): mla_query_T_take(j, 2)
                if there(j - 1): mla_norm(j - 1)
                if there(j - 3): xat_norm_stats(j - 3)
                if there(j - 2): xat_max(j - 2, 5)
                if there(j): mla_rotate_sine(j, 3)
                if there(j - 1): xat_split_x(j - 1)
                if there(j + 1): mla_normalise(j + 1)
                for e in early_expert(j, 1): expert(0, e)
                if there(j): mla_max(j, 2)
                if there(j): mla_query_T_take(j, 3)
                for e in early_expert(j, 2): expert(0, e)
                if there(j - 1): xat_bias(j - 1)
                if there(j - 2): xat_max(j - 2, 6)
                for e in early_expert(j, 3): expert(0, e)
                if there(j): mla_max(j, 3)
                if there(j + 1): mla_latents_lo(j + 1)
                if there(j - 1): xat_keys(j - 1, 0)
                if there(j - 1): xat_keys(j - 1, 1)
                if there(j): mla_out_norm(j, 1)
                if there(j + 1): mla_rotate_sine(j + 1, 0)
                if there(j + 2): mla_split(j + 2)
                if there(j - 2): xat_max(j - 2, 7)
                if there(j - 3): xat_norm(j - 3)
                if there(j - 1): xat_mask(j - 1)
                if there(j + 1): mla_query_T_take(j + 1, 0)
                if there(j - 1): xat_max(j - 1, 0)
                if there(j): mla_out_norm(j, 2)
                if there(j + 1): mla_max(j + 1, 0)
                if there(j - 1): xat_max(j - 1, 1)
                if there(j): mla_out_norm(j, 3)

            def after(c, k):
                dve.wait_ge(f_v, c * F_V + k)

            def split(c):
                for k in range(KT_D):
                    dve.wait_ge(f_hi, c * KT_D + (k + 1))
                    dve.tensor_tensor(x2Tl[:, k, :], x2T[:, k, :], f32(x2Th[:, k, :]), ALU.subtract).then_inc(f_lo, 1)

            def route(c):
                dve.wait_ge(f_lg, c + 1)
                bank = qb if isinstance(c, int) and c == 0 else mb
                dve.tensor_copy(lg[:].rearrange("p t e -> p (t e)"), bank[:, 0:TC * E]).then_inc(f_v, 1)
                after(c, 1)
                dve.tensor_copy(carry[:], lg[:, 0, 0:1])
                for t in range(TC):
                    last = dve.max(top[:, t, :], lg[:, t, :])
                last.then_inc(f_v, 1)
                after(c, 2)
                dve.tensor_tensor(dd[:].unsqueeze(2), top[:, :, 1:2], top[:, :, 0:1], ALU.subtract).then_inc(f_v, 1)
                for t in range(TC):
                    last = dve.max_index(topi[:, t, :], top[:, t, :], lg[:, t, :])
                last.then_inc(f_v, 1)

            def route_weights(c):
                after(c, 4)
                dve.tensor_copy(topf[:], topi[:, :, 0:2]).then_inc(f_v, 1)
                dve.wait_ge(f_p2, c + 1)
                dve.tensor_scalar(p2d[:], p2e[:], 1.0, None, ALU.add).then_inc(f_v, 1)
                after(c, 6)
                dve.reciprocal(pr[:, :, 0:1].rearrange("p t a -> p (t a)"), p2d[:]).then_inc(f_v, 1)
                after(c, 7)
                dve.tensor_tensor(pr[:, :, 1:2].rearrange("p t a -> p (t a)"), p2e[:],
                                  pr[:, :, 0:1].rearrange("p t a -> p (t a)"), ALU.mult).then_inc(f_v, 1)
                after(c, 8)
                for oh, a in ((oh1, 0), (oh2, 1)):
                    dve.tensor_tensor(oh[:], eidx[:].unsqueeze(1).to_broadcast([128, TC, E]),
                                      topf[:, :, a:a + 1].to_broadcast([128, TC, E]), ALU.is_equal).then_inc(f_v, 1)
                after(c, 10)
                for oh, a in ((oh1, 0), (oh2, 1)):
                    dve.tensor_tensor(oh[:], oh[:], pr[:, :, a:a + 1].to_broadcast([128, TC, E]), ALU.mult).then_inc(f_v, 1)

            def route_sum(c):
                after(c, 12)
                dve.tensor_tensor(wt[:], oh1[:], oh2[:], ALU.add).then_inc(f_v, 1)
                after(c, 13)

            def accumulate(c, e):
                for t in range(TC):
                    if t % 2 == 0:
                        dve.wait_ge(f_y, c * (2 * E) + (2 * e + t // 2 + 1))
                    if e > 0:
                        dve.wait_ge(f_ac, c * F_AC + ((e - 1) * TC + t + 1))
                    dve.scalar_tensor_tensor(acc[:, t, :], (qb, ob)[t // 2][:, (t % 2) * D:(t % 2 + 1) * D],
                                             wt[:, t, e:e + 1], (x2c if e == 0 else acc)[:, t, :], ALU.mult, ALU.add)\
                       .then_inc(f_ac, 1)

            def norm_stats(c):
                dve.wait_ge(f_ac, c * F_AC + F_AC)
                for t in range(TC):
                    dve.bn_stats(st3[:, t, :], acc[:, t, :]).then_inc(f_ln, 1)
                dve.wait_ge(f_ln, c * F_LN + TC)
                dve.tensor_copy(carry[:], st3[:, 0, 0:1])
                for t in range(TC):
                    dve.bn_aggr(mv3[:, t, :], st3[:, t, :]).then_inc(f_ln, 1)

            def norm(c):
                dve.wait_ge(f_gl, c * 2 + 2)
                if not first(c):
                    dve.wait_ge(f_st, c * 16)
                for t in range(TC):
                    dve.tensor_scalar(y3[:, t, :], acc[:, t, :], mv3[:, t, 0:1], rs3[:, t:t + 1],
                                      ALU.subtract, ALU.mult).then_inc(f_ln, 1)

            def expert(c, e):
                if e == 0:
                    if not first(c):
                        split(c)
                        accumulate(c - 1, E - 1)
                        norm_stats(c - 1)
                else:
                    if e == 1:
                        if not first(c): norm(c - 1)
                        route_sum(c)
                    accumulate(c, e - 1)
                if e == route_at(c) and not final(c): route(c + 1)
                if e == E - 1 and not final(c): route_weights(c + 1)

            mla_split(0)
            pipeline(dve, step)
            chunks(dve, expert)
            accumulate(NCH - 1, E - 1)
            norm_stats(NCH - 1)
            norm(NCH - 1)

        @block.gpsimd
        def _(gp):
            gp.wait_ge(c_ok, N_CONST)

            def power(dst, var, tmp, eps, s, i, per=2):
                gp.tensor_tensor(tmp, var, eps.to_broadcast(list(tmp.shape)), ALU.add).then_inc(s, 1)
                gp.wait_ge(s, i * per + 1)
                gp.tensor_tensor(dst, tmp, mhalf[:, 0:1].to_broadcast(list(tmp.shape)), ALU.pow).then_inc(s, 1)

            def experts_split(q):
                gp.wait_ge(wf_hi, q + 1)
                es = slice(q * E // WF_PARTS, (q + 1) * E // WF_PARTS)
                gp.tensor_tensor(wfcl[:, :, es, :], wfc[:, :, es, :], f32(wfch[:, :, es, :]), ALU.subtract).then_inc(wf_lo, 1)

            def mla_rstd(i):
                have(gp, a_sq, i, 2, 2)
                freed(gp, v_qk, i, 5, 5)
                power(rstd[:], ms[:], mse[:], rms_eps[:], g_rs, i)

            def mla_rest(i):
                have(gp, v_qk, i, 5, 3)
                freed(gp, p_aT, i, 1, 1)
                gp.tensor_tensor(kvn[:, 0:64], kc[:], ks[:], ALU.add).then_inc(g_qk, 1)
                gp.tensor_copy(qn[:, 128:192].bitcast(F32R), qraw[:]).then_inc(g_qk, 1)
                have(gp, g_qk, i, 3, 2)
                gp.tensor_tensor(qn[:, 192:256], qraw[:], qn[:, 128:192], ALU.subtract).then_inc(g_qk, 1)

            def mla_keep_values(i):
                have(gp, v_qk, i, 5, 5)
                freed(gp, p_pv, i, NCA, NCA)
                gp.tensor_tensor(kv[:, 0:KL], kvn[:, 64:128], zero[:].to_broadcast([128, KL]), ALU.add).then_inc(g_kv, 1)

            def mla_rotate(i, n):
                have(gp, a_q, i, NCA, n + 1)
                gp.tensor_tensor(rcos[:], Qs[:, :, 0:DR], cosine[:].unsqueeze(1).to_broadcast([128, HC, DR]), ALU.mult)\
                  .then_inc(g_rp, 1)
                have(gp, g_rp, i, 2 * NCA, 2 * n + 1)
                have(gp, v_rp, i, NCA, n + 1)
                gp.tensor_tensor(Qs[:, :, 0:DR], rcos[:], rsin[:], ALU.add).then_inc(g_rp, 1)

            def mla_less_max(i, n):
                have(gp, v_mx, i, NCA, n + 1)
                scores = Pa[:, n % 2, :].rearrange("p (h s) -> p h s", h=HC)
                gp.tensor_tensor(scores, scores, mxa[:].unsqueeze(2).to_broadcast([128, HC, 128]), ALU.subtract)\
                  .then_inc(g_sub, 1)

            def xat_less_max(i, n):
                have(gp, w_mx, i, NCX, n + 1)
                scores = Px[:, n % NPX, :].rearrange("p (h s) -> p h s", h=HC)
                gp.tensor_tensor(scores, scores, mxx[:, n, :].unsqueeze(2).to_broadcast([128, HC, 128]), ALU.subtract)\
                  .then_inc(h_sub, 1)

            def mla_norm(i):
                have(gp, v_l1, i, 3, 3)
                freed(gp, v_x1, i, 1, 1)
                power(rs1[:], mv1[:, 1:2], ve1[:], ln_eps[:], g_l1, i)

            def xat_keep(i):
                have(gp, v_x1, i, 1, 1)
                freed(gp, g_xb, i, 1, 1)
                gp.tensor_tensor(x1k[:], x1[:], zero[:].to_broadcast([128, D]), ALU.add).then_inc(g_x1, 1)

            def xat_keep_biased(i):
                have(gp, g_x1, i, 1, 1)
                freed(gp, w_l2, i, 3, 1)
                gp.tensor_tensor(x1b[:], x1k[:], bo[:], ALU.add).then_inc(g_xb, 1)

            def xat_arrange_lo(i):
                have(gp, b_ar, i, 2, 2)
                gp.tensor_tensor(karr[:, :, :, 1, :],
                                 qkv[:, 256:320].rearrange("p (n c) -> p n c", n=2).unsqueeze(2).to_broadcast([128, 2, 2, SLOT]),
                                 karr[:, :, :, 0, :], ALU.subtract).then_inc(g_ar, 1)
                gp.tensor_tensor(qarr[:, :, 2:4, :],
                                 qkv[:, 0:256].rearrange("p (n c) -> p n c", n=NCX).unsqueeze(2).to_broadcast([128, NCX, 2, SLOT]),
                                 qarr[:, :, 0:2, :], ALU.subtract).then_inc(g_ar, 1)

            def xat_keep_values(i):
                have(gp, w_qkv, i, 1, 1)
                freed(gp, q_pv, i, NCX, NCX)
                gp.tensor_tensor(vx[:, :, 0:HD], qkv[:, 320:384].rearrange("p (g d) -> p g d", g=G),
                                 zero[:].unsqueeze(2).to_broadcast([128, G, HD]), ALU.add).then_inc(g_vx, 1)

            def xat_norm(i):
                have(gp, w_l2, i, 3, 3)
                freed(gp, w_x2, i, 1, 1)
                power(rs2[:], mv2[:, 1:2], ve2[:], ln_eps[:], g_l2, i)

            def step(j):
                if there(j - 2): xat_arrange_lo(j - 2)
                if there(j - 3): xat_less_max(j - 3, 6)
                for e in early_expert(j, 0): expert(0, e)
                if there(j - 1): mla_less_max(j - 1, 3)
                if there(j): mla_rotate(j, 0)
                if there(j - 3): xat_less_max(j - 3, 7)
                if there(j - 2): xat_less_max(j - 2, 0)
                if there(j - 3): xat_keep_biased(j - 3)
                if there(j): mla_less_max(j, 0)
                if there(j): mla_rotate(j, 1)
                if there(j - 2): xat_keep_values(j - 2)
                if there(j - 2): xat_less_max(j - 2, 1)
                if there(j): mla_keep_values(j)
                if there(j - 2): xat_less_max(j - 2, 2)
                if there(j - 1): mla_norm(j - 1)
                if there(j - 2): xat_keep(j - 2)
                if there(j): mla_rotate(j, 2)
                if there(j - 2): xat_less_max(j - 2, 3)
                if there(j): mla_less_max(j, 1)
                if there(j + 1): mla_rstd(j + 1)
                if there(j - 2): xat_less_max(j - 2, 4)
                if there(j - 3): xat_norm(j - 3)
                for e in early_expert(j, 1): expert(0, e)
                if there(j): mla_rotate(j, 3)
                if there(j + 1): mla_rest(j + 1)
                for e in early_expert(j, 2): expert(0, e)
                if there(j - 2): xat_less_max(j - 2, 5)
                if there(j): mla_less_max(j, 2)
                for e in early_expert(j, 3): expert(0, e)
                if isinstance(j, int) and 0 <= j < WF_PARTS: experts_split(j)

            def norm(c):
                gp.wait_ge(f_ln, c * F_LN + 2 * TC)
                power(rs3[:], mv3[:, :, 1:2].rearrange("p t a -> p (t a)"), ve3[:], ln_eps[:], f_gl, c)

            def expert(c, e):
                for m in range(2):
                    gp.wait_ge(f_r, c * (2 * E) + (2 * e + m + 1))
                    earlier(gp, f_y, c, 2 * E, 2 * (e - 1))
                    gp.tensor_tensor(h2[:, e % 2, m, :], hr[:, m, :], hr[:, m, :], ALU.mult).then_inc(f_sq, 1)
                if e == 0 and not first(c): norm(c - 1)

            pipeline(gp, step)
            chunks(gp, expert)
            norm(NCH - 1)


def kernel(**inputs):
    import concourse.bacc as bacc
    from concourse.bass_utils import run_bass_kernel_spmd

    a = {k: np.asarray(v) for k, v in inputs.items()}
    x, ctx = a["x"], a["ctx_2048"]
    wq_b = a["L0_attn_wq_b"].reshape(QL, H, DN + DR)
    wkv_b = a["L0_attn_wkv_b"].reshape(KL, H, DN + DV)
    rest = slice(128, QL)
    nopeT = wq_b[:, :, :DN].transpose(2, 1, 0)
    qln = a["L0_attn_q_a_ln_w"]

    def group_order(w, axis):
        w = np.moveaxis(w, axis, -1)
        lead = w.shape[:-1]
        w = w.reshape(*lead, 2, HALF, HC, HD).swapaxes(-3, -2).reshape(*lead, XH * HD)
        return np.moveaxis(w, -1, axis)

    def tokens_last(v):
        return v.reshape(B * S, KT_D, 128).transpose(2, 1, 0)

    inv = 1.0 / np.float32(10000.0) ** (np.arange(0, DR, 2, dtype=np.float32) / np.float32(DR))
    angle = np.outer(np.arange(S, dtype=np.float32), inv.astype(np.float32)).astype(np.float32)
    cos, sin = np.cos(angle), np.sin(angle)
    row = np.arange(128)
    arrays = {
        "x": x, "xT": tokens_last(x), "ctxT": tokens_last(ctx),
        "ssmask": a["mask_SxS2_bc0"], "padmask": a["mask_BxS2_bk0"],
        "wa": np.concatenate([a["L0_attn_wq_a"], a["L0_attn_wkv_a"]], axis=1),
        "wqnT": np.concatenate([nopeT, nopeT[:, :, rest]], axis=2),
        "wkvT": np.stack([wkv_b[:, :, :DN].transpose(2, 1, 0), wkv_b[:, :, DN:].transpose(2, 1, 0)], axis=1),
        "wpe": np.stack([wq_b[:128, :, DN:], np.concatenate([wq_b[rest, :, DN:]] * 2)], axis=1),
        "wo": a["L0_attn_wo"],
        "qln": np.stack([qln[:128], np.concatenate([qln[rest]] * 2)], axis=1),
        "kvln": a["L0_attn_kv_a_ln_w"],
        "xw": np.concatenate([group_order(a["L0_xattn_Wq"], 0).T, a["L0_xattn_Wk"].T, a["L0_xattn_Wv"].T,
                              group_order(a["L0_xattn_Wo"], 1).T], axis=1),
        "bqkv": np.concatenate([group_order(a["L0_xattn_bq"], 0), a["L0_xattn_bk"], a["L0_xattn_bv"]]),
        "bo": a["L0_xattn_bo"],
        "wr": a["L0_ffn_w_router"], 
        "wfc": a["L0_ffn_w_fc"].reshape(E, KT_D, 128, D).transpose(2, 1, 0, 3),
        "wpj": a["L0_ffn_w_proj"].reshape(E, KT_D, 128, D).transpose(2, 0, 1, 3),
        "c_ident": np.eye(128, dtype=np.float32),
        "c_causal": np.where(row[None, :] > row[:, None], np.float32(-BIG), np.float32(0)),
        "c_cos": np.concatenate([cos, cos], axis=1), "c_sin": np.concatenate([-sin, sin], axis=1),
        "c_groupsel": (row[:, None] % SLOT // HD == np.arange(HALF)).astype(np.float32),
        "c_eidx": np.tile(np.arange(E, dtype=np.float32), (128, 1)),
    }
    arrays = {k: np.ascontiguousarray(v) for k, v in arrays.items()}
    nc = bacc.Bacc("TRN2", target_bir_lowering=False, num_devices=1)
    io = {k: nc.dram_tensor(f"in_{k}", v.shape, mybir.dt.from_np(v.dtype), kind="ExternalInput").ap()
          for k, v in arrays.items()}
    io["out"] = nc.dram_tensor("out_x", (B, S, D), F32, kind="ExternalOutput").ap()
    decoder_layer(nc, io)
    r = run_bass_kernel_spmd(nc, [{f"in_{k}": v for k, v in arrays.items()}], core_ids=[0])
    return r.results[0]["out_x"]
```
